# Optimizing a Trainium2 kernel written in Bass

```python
import numpy as np
import jax
import jax.numpy as jnp

def _softmax(x, axis=-1):
    return jax.nn.softmax(x, axis=axis)

def _gelu(x):
    return jax.nn.gelu(x, approximate=True)

def _silu(x):
    return jax.nn.silu(x)

def _sigmoid(x):
    return jax.nn.sigmoid(x)

def _layernorm(x, axis=-1, eps=1e-05):
    m = jnp.mean(x, axis=axis, keepdims=True)
    v = jnp.var(x, axis=axis, keepdims=True)
    return (x - m) / jnp.sqrt(v + eps)

def _scatter_add(tgt, idx, src, axis=0):
    return tgt.at[idx].add(src)

def _segment_sum(src, seg, n):
    return jax.ops.segment_sum(src, seg, n)
kernel_name = 'mk_decoder_preln_d4_seqx_r8_4b6b49'

def setup_inputs(seed: int=0):
    np.random.seed(seed)
    _w = jnp.asarray

    def _rec_inputs():
        import jax
        import jax.numpy as jnp
        _rk = jax.random.key(seed)
        x = 7.22e-05 + 1 * jax.random.normal(jax.random.fold_in(_rk, 1), (4, 512, 128), jnp.float32)
        _lenS = 512 - jax.random.randint(jax.random.fold_in(_rk, 7), (4,), 0, max(1, 512 // 4) + 1, jnp.int32)
        _lenS2 = 77 - jax.random.randint(jax.random.fold_in(_rk, 8), (4,), 0, max(1, 77 // 4) + 1, jnp.int32)
        _ctx_1024P = jax.random.normal(jax.random.fold_in(_rk, 11), (4, 16, 128), jnp.float32)
        _ctx_1024c = jax.random.dirichlet(jax.random.fold_in(_rk, 511), 0.3 * jnp.ones((16,), jnp.float32), (4, 77))
        _ctx_1024t = jnp.einsum('bsk,bkd->bsd', _ctx_1024c, _ctx_1024P)
        _ctx_1024t = _ctx_1024t * jax.lax.rsqrt(jnp.mean(jnp.square(_ctx_1024t)) + 1e-12) * 0.953939
        ctx_1024 = 4.13588e-05 + 0.999923 * (_ctx_1024t + 0.3 * jax.random.normal(jax.random.fold_in(_rk, 611), (4, 77, 128), jnp.float32))
        _validS = jnp.arange(512)[None, :] < _lenS[:, None]
        _validS2 = jnp.arange(77)[None, :] < _lenS2[:, None]
        _causal = jnp.tril(jnp.ones((512, 512), dtype=bool))
        mask_BxSxS2_bk1 = jnp.broadcast_to(_validS2[:, None, :], (4, 512, 77))
        mask_Bx1x1xS2_fk0 = jnp.where(jnp.broadcast_to(_validS2[:, None, None, :], (4, 1, 1, 77)), 0.0, 1.0).astype(jnp.float32)
        return (x, ctx_1024, mask_BxSxS2_bk1, mask_Bx1x1xS2_fk0)
    x, ctx_1024, mask_BxSxS2_bk1, mask_Bx1x1xS2_fk0 = _rec_inputs()

    def _L0_attn_setup():
        import jax, jax.numpy as jnp
        import numpy as np
        import math
        D_MODEL = 128
        N_HEADS = 16
        HEAD_DIM = D_MODEL // N_HEADS

        def alibi_slopes(n_heads: int) -> jnp.ndarray:

            def pow2_slopes(n):
                start = 2 ** (-2 ** (-(math.log2(n) - 3)))
                return [start * start ** i for i in range(n)]
            if math.log2(n_heads).is_integer():
                s = pow2_slopes(n_heads)
            else:
                c = 2 ** math.floor(math.log2(n_heads))
                s = pow2_slopes(c)
                s.extend(pow2_slopes(2 * c)[0::2][:n_heads - c])
            return jnp.array(s, dtype=jnp.float32)
        key = jax.random.key(seed)
        ks = jax.random.split(key, 5)
        B, T, C = (2, 256, D_MODEL)
        std = 1.0 / math.sqrt(C)
        return {'x': jax.random.normal(ks[0], (B, T, C), dtype=jnp.float32), 'Wq': jax.random.normal(ks[1], (C, C), dtype=jnp.float32) * std, 'bq': jnp.zeros((C,), dtype=jnp.float32), 'Wk': jax.random.normal(ks[2], (C, C), dtype=jnp.float32) * std, 'bk': jnp.zeros((C,), dtype=jnp.float32), 'Wv': jax.random.normal(ks[3], (C, C), dtype=jnp.float32) * std, 'bv': jnp.zeros((C,), dtype=jnp.float32), 'Wo': jax.random.normal(ks[4], (C, C), dtype=jnp.float32) * std, 'bo': jnp.zeros((C,), dtype=jnp.float32)}
    _L0_attn_all = _L0_attn_setup()
    _L0_attn_in = {k: v for k, v in _L0_attn_all.items() if k in ('Wq', 'bq', 'Wk', 'bk', 'Wv', 'bv', 'Wo', 'bo')}
    del _L0_attn_all

    def _L0_xattn_setup():
        import jax, jax.numpy as jnp
        import numpy as np
        from math import sqrt
        B, NQ, SK, ISIZE, HSIZE, OSIZE, H = (4, 256, 256, 128, 128, 128, 16)
        D = HSIZE // H
        IEPS = 1e-32
        NEG = -1e+32
        key = jax.random.key(seed)
        ks = jax.random.split(key, 9)
        scale = 1.0 / sqrt(ISIZE)
        return {'iQ': jax.random.normal(ks[0], (B, NQ, ISIZE), jnp.float32), 'iK': jax.random.normal(ks[1], (B, SK, ISIZE), jnp.float32), 'iV': jax.random.normal(ks[2], (B, SK, ISIZE), jnp.float32), 'mask': jax.random.randint(ks[3], (B, NQ, SK), 0, 2).astype(bool), 'Wq': jax.random.normal(ks[4], (HSIZE, ISIZE), jnp.float32) * scale, 'Wk': jax.random.normal(ks[5], (HSIZE, ISIZE), jnp.float32) * scale, 'Wv': jax.random.normal(ks[6], (HSIZE, ISIZE), jnp.float32) * scale, 'Wo': jax.random.normal(ks[7], (OSIZE, HSIZE), jnp.float32) * scale, 'sn_bias': jnp.zeros((1,), jnp.float32)}
    _L0_xattn_all = _L0_xattn_setup()
    _L0_xattn_in = {k: v for k, v in _L0_xattn_all.items() if k in ('Wq', 'Wk', 'Wv', 'Wo', 'sn_bias')}
    del _L0_xattn_all

    def _L0_ffn_setup():
        import jax, jax.numpy as jnp
        import numpy as np
        B, L, D = (2, 256, 128)
        E = 15
        H = D * 1
        K = 3
        T = 1.0
        key = jax.random.key(seed)
        ks = jax.random.split(key, 12)
        s = 0.02
        return {'x': jax.random.normal(ks[0], (B, L, D), dtype=jnp.float32), 'router_W': jax.random.normal(ks[1], (D, E), dtype=jnp.float32) * s, 'router_b': jnp.zeros((E,), dtype=jnp.float32), 'sW1': jax.random.normal(ks[2], (D, H), dtype=jnp.float32) * s, 'sb1': jnp.zeros((H,), dtype=jnp.float32), 'sW2': jax.random.normal(ks[3], (H, D), dtype=jnp.float32) * s, 'sb2': jnp.zeros((D,), dtype=jnp.float32), 'eW1': jax.random.normal(ks[4], (E, D, H), dtype=jnp.float32) * s, 'eb1': jnp.zeros((E, H), dtype=jnp.float32), 'eW2': jax.random.normal(ks[5], (E, H, D), dtype=jnp.float32) * s, 'eb2': jnp.zeros((E, D), dtype=jnp.float32)}
    _L0_ffn_all = _L0_ffn_setup()
    _L0_ffn_in = {k: v for k, v in _L0_ffn_all.items() if k in ('router_W', 'router_b', 'sW1', 'sb1', 'sW2', 'sb2', 'eW1', 'eb1', 'eW2', 'eb2')}
    del _L0_ffn_all

    def _L1_attn_setup():
        import jax, jax.numpy as jnp
        import numpy as np
        B, N, C = (2, 256, 128)
        H = 16
        HD = C // H
        KA_IN = 2 * HD
        KA_OUT = HD
        T = 4
        KA_HID = KA_IN // 2
        KA_O = KA_OUT // T
        TEMPERATURE = 0.72
        SCALE = HD ** (-0.5)
        LN_EPS = 1e-05
        key = jax.random.key(seed)
        ks = jax.random.split(key, 20)

        def w(k, shape, fan_in):
            return jax.random.normal(k, shape, jnp.float32) / np.sqrt(fan_in)
        return {'x': jax.random.normal(ks[0], (B, N, C), jnp.float32), 'Wqkv': w(ks[1], (C, 3 * C), C), 'Wproj': w(ks[2], (C, C), C), 'bproj': jnp.zeros((C,), jnp.float32), 'alpha': jnp.ones((H,), jnp.float32), 'beta': jnp.ones((H,), jnp.float32), 'gamma': jnp.ones((H,), jnp.float32), 'A': w(ks[3], (T, KA_IN, KA_IN), KA_IN), 'Wphi1': w(ks[4], (T, KA_IN, KA_HID), KA_IN), 'bphi1': jnp.zeros((T, KA_HID), jnp.float32), 'Wphi2': w(ks[5], (T, KA_HID, KA_O), KA_HID), 'bphi2': jnp.zeros((T, KA_O), jnp.float32), 'Wpsi1': w(ks[6], (T, KA_IN, KA_IN), KA_IN), 'bpsi1': jnp.zeros((T, KA_IN), jnp.float32), 'ln_g': jnp.ones((T, KA_IN), jnp.float32), 'ln_b': jnp.zeros((T, KA_IN), jnp.float32), 'Wpsi2': w(ks[7], (T, KA_IN, KA_O), KA_IN), 'bpsi2': jnp.zeros((T, KA_O), jnp.float32), 'mixing': jnp.full((T,), 1.0 / T, jnp.float32), 'temp_scale': jnp.asarray(TEMPERATURE, jnp.float32)}
    _L1_attn_all = _L1_attn_setup()
    _L1_attn_in = {k: v for k, v in _L1_attn_all.items() if k in ('Wqkv', 'Wproj', 'bproj', 'alpha', 'beta', 'gamma', 'A', 'Wphi1', 'bphi1', 'Wphi2', 'bphi2', 'Wpsi1', 'bpsi1', 'ln_g', 'ln_b', 'Wpsi2', 'bpsi2', 'mixing', 'temp_scale')}
    del _L1_attn_all

    def _L1_xattn_setup():
        import jax, jax.numpy as jnp
        import numpy as np
        DIM = 128
        DIM_HEAD = 64
        HEADS = 16
        INNER = DIM_HEAD * HEADS
        EPS = 1e-05

        def layer_norm(x, g, b):
            m = jnp.mean(x, axis=-1, keepdims=True)
            v = jnp.mean(jnp.square(x - m), axis=-1, keepdims=True)
            return (x - m) * jax.lax.rsqrt(v + EPS) * g + b
        key = jax.random.key(seed)
        ks = jax.random.split(key, 8)
        B, N_IMG, N_LAT = (4, 512, 64)
        std = 1.0 / np.sqrt(DIM)
        return {'image_embeds': jax.random.normal(ks[0], (B, N_IMG, DIM), dtype=jnp.float32), 'latents': jax.random.normal(ks[1], (B, N_LAT, DIM), dtype=jnp.float32), 'ln1_g': jnp.ones((DIM,), jnp.float32), 'ln1_b': jnp.zeros((DIM,), jnp.float32), 'ln2_g': jnp.ones((DIM,), jnp.float32), 'ln2_b': jnp.zeros((DIM,), jnp.float32), 'Wq': jax.random.normal(ks[2], (DIM, INNER), dtype=jnp.float32) * std, 'Wkv': jax.random.normal(ks[3], (DIM, 2 * INNER), dtype=jnp.float32) * std, 'Wo': jax.random.normal(ks[4], (INNER, DIM), dtype=jnp.float32) * std}
    _L1_xattn_all = _L1_xattn_setup()
    _L1_xattn_in = {k: v for k, v in _L1_xattn_all.items() if k in ('ln1_g', 'ln1_b', 'ln2_g', 'ln2_b', 'Wq', 'Wkv', 'Wo')}
    del _L1_xattn_all

    def _L1_ffn_setup():
        import jax, jax.numpy as jnp
        import numpy as np
        DIM = 128
        HIDDEN = 384
        SCALE = 1.0 / 127.0

        def _dequant(w_int, dtype):
            return w_int.astype(dtype) * jnp.asarray(SCALE, dtype)
        key = jax.random.key(seed)
        k_x, k_g, k_u, k_d = jax.random.split(key, 4)
        x = jax.random.normal(k_x, (4, 256, DIM), dtype=jnp.float32)
        w_gate = jax.random.randint(k_g, (HIDDEN, DIM), -127, 128, dtype=jnp.int32)
        w_up = jax.random.randint(k_u, (HIDDEN, DIM), -127, 128, dtype=jnp.int32)
        w_down = jax.random.randint(k_d, (DIM, HIDDEN), -127, 128, dtype=jnp.int32)
        return {'x': x, 'w_gate': w_gate, 'w_up': w_up, 'w_down': w_down}
    _L1_ffn_all = _L1_ffn_setup()
    _L1_ffn_in = {k: v for k, v in _L1_ffn_all.items() if k in ('w_gate', 'w_up', 'w_down')}
    del _L1_ffn_all

    def _L2_attn_setup():
        import jax, jax.numpy as jnp
        import numpy as np
        D = 128
        H = 16
        KVH = 4
        HD = D // H
        LAT = 32
        WIN = 32
        B, S = (1, 256)
        BASE_G, BASE_L = (1000000.0, 10000.0)
        EPS = 1e-06

        def rmsnorm(x, w):
            return x * jax.lax.rsqrt(jnp.mean(x * x, axis=-1, keepdims=True) + EPS) * w

        def qk_norm(x):
            return x * jax.lax.rsqrt(jnp.mean(x * x, axis=-1, keepdims=True) + EPS)

        def rope(x, base):
            s, hd = (x.shape[-2], x.shape[-1])
            inv_freq = 1.0 / base ** (jnp.arange(0, hd, 2, dtype=jnp.float32) / hd)
            freqs = jnp.arange(s, dtype=jnp.float32)[:, None] * inv_freq[None, :]
            cos, sin = (jnp.cos(freqs), jnp.sin(freqs))
            xe, xo = (x[..., ::2], x[..., 1::2])
            out = jnp.stack([xe * cos - xo * sin, xe * sin + xo * cos], axis=-1)
            return out.reshape(x.shape)

        def split_heads(x, n_heads):
            b, s, _ = x.shape
            return x.reshape(b, s, n_heads, HD).transpose(0, 2, 1, 3)

        def repeat_kv(x):
            return jnp.repeat(x, H // KVH, axis=1)

        def sdpa(q, k, v, mask):
            scores = jnp.einsum('bhqd,bhkd->bhqk', q, k) / np.sqrt(HD).astype(np.float32)
            scores = jnp.where(mask, scores, jnp.float32(-1e+30))
            probs = jax.nn.softmax(scores, axis=-1)
            return jnp.einsum('bhqk,bhkd->bhqd', probs, v)

        def merge_heads(x):
            b, h, s, hd = x.shape
            return x.transpose(0, 2, 1, 3).reshape(b, s, h * hd)

        def global_latent_attn(x, wq, w_kv_down, w_k_up, w_v_up, wo):
            q = split_heads(x @ wq, H)
            latent = x @ w_kv_down
            k = split_heads(latent @ w_k_up, KVH)
            v = split_heads(latent @ w_v_up, KVH)
            q, k = (rope(q, BASE_G), rope(k, BASE_G))
            q, k = (qk_norm(q), qk_norm(k))
            k, v = (repeat_kv(k), repeat_kv(v))
            i = jnp.arange(x.shape[1])
            causal = i[:, None] >= i[None, :]
            return merge_heads(sdpa(q, k, v, causal)) @ wo

        def local_gqa_attn(x, wq, wk, wv, wo):
            q = split_heads(x @ wq, H)
            k = split_heads(x @ wk, KVH)
            v = split_heads(x @ wv, KVH)
            q, k = (rope(q, BASE_L), rope(k, BASE_L))
            q, k = (qk_norm(q), qk_norm(k))
            k, v = (repeat_kv(k), repeat_kv(v))
            i = jnp.arange(x.shape[1])
            diff = i[:, None] - i[None, :]
            mask = (diff >= 0) & (diff < WIN)
            return merge_heads(sdpa(q, k, v, mask)) @ wo
        key = jax.random.key(seed)
        ks = jax.random.split(key, 12)
        std = 0.02
        return {'hidden': jax.random.normal(ks[0], (B, S, D), dtype=jnp.float32), 'norm1_w': jnp.ones((D,), jnp.float32), 'norm2_w': jnp.ones((D,), jnp.float32), 'g_wq': jax.random.normal(ks[1], (D, H * HD), jnp.float32) * std, 'g_kv_down': jax.random.normal(ks[2], (D, LAT), jnp.float32) * std, 'g_k_up': jax.random.normal(ks[3], (LAT, KVH * HD), jnp.float32) * std, 'g_v_up': jax.random.normal(ks[4], (LAT, KVH * HD), jnp.float32) * std, 'g_wo': jax.random.normal(ks[5], (D, D), jnp.float32) * std, 'l_wq': jax.random.normal(ks[6], (D, H * HD), jnp.float32) * std, 'l_wk': jax.random.normal(ks[7], (D, KVH * HD), jnp.float32) * std, 'l_wv': jax.random.normal(ks[8], (D, KVH * HD), jnp.float32) * std, 'l_wo': jax.random.normal(ks[9], (D, D), jnp.float32) * std}
    _L2_attn_all = _L2_attn_setup()
    _L2_attn_in = {k: v for k, v in _L2_attn_all.items() if k in ('norm1_w', 'norm2_w', 'g_wq', 'g_kv_down', 'g_k_up', 'g_v_up', 'g_wo', 'l_wq', 'l_wk', 'l_wv', 'l_wo')}
    del _L2_attn_all

    def _L2_xattn_setup():
        import jax, jax.numpy as jnp
        import numpy as np
        DIM = 128
        HEAD_DIM = 64
        NUM_HEADS = 8
        INNER = HEAD_DIM * NUM_HEADS
        ROT_DIM = HEAD_DIM
        ROPE_BASE = 10000.0
        EPS = 1e-05

        def layer_norm(x, g, b):
            mu = jnp.mean(x, axis=-1, keepdims=True)
            var = jnp.var(x, axis=-1, keepdims=True)
            return (x - mu) * jax.lax.rsqrt(var + EPS) * g + b

        def rope_rotate_k(k):
            n = k.shape[1]
            half = ROT_DIM // 2
            inv_freq = 1.0 / ROPE_BASE ** (jnp.arange(0, ROT_DIM, 2, dtype=jnp.float32) / ROT_DIM)
            theta = jnp.arange(n, dtype=jnp.float32)[:, None] * inv_freq[None, :]
            angles = jnp.concatenate([theta, theta], axis=-1)
            cos = jnp.cos(angles)[None, :, None, :].astype(k.dtype)
            sin = jnp.sin(angles)[None, :, None, :].astype(k.dtype)
            k_rope, k_pass = (k[..., :ROT_DIM], k[..., ROT_DIM:])
            neg_half = jnp.concatenate([-k_rope[..., half:], k_rope[..., :half]], axis=-1)
            k_rope = k_rope * cos + neg_half * sin
            return jnp.concatenate([k_rope, k_pass], axis=-1)
        key = jax.random.key(seed)
        ks = jax.random.split(key, 5)
        b, n, m = (8, 1024, 64)
        s = 1.0 / np.sqrt(DIM)
        return {'x': jax.random.normal(ks[0], (b, n, DIM), jnp.float32), 'latents': jax.random.normal(ks[1], (b, m, DIM), jnp.float32), 'gamma_x': jnp.ones((DIM,), jnp.float32), 'beta_x': jnp.zeros((DIM,), jnp.float32), 'gamma_l': jnp.ones((DIM,), jnp.float32), 'beta_l': jnp.zeros((DIM,), jnp.float32), 'Wq': jax.random.normal(ks[2], (DIM, INNER), jnp.float32) * s, 'Wkv': jax.random.normal(ks[3], (DIM, 2 * INNER), jnp.float32) * s, 'Wo': jax.random.normal(ks[4], (INNER, DIM), jnp.float32) * (1.0 / np.sqrt(INNER))}
    _L2_xattn_all = _L2_xattn_setup()
    _L2_xattn_in = {k: v for k, v in _L2_xattn_all.items() if k in ('gamma_x', 'beta_x', 'gamma_l', 'beta_l', 'Wq', 'Wkv', 'Wo')}
    del _L2_xattn_all

    def _L2_ffn_setup():
        import jax, jax.numpy as jnp
        import numpy as np
        B, N, D = (4, 256, 128)
        SPARSITY = 0.01
        key = jax.random.key(seed)
        k1, k2, k3 = jax.random.split(key, 3)
        x = jax.random.normal(k1, (B, N, D), dtype=jnp.float32)
        spatial = jax.random.normal(k2, (D, D), dtype=jnp.float32) * 0.02
        freq = jnp.fft.fft(spatial, axis=-1)
        k = int(D * SPARSITY)
        mag = jnp.abs(freq)
        kth = jax.lax.top_k(mag, k)[0][:, -1:]
        w_sparse = jnp.where(mag >= kth, freq, 0.0 + 0j)
        bias = jax.random.normal(k3, (D,), dtype=jnp.float32) * 0.01
        return {'x': x, 'w_freq_real': jnp.real(w_sparse).astype(jnp.float32), 'w_freq_imag': jnp.imag(w_sparse).astype(jnp.float32), 'bias': bias}
    _L2_ffn_all = _L2_ffn_setup()
    _L2_ffn_in = {k: v for k, v in _L2_ffn_all.items() if k in ('w_freq_real', 'w_freq_imag', 'bias')}
    del _L2_ffn_all

    def _L3_attn_setup():
        import jax, jax.numpy as jnp
        import numpy as np
        DIM = 128
        HEADS = 16
        DIM_HEAD = 64
        INNER = HEADS * DIM_HEAD

        def _attention(x, ln_gamma, ln_beta, w_qkv, w_out, b_out):
            b, n, _ = x.shape
            scale = DIM_HEAD ** (-0.5)
            mu = jnp.mean(x, axis=-1, keepdims=True)
            var = jnp.var(x, axis=-1, keepdims=True)
            xn = (x - mu) / jnp.sqrt(var + 1e-05) * ln_gamma + ln_beta
            qkv = jnp.einsum('bnd,ed->bne', xn, w_qkv)
            q, k, v = jnp.split(qkv, 3, axis=-1)
            reshape = lambda t: t.reshape(b, n, HEADS, DIM_HEAD).transpose(0, 2, 1, 3)
            q, k, v = (reshape(q) * scale, reshape(k), reshape(v))
            sim = jnp.einsum('bhid,bhjd->bhij', q, k)
            mask_value = -jnp.finfo(sim.dtype).max
            causal = jnp.triu(jnp.ones((n, n), dtype=bool), k=1)
            sim = jnp.where(causal, mask_value, sim)
            sim = sim - jax.lax.stop_gradient(jnp.max(sim, axis=-1, keepdims=True))
            attn = jax.nn.softmax(sim, axis=-1)
            out = jnp.einsum('bhij,bhjd->bhid', attn, v)
            out = out.transpose(0, 2, 1, 3).reshape(b, n, INNER)
            return jnp.einsum('bne,de->bnd', out, w_out) + b_out
        key = jax.random.key(seed)
        ks = jax.random.split(key, 6)
        x = jax.random.normal(ks[0], (2, 256, DIM), dtype=jnp.float32)
        ln_gamma = jnp.ones((DIM,), dtype=jnp.float32)
        ln_beta = jnp.zeros((DIM,), dtype=jnp.float32)
        w_qkv = jax.random.normal(ks[1], (3 * INNER, DIM), dtype=jnp.float32) * DIM ** (-0.5)
        w_out = jax.random.normal(ks[2], (DIM, INNER), dtype=jnp.float32) * INNER ** (-0.5)
        b_out = jax.random.normal(ks[3], (DIM,), dtype=jnp.float32) * 0.02
        return {'x': x, 'ln_gamma': ln_gamma, 'ln_beta': ln_beta, 'w_qkv': w_qkv, 'w_out': w_out, 'b_out': b_out}
    _L3_attn_all = _L3_attn_setup()
    _L3_attn_in = {k: v for k, v in _L3_attn_all.items() if k in ('ln_gamma', 'ln_beta', 'w_qkv', 'w_out', 'b_out')}
    del _L3_attn_all

    def _L3_xattn_setup():
        import jax, jax.numpy as jnp
        import numpy as np
        B, S, D, H = (4, 256, 128, 16)
        DEPTH = D // H

        def _split_heads(x):
            b, s, _ = x.shape
            return x.reshape(b, s, H, DEPTH).transpose(0, 2, 1, 3)
        key = jax.random.key(seed)
        ks = jax.random.split(key, 12)
        inp = {'v': jax.random.normal(ks[0], (B, S, D), dtype=jnp.float32), 'k': jax.random.normal(ks[1], (B, S, D), dtype=jnp.float32), 'q': jax.random.normal(ks[2], (B, S, D), dtype=jnp.float32), 'mask': jax.random.randint(ks[3], (B, 1, 1, S), 0, 2).astype(jnp.float32), 'Wq': jax.random.normal(ks[4], (D, D), dtype=jnp.float32) / np.sqrt(D), 'bq': jnp.zeros((D,), dtype=jnp.float32), 'Wk': jax.random.normal(ks[5], (D, D), dtype=jnp.float32) / np.sqrt(D), 'bk': jnp.zeros((D,), dtype=jnp.float32), 'Wv': jax.random.normal(ks[6], (D, D), dtype=jnp.float32) / np.sqrt(D), 'bv': jnp.zeros((D,), dtype=jnp.float32), 'Wo': jax.random.normal(ks[7], (D, D), dtype=jnp.float32) / np.sqrt(D), 'bo': jnp.zeros((D,), dtype=jnp.float32)}
        return inp
    _L3_xattn_all = _L3_xattn_setup()
    _L3_xattn_in = {k: v for k, v in _L3_xattn_all.items() if k in ('Wq', 'bq', 'Wk', 'bk', 'Wv', 'bv', 'Wo', 'bo')}
    del _L3_xattn_all

    def _L3_ffn_setup():
        import jax, jax.numpy as jnp
        import numpy as np
        H = 128
        I = 352
        E = 8
        TOP_K = 2

        def _moe(hidden_states, router_w, gate_w, up_w, down_w):
            B, S, Hd = hidden_states.shape
            x = hidden_states.reshape(-1, Hd)
            logits = x @ router_w.T
            probs = jax.nn.softmax(logits.astype(jnp.float32), axis=-1)
            top_w, top_idx = jax.lax.top_k(probs, TOP_K)
            top_w = top_w.astype(x.dtype)
            onehot = jax.nn.one_hot(top_idx, E, dtype=x.dtype)
            w_te = jnp.einsum('tk,tke->te', top_w, onehot)
            g = jnp.einsum('th,eih->tei', x, gate_w)
            u = jnp.einsum('th,eih->tei', x, up_w)
            h = jax.nn.silu(g) * u
            y = jnp.einsum('tei,ehi,te->th', h, down_w, w_te)
            return y.reshape(B, S, Hd)
        key = jax.random.key(seed)
        ks = jax.random.split(key, 5)
        s = 0.02
        return {'hidden_states': jax.random.normal(ks[0], (2, 128, H), dtype=jnp.float32), 'router_w': jax.random.normal(ks[1], (E, H), dtype=jnp.float32) * s, 'gate_w': jax.random.normal(ks[2], (E, I, H), dtype=jnp.float32) * s, 'up_w': jax.random.normal(ks[3], (E, I, H), dtype=jnp.float32) * s, 'down_w': jax.random.normal(ks[4], (E, H, I), dtype=jnp.float32) * s}
    _L3_ffn_all = _L3_ffn_setup()
    _L3_ffn_in = {k: v for k, v in _L3_ffn_all.items() if k in ('router_w', 'gate_w', 'up_w', 'down_w')}
    del _L3_ffn_all
    return {'x': x, 'ctx_1024': ctx_1024, 'mask_BxSxS2_bk1': mask_BxSxS2_bk1, 'mask_Bx1x1xS2_fk0': mask_Bx1x1xS2_fk0, 'L0_attn_Wq': _L0_attn_in['Wq'], 'L0_attn_bq': _L0_attn_in['bq'], 'L0_attn_Wk': _L0_attn_in['Wk'], 'L0_attn_bk': _L0_attn_in['bk'], 'L0_attn_Wv': _L0_attn_in['Wv'], 'L0_attn_bv': _L0_attn_in['bv'], 'L0_attn_Wo': _L0_attn_in['Wo'], 'L0_attn_bo': _L0_attn_in['bo'], 'L0_xattn_Wq': _L0_xattn_in['Wq'], 'L0_xattn_Wk': _L0_xattn_in['Wk'], 'L0_xattn_Wv': _L0_xattn_in['Wv'], 'L0_xattn_Wo': _L0_xattn_in['Wo'], 'L0_xattn_sn_bias': _L0_xattn_in['sn_bias'], 'L0_ffn_router_W': _L0_ffn_in['router_W'], 'L0_ffn_router_b': _L0_ffn_in['router_b'], 'L0_ffn_sW1': _L0_ffn_in['sW1'], 'L0_ffn_sb1': _L0_ffn_in['sb1'], 'L0_ffn_sW2': _L0_ffn_in['sW2'], 'L0_ffn_sb2': _L0_ffn_in['sb2'], 'L0_ffn_eW1': _L0_ffn_in['eW1'], 'L0_ffn_eb1': _L0_ffn_in['eb1'], 'L0_ffn_eW2': _L0_ffn_in['eW2'], 'L0_ffn_eb2': _L0_ffn_in['eb2'], 'L1_attn_Wqkv': _L1_attn_in['Wqkv'], 'L1_attn_Wproj': _L1_attn_in['Wproj'], 'L1_attn_bproj': _L1_attn_in['bproj'], 'L1_attn_alpha': _L1_attn_in['alpha'], 'L1_attn_beta': _L1_attn_in['beta'], 'L1_attn_gamma': _L1_attn_in['gamma'], 'L1_attn_A': _L1_attn_in['A'], 'L1_attn_Wphi1': _L1_attn_in['Wphi1'], 'L1_attn_bphi1': _L1_attn_in['bphi1'], 'L1_attn_Wphi2': _L1_attn_in['Wphi2'], 'L1_attn_bphi2': _L1_attn_in['bphi2'], 'L1_attn_Wpsi1': _L1_attn_in['Wpsi1'], 'L1_attn_bpsi1': _L1_attn_in['bpsi1'], 'L1_attn_ln_g': _L1_attn_in['ln_g'], 'L1_attn_ln_b': _L1_attn_in['ln_b'], 'L1_attn_Wpsi2': _L1_attn_in['Wpsi2'], 'L1_attn_bpsi2': _L1_attn_in['bpsi2'], 'L1_attn_mixing': _L1_attn_in['mixing'], 'L1_attn_temp_scale': _L1_attn_in['temp_scale'], 'L1_xattn_ln1_g': _L1_xattn_in['ln1_g'], 'L1_xattn_ln1_b': _L1_xattn_in['ln1_b'], 'L1_xattn_ln2_g': _L1_xattn_in['ln2_g'], 'L1_xattn_ln2_b': _L1_xattn_in['ln2_b'], 'L1_xattn_Wq': _L1_xattn_in['Wq'], 'L1_xattn_Wkv': _L1_xattn_in['Wkv'], 'L1_xattn_Wo': _L1_xattn_in['Wo'], 'L1_ffn_w_gate': _L1_ffn_in['w_gate'], 'L1_ffn_w_up': _L1_ffn_in['w_up'], 'L1_ffn_w_down': _L1_ffn_in['w_down'], 'L2_attn_norm1_w': _L2_attn_in['norm1_w'], 'L2_attn_norm2_w': _L2_attn_in['norm2_w'], 'L2_attn_g_wq': _L2_attn_in['g_wq'], 'L2_attn_g_kv_down': _L2_attn_in['g_kv_down'], 'L2_attn_g_k_up': _L2_attn_in['g_k_up'], 'L2_attn_g_v_up': _L2_attn_in['g_v_up'], 'L2_attn_g_wo': _L2_attn_in['g_wo'], 'L2_attn_l_wq': _L2_attn_in['l_wq'], 'L2_attn_l_wk': _L2_attn_in['l_wk'], 'L2_attn_l_wv': _L2_attn_in['l_wv'], 'L2_attn_l_wo': _L2_attn_in['l_wo'], 'L2_xattn_gamma_x': _L2_xattn_in['gamma_x'], 'L2_xattn_beta_x': _L2_xattn_in['beta_x'], 'L2_xattn_gamma_l': _L2_xattn_in['gamma_l'], 'L2_xattn_beta_l': _L2_xattn_in['beta_l'], 'L2_xattn_Wq': _L2_xattn_in['Wq'], 'L2_xattn_Wkv': _L2_xattn_in['Wkv'], 'L2_xattn_Wo': _L2_xattn_in['Wo'], 'L2_ffn_w_freq_real': _L2_ffn_in['w_freq_real'], 'L2_ffn_w_freq_imag': _L2_ffn_in['w_freq_imag'], 'L2_ffn_bias': _L2_ffn_in['bias'], 'L3_attn_ln_gamma': _L3_attn_in['ln_gamma'], 'L3_attn_ln_beta': _L3_attn_in['ln_beta'], 'L3_attn_w_qkv': _L3_attn_in['w_qkv'], 'L3_attn_w_out': _L3_attn_in['w_out'], 'L3_attn_b_out': _L3_attn_in['b_out'], 'L3_xattn_Wq': _L3_xattn_in['Wq'], 'L3_xattn_bq': _L3_xattn_in['bq'], 'L3_xattn_Wk': _L3_xattn_in['Wk'], 'L3_xattn_bk': _L3_xattn_in['bk'], 'L3_xattn_Wv': _L3_xattn_in['Wv'], 'L3_xattn_bv': _L3_xattn_in['bv'], 'L3_xattn_Wo': _L3_xattn_in['Wo'], 'L3_xattn_bo': _L3_xattn_in['bo'], 'L3_ffn_router_w': _L3_ffn_in['router_w'], 'L3_ffn_gate_w': _L3_ffn_in['gate_w'], 'L3_ffn_up_w': _L3_ffn_in['up_w'], 'L3_ffn_down_w': _L3_ffn_in['down_w']}

def reference(x, ctx_1024, mask_BxSxS2_bk1, mask_Bx1x1xS2_fk0, L0_attn_Wq, L0_attn_bq, L0_attn_Wk, L0_attn_bk, L0_attn_Wv, L0_attn_bv, L0_attn_Wo, L0_attn_bo, L0_xattn_Wq, L0_xattn_Wk, L0_xattn_Wv, L0_xattn_Wo, L0_xattn_sn_bias, L0_ffn_router_W, L0_ffn_router_b, L0_ffn_sW1, L0_ffn_sb1, L0_ffn_sW2, L0_ffn_sb2, L0_ffn_eW1, L0_ffn_eb1, L0_ffn_eW2, L0_ffn_eb2, L1_attn_Wqkv, L1_attn_Wproj, L1_attn_bproj, L1_attn_alpha, L1_attn_beta, L1_attn_gamma, L1_attn_A, L1_attn_Wphi1, L1_attn_bphi1, L1_attn_Wphi2, L1_attn_bphi2, L1_attn_Wpsi1, L1_attn_bpsi1, L1_attn_ln_g, L1_attn_ln_b, L1_attn_Wpsi2, L1_attn_bpsi2, L1_attn_mixing, L1_attn_temp_scale, L1_xattn_ln1_g, L1_xattn_ln1_b, L1_xattn_ln2_g, L1_xattn_ln2_b, L1_xattn_Wq, L1_xattn_Wkv, L1_xattn_Wo, L1_ffn_w_gate, L1_ffn_w_up, L1_ffn_w_down, L2_attn_norm1_w, L2_attn_norm2_w, L2_attn_g_wq, L2_attn_g_kv_down, L2_attn_g_k_up, L2_attn_g_v_up, L2_attn_g_wo, L2_attn_l_wq, L2_attn_l_wk, L2_attn_l_wv, L2_attn_l_wo, L2_xattn_gamma_x, L2_xattn_beta_x, L2_xattn_gamma_l, L2_xattn_beta_l, L2_xattn_Wq, L2_xattn_Wkv, L2_xattn_Wo, L2_ffn_w_freq_real, L2_ffn_w_freq_imag, L2_ffn_bias, L3_attn_ln_gamma, L3_attn_ln_beta, L3_attn_w_qkv, L3_attn_w_out, L3_attn_b_out, L3_xattn_Wq, L3_xattn_bq, L3_xattn_Wk, L3_xattn_bk, L3_xattn_Wv, L3_xattn_bv, L3_xattn_Wo, L3_xattn_bo, L3_ffn_router_w, L3_ffn_gate_w, L3_ffn_up_w, L3_ffn_down_w):
    import jax
    import jax.numpy as jnp

    def _L0_attn_ref(x, Wq, bq, Wk, bk, Wv, bv, Wo, bo):
        import jax, jax.numpy as jnp
        import numpy as np
        import math
        D_MODEL = 128
        N_HEADS = 16
        HEAD_DIM = D_MODEL // N_HEADS

        def alibi_slopes(n_heads: int) -> jnp.ndarray:

            def pow2_slopes(n):
                start = 2 ** (-2 ** (-(math.log2(n) - 3)))
                return [start * start ** i for i in range(n)]
            if math.log2(n_heads).is_integer():
                s = pow2_slopes(n_heads)
            else:
                c = 2 ** math.floor(math.log2(n_heads))
                s = pow2_slopes(c)
                s.extend(pow2_slopes(2 * c)[0::2][:n_heads - c])
            return jnp.array(s, dtype=jnp.float32)
        B, T, C = x.shape
        H, D = (N_HEADS, HEAD_DIM)
        scale = D ** (-0.5)
        q = (x @ Wq + bq).reshape(B, T, H, D).transpose(0, 2, 1, 3)
        k = (x @ Wk + bk).reshape(B, T, H, D).transpose(0, 2, 1, 3)
        v = (x @ Wv + bv).reshape(B, T, H, D).transpose(0, 2, 1, 3)
        scores = jnp.einsum('bhqd,bhkd->bhqk', q, k) * scale
        pos = (jnp.arange(T)[:, None] - jnp.arange(T)[None, :]).astype(jnp.float32)
        bias = alibi_slopes(H)[:, None, None] * pos
        scores = scores + bias[None]
        causal = jnp.tril(jnp.ones((T, T), dtype=bool))
        scores = jnp.where(causal, scores, -jnp.inf)
        attn = jax.nn.softmax(scores, axis=-1)
        out = jnp.einsum('bhqk,bhkd->bhqd', attn, v)
        out = out.transpose(0, 2, 1, 3).reshape(B, T, C)
        return out @ Wo + bo

    def _L0_xattn_ref(iQ, iK, iV, mask, Wq, Wk, Wv, Wo, sn_bias):
        import jax, jax.numpy as jnp
        import numpy as np
        from math import sqrt
        B, NQ, SK, ISIZE, HSIZE, OSIZE, H = (4, 256, 256, 128, 128, 128, 16)
        D = HSIZE // H
        IEPS = 1e-32
        NEG = -1e+32
        b, nq, _ = iQ.shape
        sk = iK.shape[1]
        q = (iQ @ Wq.T).reshape(b, nq, H, D).transpose(0, 2, 1, 3)
        k = (iK @ Wk.T).reshape(b, sk, H, D).transpose(0, 2, 1, 3)
        v = (iV @ Wv.T).reshape(b, sk, H, D).transpose(0, 2, 1, 3)
        scores = jnp.einsum('bhqd,bhkd->bhqk', q, k) / sqrt(D)
        scores = jnp.where(mask[:, None, :, :], NEG, scores)
        t = jax.nn.relu(scores + sn_bias)
        t = t * t
        attn = t / (t.sum(-1, keepdims=True) + IEPS)
        o = jnp.einsum('bhqk,bhkd->bhqd', attn, v)
        o = o.transpose(0, 2, 1, 3).reshape(b, nq, HSIZE)
        return o @ Wo.T

    def _L0_ffn_ref(x, router_W, router_b, sW1, sb1, sW2, sb2, eW1, eb1, eW2, eb2):
        import jax, jax.numpy as jnp
        import numpy as np
        B, L, D = (2, 256, 128)
        E = 15
        H = D * 1
        K = 3
        T = 1.0
        b, l, d = x.shape
        n = b * l
        xt = x.reshape(n, d)
        shared = jax.nn.relu(xt @ sW1 + sb1) @ sW2 + sb2
        logits = xt @ router_W + router_b
        probs = jax.nn.softmax(logits / T, axis=-1)
        top_p, top_i = jax.lax.top_k(probs, K)
        cw = jnp.zeros((n, E), dtype=probs.dtype)
        cw = cw.at[jnp.arange(n)[:, None], top_i].set(top_p)
        h = jax.nn.relu(jnp.einsum('nd,edh->neh', xt, eW1) + eb1)
        ye = jnp.einsum('neh,ehd->ned', h, eW2) + eb2
        routed = jnp.einsum('ned,ne->nd', ye, cw)
        return (shared + routed).reshape(b, l, d)

    def _L1_attn_ref(x, Wqkv, Wproj, bproj, alpha, beta, gamma, A, Wphi1, bphi1, Wphi2, bphi2, Wpsi1, bpsi1, ln_g, ln_b, Wpsi2, bpsi2, mixing, temp_scale):
        import jax, jax.numpy as jnp
        import numpy as np
        B, N, C = (2, 256, 128)
        H = 16
        HD = C // H
        KA_IN = 2 * HD
        KA_OUT = HD
        T = 4
        KA_HID = KA_IN // 2
        KA_O = KA_OUT // T
        TEMPERATURE = 0.72
        SCALE = HD ** (-0.5)
        LN_EPS = 1e-05
        Bx, Nx, Cx = x.shape
        qkv = (x @ Wqkv).reshape(Bx, Nx, 3, H, HD).transpose(2, 0, 3, 1, 4)
        q, k, v = (qkv[0], qkv[1], qkv[2])
        attn = jnp.einsum('bhnd,bhmd->bhnm', q, k) * (SCALE / TEMPERATURE)
        attn = attn * alpha[None, :, None, None] + beta[None, :, None, None]
        attn = jax.nn.softmax(attn, axis=-1) * gamma[None, :, None, None]
        qk = jnp.concatenate([q.mean(-2), k.mean(-2)], -1).reshape(Bx * H, KA_IN)
        Ax = jnp.einsum('md,tde->tme', qk, A)
        phi = jax.nn.silu(jnp.einsum('md,tdh->tmh', qk, Wphi1) + bphi1[:, None, :])
        phi = jnp.einsum('tmh,tho->tmo', phi, Wphi2) + bphi2[:, None, :]
        psi = jnp.einsum('tme,teg->tmg', Ax, Wpsi1) + bpsi1[:, None, :]
        mu = psi.mean(-1, keepdims=True)
        var = ((psi - mu) ** 2).mean(-1, keepdims=True)
        psi = (psi - mu) / jnp.sqrt(var + LN_EPS) * ln_g[:, None, :] + ln_b[:, None, :]
        psi = jax.nn.gelu(psi, approximate=False)
        psi = jnp.einsum('tmg,tgo->tmo', psi, Wpsi2) + bpsi2[:, None, :]
        terms = phi * psi * temp_scale * mixing[:, None, None]
        ka = jnp.transpose(terms, (1, 0, 2)).reshape(Bx, H, 1, HD)
        enhanced_v = v * (1.0 + ka)
        out = jnp.einsum('bhnm,bhmd->bhnd', attn, enhanced_v)
        out = out.transpose(0, 2, 1, 3).reshape(Bx, Nx, Cx)
        return out @ Wproj + bproj

    def _L1_xattn_ref(image_embeds, latents, ln1_g, ln1_b, ln2_g, ln2_b, Wq, Wkv, Wo):
        import jax, jax.numpy as jnp
        import numpy as np
        DIM = 128
        DIM_HEAD = 64
        HEADS = 16
        INNER = DIM_HEAD * HEADS
        EPS = 1e-05

        def layer_norm(x, g, b):
            m = jnp.mean(x, axis=-1, keepdims=True)
            v = jnp.mean(jnp.square(x - m), axis=-1, keepdims=True)
            return (x - m) * jax.lax.rsqrt(v + EPS) * g + b
        B, S_lat, _ = latents.shape
        x = layer_norm(image_embeds, ln1_g, ln1_b)
        l = layer_norm(latents, ln2_g, ln2_b)
        q = l @ Wq
        kv_in = jnp.concatenate([x, l], axis=1)
        kv = kv_in @ Wkv
        k, v = jnp.split(kv, 2, axis=-1)

        def to_heads(t):
            return t.reshape(t.shape[0], t.shape[1], HEADS, DIM_HEAD).transpose(0, 2, 1, 3)
        q, k, v = (to_heads(q), to_heads(k), to_heads(v))
        scale = 1.0 / np.sqrt(np.sqrt(DIM_HEAD))
        w = jnp.einsum('bhqd,bhkd->bhqk', q * scale, k * scale)
        w = jax.nn.softmax(w.astype(jnp.float32), axis=-1).astype(q.dtype)
        out = jnp.einsum('bhqk,bhkd->bhqd', w, v)
        out = out.transpose(0, 2, 1, 3).reshape(B, S_lat, INNER)
        return out @ Wo

    def _L1_ffn_ref(x, w_gate, w_up, w_down):
        import jax, jax.numpy as jnp
        import numpy as np
        DIM = 128
        HIDDEN = 384
        SCALE = 1.0 / 127.0

        def _dequant(w_int, dtype):
            return w_int.astype(dtype) * jnp.asarray(SCALE, dtype)
        wg = _dequant(w_gate, x.dtype)
        wu = _dequant(w_up, x.dtype)
        wd = _dequant(w_down, x.dtype)
        gate = jnp.einsum('bsd,hd->bsh', x, wg)
        up = jnp.einsum('bsd,hd->bsh', x, wu)
        h = jax.nn.silu(gate) * up
        return jnp.einsum('bsh,dh->bsd', h, wd)

    def _L2_attn_ref(hidden, norm1_w, norm2_w, g_wq, g_kv_down, g_k_up, g_v_up, g_wo, l_wq, l_wk, l_wv, l_wo):
        import jax, jax.numpy as jnp
        import numpy as np
        D = 128
        H = 16
        KVH = 4
        HD = D // H
        LAT = 32
        WIN = 32
        B, S = (1, 256)
        BASE_G, BASE_L = (1000000.0, 10000.0)
        EPS = 1e-06

        def rmsnorm(x, w):
            return x * jax.lax.rsqrt(jnp.mean(x * x, axis=-1, keepdims=True) + EPS) * w

        def qk_norm(x):
            return x * jax.lax.rsqrt(jnp.mean(x * x, axis=-1, keepdims=True) + EPS)

        def rope(x, base):
            s, hd = (x.shape[-2], x.shape[-1])
            inv_freq = 1.0 / base ** (jnp.arange(0, hd, 2, dtype=jnp.float32) / hd)
            freqs = jnp.arange(s, dtype=jnp.float32)[:, None] * inv_freq[None, :]
            cos, sin = (jnp.cos(freqs), jnp.sin(freqs))
            xe, xo = (x[..., ::2], x[..., 1::2])
            out = jnp.stack([xe * cos - xo * sin, xe * sin + xo * cos], axis=-1)
            return out.reshape(x.shape)

        def split_heads(x, n_heads):
            b, s, _ = x.shape
            return x.reshape(b, s, n_heads, HD).transpose(0, 2, 1, 3)

        def repeat_kv(x):
            return jnp.repeat(x, H // KVH, axis=1)

        def sdpa(q, k, v, mask):
            scores = jnp.einsum('bhqd,bhkd->bhqk', q, k) / np.sqrt(HD).astype(np.float32)
            scores = jnp.where(mask, scores, jnp.float32(-1e+30))
            probs = jax.nn.softmax(scores, axis=-1)
            return jnp.einsum('bhqk,bhkd->bhqd', probs, v)

        def merge_heads(x):
            b, h, s, hd = x.shape
            return x.transpose(0, 2, 1, 3).reshape(b, s, h * hd)

        def global_latent_attn(x, wq, w_kv_down, w_k_up, w_v_up, wo):
            q = split_heads(x @ wq, H)
            latent = x @ w_kv_down
            k = split_heads(latent @ w_k_up, KVH)
            v = split_heads(latent @ w_v_up, KVH)
            q, k = (rope(q, BASE_G), rope(k, BASE_G))
            q, k = (qk_norm(q), qk_norm(k))
            k, v = (repeat_kv(k), repeat_kv(v))
            i = jnp.arange(x.shape[1])
            causal = i[:, None] >= i[None, :]
            return merge_heads(sdpa(q, k, v, causal)) @ wo

        def local_gqa_attn(x, wq, wk, wv, wo):
            q = split_heads(x @ wq, H)
            k = split_heads(x @ wk, KVH)
            v = split_heads(x @ wv, KVH)
            q, k = (rope(q, BASE_L), rope(k, BASE_L))
            q, k = (qk_norm(q), qk_norm(k))
            k, v = (repeat_kv(k), repeat_kv(v))
            i = jnp.arange(x.shape[1])
            diff = i[:, None] - i[None, :]
            mask = (diff >= 0) & (diff < WIN)
            return merge_heads(sdpa(q, k, v, mask)) @ wo
        x = hidden
        x = x + global_latent_attn(rmsnorm(x, norm1_w), g_wq, g_kv_down, g_k_up, g_v_up, g_wo)
        x = x + local_gqa_attn(rmsnorm(x, norm2_w), l_wq, l_wk, l_wv, l_wo)
        return x

    def _L2_xattn_ref(x, latents, gamma_x, beta_x, gamma_l, beta_l, Wq, Wkv, Wo):
        import jax, jax.numpy as jnp
        import numpy as np
        DIM = 128
        HEAD_DIM = 64
        NUM_HEADS = 8
        INNER = HEAD_DIM * NUM_HEADS
        ROT_DIM = HEAD_DIM
        ROPE_BASE = 10000.0
        EPS = 1e-05

        def layer_norm(x, g, b):
            mu = jnp.mean(x, axis=-1, keepdims=True)
            var = jnp.var(x, axis=-1, keepdims=True)
            return (x - mu) * jax.lax.rsqrt(var + EPS) * g + b

        def rope_rotate_k(k):
            n = k.shape[1]
            half = ROT_DIM // 2
            inv_freq = 1.0 / ROPE_BASE ** (jnp.arange(0, ROT_DIM, 2, dtype=jnp.float32) / ROT_DIM)
            theta = jnp.arange(n, dtype=jnp.float32)[:, None] * inv_freq[None, :]
            angles = jnp.concatenate([theta, theta], axis=-1)
            cos = jnp.cos(angles)[None, :, None, :].astype(k.dtype)
            sin = jnp.sin(angles)[None, :, None, :].astype(k.dtype)
            k_rope, k_pass = (k[..., :ROT_DIM], k[..., ROT_DIM:])
            neg_half = jnp.concatenate([-k_rope[..., half:], k_rope[..., :half]], axis=-1)
            k_rope = k_rope * cos + neg_half * sin
            return jnp.concatenate([k_rope, k_pass], axis=-1)
        b, n, _ = x.shape
        m = latents.shape[1]
        h, d = (NUM_HEADS, HEAD_DIM)
        scale = d ** (-0.5)
        xn = layer_norm(x, gamma_x, beta_x)
        ln = layer_norm(latents, gamma_l, beta_l)
        q = (ln @ Wq).reshape(b, m, h, d)
        kv_x = xn @ Wkv
        k_x, v_x = (kv_x[..., :INNER], kv_x[..., INNER:])
        kv_l = ln @ Wkv
        k_l, v_l = (kv_l[..., :INNER], kv_l[..., INNER:])
        k_x = k_x.reshape(b, n, h, d)
        v_x = v_x.reshape(b, n, h, d)
        k_x = rope_rotate_k(k_x)
        q = jnp.transpose(q, (0, 2, 1, 3)) * scale
        k_x = jnp.transpose(k_x, (0, 2, 1, 3))
        v_x = jnp.transpose(v_x, (0, 2, 1, 3))
        k_l = jnp.transpose(k_l.reshape(b, m, h, d), (0, 2, 1, 3))
        v_l = jnp.transpose(v_l.reshape(b, m, h, d), (0, 2, 1, 3))
        k = jnp.concatenate([k_x, k_l], axis=2)
        v = jnp.concatenate([v_x, v_l], axis=2)
        sim = jnp.einsum('bhid,bhjd->bhij', q, k)
        attn = jax.nn.softmax(sim, axis=-1)
        out = jnp.einsum('bhij,bhjd->bhid', attn, v)
        out = jnp.transpose(out, (0, 2, 1, 3)).reshape(b, m, INNER)
        return out @ Wo

    def _L2_ffn_ref(x, w_freq_real, w_freq_imag, bias):
        import jax, jax.numpy as jnp
        import numpy as np
        B, N, D = (4, 256, 128)
        SPARSITY = 0.01
        w = jax.lax.complex(w_freq_real, w_freq_imag)
        x_freq = jnp.fft.fft(x, axis=-1)
        y_freq = jnp.einsum('bnd,do->bno', x_freq, w)
        y = jnp.real(jnp.fft.ifft(y_freq, axis=-1))
        return y + bias

    def _L3_attn_ref(x, ln_gamma, ln_beta, w_qkv, w_out, b_out):
        import jax, jax.numpy as jnp
        import numpy as np
        DIM = 128
        HEADS = 16
        DIM_HEAD = 64
        INNER = HEADS * DIM_HEAD

        def _attention(x, ln_gamma, ln_beta, w_qkv, w_out, b_out):
            b, n, _ = x.shape
            scale = DIM_HEAD ** (-0.5)
            mu = jnp.mean(x, axis=-1, keepdims=True)
            var = jnp.var(x, axis=-1, keepdims=True)
            xn = (x - mu) / jnp.sqrt(var + 1e-05) * ln_gamma + ln_beta
            qkv = jnp.einsum('bnd,ed->bne', xn, w_qkv)
            q, k, v = jnp.split(qkv, 3, axis=-1)
            reshape = lambda t: t.reshape(b, n, HEADS, DIM_HEAD).transpose(0, 2, 1, 3)
            q, k, v = (reshape(q) * scale, reshape(k), reshape(v))
            sim = jnp.einsum('bhid,bhjd->bhij', q, k)
            mask_value = -jnp.finfo(sim.dtype).max
            causal = jnp.triu(jnp.ones((n, n), dtype=bool), k=1)
            sim = jnp.where(causal, mask_value, sim)
            sim = sim - jax.lax.stop_gradient(jnp.max(sim, axis=-1, keepdims=True))
            attn = jax.nn.softmax(sim, axis=-1)
            out = jnp.einsum('bhij,bhjd->bhid', attn, v)
            out = out.transpose(0, 2, 1, 3).reshape(b, n, INNER)
            return jnp.einsum('bne,de->bnd', out, w_out) + b_out
        return _attention(x, ln_gamma, ln_beta, w_qkv, w_out, b_out)

    def _L3_xattn_ref(v, k, q, mask, Wq, bq, Wk, bk, Wv, bv, Wo, bo):
        import jax, jax.numpy as jnp
        import numpy as np
        B, S, D, H = (4, 256, 128, 16)
        DEPTH = D // H

        def _split_heads(x):
            b, s, _ = x.shape
            return x.reshape(b, s, H, DEPTH).transpose(0, 2, 1, 3)
        qh = _split_heads(q @ Wq + bq)
        kh = _split_heads(k @ Wk + bk)
        vh = _split_heads(v @ Wv + bv)
        logits = jnp.einsum('bhqd,bhkd->bhqk', qh, kh) / jnp.sqrt(jnp.asarray(DEPTH, dtype=qh.dtype))
        logits = logits + mask * -1000000000.0
        attn = jax.nn.softmax(logits, axis=-1)
        out = jnp.einsum('bhqk,bhkd->bhqd', attn, vh)
        out = out.transpose(0, 2, 1, 3).reshape(q.shape[0], -1, D)
        return out @ Wo + bo

    def _L3_ffn_ref(hidden_states, router_w, gate_w, up_w, down_w):
        import jax, jax.numpy as jnp
        import numpy as np
        H = 128
        I = 352
        E = 8
        TOP_K = 2

        def _moe(hidden_states, router_w, gate_w, up_w, down_w):
            B, S, Hd = hidden_states.shape
            x = hidden_states.reshape(-1, Hd)
            logits = x @ router_w.T
            probs = jax.nn.softmax(logits.astype(jnp.float32), axis=-1)
            top_w, top_idx = jax.lax.top_k(probs, TOP_K)
            top_w = top_w.astype(x.dtype)
            onehot = jax.nn.one_hot(top_idx, E, dtype=x.dtype)
            w_te = jnp.einsum('tk,tke->te', top_w, onehot)
            g = jnp.einsum('th,eih->tei', x, gate_w)
            u = jnp.einsum('th,eih->tei', x, up_w)
            h = jax.nn.silu(g) * u
            y = jnp.einsum('tei,ehi,te->th', h, down_w, w_te)
            return y.reshape(B, S, Hd)
        return _moe(hidden_states, router_w, gate_w, up_w, down_w)
    x = x + _L0_attn_ref(_layernorm(x, axis=-1), L0_attn_Wq, L0_attn_bq, L0_attn_Wk, L0_attn_bk, L0_attn_Wv, L0_attn_bv, L0_attn_Wo, L0_attn_bo)
    x = x + _L0_xattn_ref(_layernorm(x, axis=-1), ctx_1024, ctx_1024, mask_BxSxS2_bk1, L0_xattn_Wq, L0_xattn_Wk, L0_xattn_Wv, L0_xattn_Wo, L0_xattn_sn_bias)
    x = x + _L0_ffn_ref(_layernorm(x, axis=-1), L0_ffn_router_W, L0_ffn_router_b, L0_ffn_sW1, L0_ffn_sb1, L0_ffn_sW2, L0_ffn_sb2, L0_ffn_eW1, L0_ffn_eb1, L0_ffn_eW2, L0_ffn_eb2)
    x = x + _L1_attn_ref(_layernorm(x, axis=-1), L1_attn_Wqkv, L1_attn_Wproj, L1_attn_bproj, L1_attn_alpha, L1_attn_beta, L1_attn_gamma, L1_attn_A, L1_attn_Wphi1, L1_attn_bphi1, L1_attn_Wphi2, L1_attn_bphi2, L1_attn_Wpsi1, L1_attn_bpsi1, L1_attn_ln_g, L1_attn_ln_b, L1_attn_Wpsi2, L1_attn_bpsi2, L1_attn_mixing, L1_attn_temp_scale)
    x = x + _L1_xattn_ref(ctx_1024, _layernorm(x, axis=-1), L1_xattn_ln1_g, L1_xattn_ln1_b, L1_xattn_ln2_g, L1_xattn_ln2_b, L1_xattn_Wq, L1_xattn_Wkv, L1_xattn_Wo)
    x = x + _L1_ffn_ref(_layernorm(x, axis=-1), L1_ffn_w_gate, L1_ffn_w_up, L1_ffn_w_down)
    x = x + _L2_attn_ref(_layernorm(x, axis=-1), L2_attn_norm1_w, L2_attn_norm2_w, L2_attn_g_wq, L2_attn_g_kv_down, L2_attn_g_k_up, L2_attn_g_v_up, L2_attn_g_wo, L2_attn_l_wq, L2_attn_l_wk, L2_attn_l_wv, L2_attn_l_wo)
    x = x + _L2_xattn_ref(ctx_1024, _layernorm(x, axis=-1), L2_xattn_gamma_x, L2_xattn_beta_x, L2_xattn_gamma_l, L2_xattn_beta_l, L2_xattn_Wq, L2_xattn_Wkv, L2_xattn_Wo)
    x = x + _L2_ffn_ref(_layernorm(x, axis=-1), L2_ffn_w_freq_real, L2_ffn_w_freq_imag, L2_ffn_bias)
    x = x + _L3_attn_ref(_layernorm(x, axis=-1), L3_attn_ln_gamma, L3_attn_ln_beta, L3_attn_w_qkv, L3_attn_w_out, L3_attn_b_out)
    x = x + _L3_xattn_ref(ctx_1024, ctx_1024, _layernorm(x, axis=-1), mask_Bx1x1xS2_fk0, L3_xattn_Wq, L3_xattn_bq, L3_xattn_Wk, L3_xattn_bk, L3_xattn_Wv, L3_xattn_bv, L3_xattn_Wo, L3_xattn_bo)
    x = x + _L3_ffn_ref(_layernorm(x, axis=-1), L3_ffn_router_w, L3_ffn_gate_w, L3_ffn_up_w, L3_ffn_down_w)
    return x

_drawn_inputs = setup_inputs


def setup_inputs(seed=0):
    import zlib

    import numpy as np

    out = dict(_drawn_inputs(seed))
    spreads = {'L0_attn_bq': (0.0, 0.1),
     'L0_attn_bk': (0.0, 2.0),
     'L0_attn_bv': (0.0, 0.1),
     'L0_attn_bo': (0.0, 0.1),
     'L0_ffn_router_b': (0.0, 0.8),
     'L0_ffn_sb1': (0.0, 0.416),
     'L0_ffn_sb2': (0.0, 0.1),
     'L0_ffn_eb1': (0.0, 0.8),
     'L0_ffn_eb2': (0.0, 0.544),
     'L1_attn_bproj': (0.0, 0.1),
     'L1_attn_alpha': (1.0, 0.2),
     'L1_attn_beta': (1.0, 0.6),
     'L1_attn_gamma': (1.0, 0.2),
     'L1_attn_bphi1': (0.0, 0.8),
     'L1_attn_bphi2': (0.0, 0.8),
     'L1_attn_bpsi1': (0.0, 0.8),
     'L1_attn_ln_g': (1.0, 0.6),
     'L1_attn_ln_b': (0.0, 0.8),
     'L1_attn_bpsi2': (0.0, 0.8),
     'L1_attn_mixing': (0.25, 0.6),
     'L1_xattn_ln1_g': (1.0, 0.2),
     'L1_xattn_ln1_b': (0.0, 0.1),
     'L1_xattn_ln2_g': (1.0, 0.2),
     'L1_xattn_ln2_b': (0.0, 0.1),
     'L2_attn_norm1_w': (1.0, 0.6),
     'L2_attn_norm2_w': (1.0, 0.6),
     'L2_xattn_gamma_x': (1.0, 0.6),
     'L2_xattn_beta_x': (0.0, 0.8),
     'L2_xattn_gamma_l': (1.0, 0.6),
     'L2_xattn_beta_l': (0.0, 0.8),
     'L3_attn_ln_gamma': (1.0, 0.6),
     'L3_attn_ln_beta': (0.0, 0.8),
     'L3_xattn_bq': (0.0, 0.8),
     'L3_xattn_bk': (0.0, 2.0),
     'L3_xattn_bv': (0.0, 2.0),
     'L3_xattn_bo': (0.0, 2.0)}
    factors = {'L0_ffn_router_W': 4.473,
     'L0_ffn_eW1': 8.0,
     'L0_ffn_eW2': 8.0,
     'L1_attn_A': 4.768,
     'L1_attn_Wphi1': 3.68,
     'L1_attn_Wphi2': 4.945,
     'L1_attn_Wpsi1': 4.535,
     'L1_attn_Wpsi2': 3.657,
     'L2_attn_g_wq': 23.582,
     'L2_attn_g_kv_down': 8.0,
     'L2_attn_g_k_up': 22.56,
     'L2_attn_g_v_up': 8.0,
     'L2_attn_g_wo': 8.0,
     'L2_attn_l_wq': 58.54,
     'L2_attn_l_wk': 64.0,
     'L2_attn_l_wv': 8.0,
     'L2_attn_l_wo': 8.0,
     'L2_xattn_Wq': 8.0,
     'L2_xattn_Wkv': 8.0,
     'L2_xattn_Wo': 8.0,
     'L2_ffn_w_freq_real': 22.524,
     'L2_ffn_w_freq_imag': 22.655,
     'L2_ffn_bias': 200.0,
     'L3_attn_w_qkv': 8.0,
     'L3_attn_w_out': 8.0,
     'L3_attn_b_out': 184.598,
     'L3_xattn_Wq': 8.0,
     'L3_xattn_Wk': 8.0,
     'L3_xattn_Wv': 8.0,
     'L3_xattn_Wo': 8.0,
     'L3_ffn_router_w': 49.089,
     'L3_ffn_gate_w': 51.743,
     'L3_ffn_up_w': 46.741,
     'L3_ffn_down_w': 47.222}
    for name, (base, spread) in spreads.items():
        noise = np.random.default_rng([zlib.crc32(name.encode()), seed]).standard_normal(out[name].shape)
        drawn = base * np.exp(spread * noise) if base else spread * noise
        out[name] = jnp.asarray(drawn.astype(out[name].dtype))
    for name, factor in factors.items():
        out[name] = (out[name] * factor).astype(out[name].dtype)
    return out
```

```python
from contextlib import ExitStack, contextmanager

import numpy as np

import concourse.bass as bass
from concourse import mybir

F32 = mybir.dt.float32
F32R = mybir.dt.float32r
BF16 = mybir.dt.bfloat16
I32 = mybir.dt.int32
U8 = mybir.dt.uint8
ALU = mybir.AluOpType
ACT = mybir.ActivationFunctionType
AX = mybir.AxisListType

B, N, D = 4, 512, 128
NC = 77
NT = N // 128
HEADS = 16
STRIP = 32
BANK = 512
COPIES = 3
MAX_ROW, BY_KEY, BY_QUERY, MASKED = 24, 25, 27, 29
NEG = -1e30
LN_EPS = 1e-5
RMS_EPS = 1e-6

STAGES = (0, 11)
BATCHES = B
X_OVERRIDE = None


PLAIN = [4 * c + s for c in range(4) for s in range(4)]
GROUPED = [4 * s + c for c in range(4) for s in range(4)]


class Pack:

    def __init__(self):
        self.at, self.width, self.parts = {}, 0, []

    def add(self, name, a):
        a = np.asarray(a)
        a = a.reshape(a.shape[0], -1)
        self.at[name] = (self.width, a.shape[1], a.shape[0])
        self.width += a.shape[1]
        self.parts.append(a)

    def array(self):
        out = np.zeros((128, self.width), self.parts[0].dtype)
        for (col, wide, rows), a in zip(self.at.values(), self.parts):
            out[:rows, col:col + wide] = a
        return out


def strips(w, order, extra=None):
    rows = w.shape[0]
    out = np.zeros((rows, len(order), STRIP), w.dtype)
    for n in range(COPIES):
        out[:, :, 8 * n:8 * n + 8] = w.reshape(rows, -1, 8)[:, order, :]
    for feature, v in (extra or {}).items():
        out[:, :, feature] = v[:, order]
    return out.reshape(rows, -1)


def split_columns():
    cols = {}
    for name, low, ones in (("q", (slice(16, 24), BY_KEY + 1, BY_QUERY + 1), (MASKED, MASKED + 1)),
                            ("k", (slice(8, 16), MASKED + 1), (MAX_ROW, BY_QUERY, BY_QUERY + 1))):
        a, b, bias = np.zeros((4, STRIP), np.float32), np.ones((4, STRIP), np.float32), \
            np.zeros((4, STRIP), np.float32)
        for f in low:
            a[:, f], b[:, f] = 1, -1
        for f in ones:
            bias[:, f] = 1
        cols[name] = [v.reshape(128, 1) for v in (a, b, bias)]
    return cols


def strip_column(head_values, order, extra):
    n = len(order)
    out = np.zeros((n, STRIP), np.float32)
    if head_values is not None:
        out[:, 0:8 * COPIES] = np.tile(head_values.reshape(-1, 8)[order], (1, COPIES))
    for row, v in extra.items():
        out[:, row] = v if np.isscalar(v) else np.asarray(v)[order]
    return np.ascontiguousarray(out.reshape(n // 4, 128).T)


def by_head(w, order):
    return w.reshape(w.shape[0], -1, 8)[:, order, :].reshape(w.shape[0], -1)


def swap_pairs(w):
    return w.reshape(w.shape[0], -1, 2)[:, :, ::-1].reshape(w.shape[0], -1)


def chunks_of_rows(w):
    n = w.shape[0] // 128
    return w.reshape(n, 128, -1).transpose(1, 0, 2).reshape(128, -1)


def row(v):
    return np.asarray(v, np.float32).reshape(1, -1)


def col(v):
    return np.asarray(v, np.float32).reshape(-1, 1)


def rope_tables(base):
    inv = (1.0 / np.float32(base) ** (np.arange(0, 8, 2, dtype=np.float32) / np.float32(8))).astype(np.float32)
    f = np.arange(N, dtype=np.float32)[:, None] * inv[None, :]
    cos, sin = np.cos(f), np.sin(f)
    c, s = np.zeros((4, STRIP, N), np.float32), np.zeros((4, STRIP, N), np.float32)
    for d in range(8 * COPIES):
        c[:, d] = cos[:, d % 8 // 2]
        s[:, d] = sin[:, d % 8 // 2] * (-1.0 if d % 2 == 0 else 1.0)
    return c.reshape(128, N), s.reshape(128, N)


def context_rope_tables():
    half = 32
    inv = (1.0 / np.float32(10000.0) ** (np.arange(0, 64, 2, dtype=np.float32) / np.float32(64))).astype(np.float32)
    theta = np.arange(NC, dtype=np.float32)[:, None] * inv[None, :]
    c = np.concatenate([np.cos(theta)] * 2, 1).T
    s = np.concatenate([-np.sin(theta), np.sin(theta)], 1).T
    assert c.shape[0] == 2 * half
    return np.concatenate([c, c], 0), np.concatenate([s, s], 0)


def alibi_slopes():
    start = 2 ** (-2 ** (-(np.log2(HEADS) - 3)))
    return np.array([start * start ** i for i in range(HEADS)], np.float32)


def masks():
    p = Pack()
    i = np.arange(128)
    p.add("causal", np.where(i[None, :] <= i[:, None], 0, NEG).astype(np.float32))
    p.add("causal_t", np.where(i[None, :] >= i[:, None], 0, NEG).astype(np.float32))
    wide = np.arange(128 + STRIP)
    gap = i[:, None] + 32 - wide[None, :]
    p.add("local", np.where((gap >= 0) & (gap < 32), 0, NEG).astype(np.float32))
    gap = wide[None, :] - i[:, None]
    p.add("local_t", np.where((gap >= 0) & (gap < 32), 0, NEG).astype(np.float32))
    return p


def constants():
    p = Pack()
    i = np.arange(128)
    p.add("identity", np.eye(128, dtype=np.float32))
    same = (i[:, None] // STRIP == i[None, :] // STRIP) & (i[:, None] % STRIP < 8) & (i[None, :] % STRIP < 8 * COPIES)
    p.add("strip_mean", np.where(same, 1 / 8, 0).astype(np.float32))
    p.add("rms_eps", np.full((128, 1), RMS_EPS, np.float32))
    p.add("ones", np.ones((1, N), np.float32))
    p.add("ones_and_position", np.stack([np.ones(N), np.arange(N)]).astype(np.float32))
    for name, cols in split_columns().items():
        for part, v in zip(("a", "b", "bias"), cols):
            p.add(f"{name}_{part}", v)
    at = np.arange(128) % STRIP
    scale = np.where(at < 8 * COPIES, np.float32(8 ** -0.5 / 0.72), np.float32(1)).reshape(128, 1)
    for part in (0, 1):
        p.add("alpha_" + "ab"[part], np.repeat(split_columns()["q"][part] * scale, 4, axis=1))
    m = np.zeros((1, 4, STRIP), np.float32)
    m[:, :, MASKED:MASKED + 2] = -1e9 * np.sqrt(8.0)
    p.add("mask_row", m.reshape(1, -1))
    a = 2 * np.pi * ((i[:, None] * i[None, :]) % 128) / 128
    p.add("dft_cos", np.cos(a).astype(np.float32))
    p.add("dft_sin", np.sin(a).astype(np.float32))
    p.add("dft_minus_sin", -np.sin(a).astype(np.float32))
    return p


def packs(w):
    f = {k: np.asarray(v) for k, v in w.items()}
    out = {}

    p = out["L0_attn"] = Pack()
    p.add("wq", strips(f["L0_attn_Wq"], PLAIN))
    p.add("wk", strips(f["L0_attn_Wk"], PLAIN))
    p.add("wv", f["L0_attn_Wv"])
    p.add("wo", f["L0_attn_Wo"])
    slope = alibi_slopes() * np.float32(np.sqrt(8.0))
    none, one = np.zeros(HEADS, np.float32), np.ones(HEADS, np.float32)
    nothing = np.zeros((1, 128), np.float32)
    p.add("q_add", strips(np.concatenate([row(f["L0_attn_bq"]), nothing]), PLAIN,
                          {BY_KEY: np.stack([-slope, none]), BY_KEY + 1: np.stack([-slope, none]),
                           BY_QUERY: np.stack([none, slope]), BY_QUERY + 1: np.stack([none, slope])}))
    p.add("k_add", strips(np.concatenate([row(f["L0_attn_bk"]), nothing]), PLAIN,
                          {BY_KEY: np.stack([none, one]), BY_KEY + 1: np.stack([none, one])}))
    p.add("bv", row(f["L0_attn_bv"]))
    p.add("bo", row(f["L0_attn_bo"]))

    p = out["L0_xattn"] = Pack()
    p.add("wq", strips(f["L0_xattn_Wq"].T, PLAIN))
    p.add("wk", strips(f["L0_xattn_Wk"].T, PLAIN))
    p.add("wv", f["L0_xattn_Wv"].T)
    p.add("wo", f["L0_xattn_Wo"].T)
    p.add("sn_bias", np.broadcast_to(f["L0_xattn_sn_bias"].reshape(1, 1), (128, 1)))

    p = out["L0_ffn"] = Pack()
    p.add("w1", np.concatenate([f["L0_ffn_eW1"], f["L0_ffn_sW1"][None]]).transpose(1, 0, 2))
    p.add("w2", np.concatenate([f["L0_ffn_eW2"], f["L0_ffn_sW2"][None]]).transpose(1, 0, 2))
    p.add("b1", np.concatenate([f["L0_ffn_eb1"], f["L0_ffn_sb1"][None]]).T)
    p.add("b2", np.concatenate([f["L0_ffn_eb2"], f["L0_ffn_sb2"][None]]))
    p.add("router", f["L0_ffn_router_W"])
    p.add("router_b", row(f["L0_ffn_router_b"]))

    p = out["L1_attn"] = Pack()
    wqkv = f["L1_attn_Wqkv"]
    p.add("wq", strips(wqkv[:, 0:128], PLAIN))
    p.add("wk", strips(wqkv[:, 128:256], PLAIN))
    p.add("wv", wqkv[:, 256:384])
    p.add("wo", f["L1_attn_Wproj"])
    p.add("bo", row(f["L1_attn_bproj"]))
    p.add("alpha", strip_column(np.repeat(f["L1_attn_alpha"], 8), PLAIN, {BY_QUERY: 1.0, BY_QUERY + 1: 1.0}))
    beta = row(f["L1_attn_beta"])
    p.add("q_add", strips(nothing, PLAIN, {BY_QUERY: beta, BY_QUERY + 1: beta}))
    p.add("wqk_mean", wqkv[:, 0:256].reshape(128, 2, 16, 8).transpose(0, 2, 1, 3))
    p.add("ka_a", f["L1_attn_A"].transpose(1, 0, 2))
    p.add("ka_phi1", f["L1_attn_Wphi1"].transpose(1, 0, 2))
    p.add("ka_bphi1", f["L1_attn_bphi1"].T)
    p.add("ka_phi2", f["L1_attn_Wphi2"].transpose(1, 0, 2))
    p.add("ka_psi1", f["L1_attn_Wpsi1"].transpose(1, 0, 2))
    p.add("ka_psi2", f["L1_attn_Wpsi2"].transpose(1, 0, 2))
    over_heads = lambda a: np.broadcast_to(np.asarray(a).reshape(1, -1), (16, np.asarray(a).size))
    p.add("ka_bpsi1", over_heads(f["L1_attn_bpsi1"]))
    p.add("ka_g", over_heads(f["L1_attn_ln_g"]))
    p.add("ka_b", over_heads(f["L1_attn_ln_b"]))
    p.add("ka_bphi2", over_heads(f["L1_attn_bphi2"]))
    p.add("ka_bpsi2", over_heads(f["L1_attn_bpsi2"]))
    p.add("ka_mix", over_heads(np.repeat(f["L1_attn_mixing"], 2)))
    p.add("ka_temp", over_heads(f["L1_attn_temp_scale"]))
    p.add("gamma", f["L1_attn_gamma"].reshape(16, 1))

    p = out["L1_xattn"] = Pack()
    p.add("wq", f["L1_xattn_Wq"])
    p.add("wk", f["L1_xattn_Wkv"][:, 0:1024])
    p.add("wv", f["L1_xattn_Wkv"][:, 1024:2048])
    p.add("wo", chunks_of_rows(f["L1_xattn_Wo"]))
    p.add("g_ctx", col(f["L1_xattn_ln1_g"]))
    p.add("b_ctx", col(f["L1_xattn_ln1_b"]))
    p.add("g", col(f["L1_xattn_ln2_g"]))
    p.add("b", col(f["L1_xattn_ln2_b"]))

    p = out["L1_ffn"] = Pack()
    p.add("gate", f["L1_ffn_w_gate"].T)
    p.add("up", f["L1_ffn_w_up"].T)
    p.add("down", chunks_of_rows(f["L1_ffn_w_down"].T))

    for kind, base, key in (("g", 1e6, "L2_attn_g"), ("l", 1e4, "L2_attn_l")):
        p = out[key] = Pack()
        wq = f[f"L2_attn_{kind}_wq"]
        p.add("wq", strips(wq, GROUPED))
        p.add("wq_swapped", strips(swap_pairs(wq), GROUPED))
        kv = list(range(4))
        if kind == "g":
            p.add("down", f["L2_attn_g_kv_down"])
            wk, wv = f["L2_attn_g_k_up"], f["L2_attn_g_v_up"]
        else:
            wk, wv = f["L2_attn_l_wk"], f["L2_attn_l_wv"]
        p.add("wk", strips(wk, kv))
        p.add("wk_swapped", strips(swap_pairs(wk), kv))
        p.add("wv", by_head(wv, [h // 4 for h in GROUPED]))
        p.add("wo", f[f"L2_attn_{kind}_wo"].reshape(16, 8, 128)[GROUPED].reshape(128, 128))
        p.add("g", col(f["L2_attn_norm1_w" if kind == "g" else "L2_attn_norm2_w"]))
        c, s = rope_tables(base)
        p.add("cos", c)
        p.add("sin", s)

    p = out["L2_xattn"] = Pack()
    wk = f["L2_xattn_Wkv"][:, 0:512]
    p.add("wq", f["L2_xattn_Wq"])
    p.add("wk", wk)
    p.add("wk_swapped", wk.reshape(128, 8, 2, 32)[:, :, ::-1, :].reshape(128, 512))
    p.add("wv", f["L2_xattn_Wkv"][:, 512:1024])
    p.add("wo", chunks_of_rows(f["L2_xattn_Wo"]))
    p.add("g_ctx", col(f["L2_xattn_gamma_x"]))
    p.add("b_ctx", col(f["L2_xattn_beta_x"]))
    p.add("g", col(f["L2_xattn_gamma_l"]))
    p.add("b", col(f["L2_xattn_beta_l"]))
    c, s = context_rope_tables()
    p.add("cos", c)
    p.add("sin", s)

    p = out["L2_ffn"] = Pack()
    p.add("real", f["L2_ffn_w_freq_real"])
    p.add("imag", f["L2_ffn_w_freq_imag"])
    p.add("bo", row(f["L2_ffn_bias"]))

    p = out["L3_attn"] = Pack()
    w3 = f["L3_attn_w_qkv"].T
    p.add("wq", w3[:, 0:1024])
    p.add("wk", w3[:, 1024:2048])
    p.add("wv", w3[:, 2048:3072])
    p.add("wo", chunks_of_rows(f["L3_attn_w_out"].T))
    p.add("bo", row(f["L3_attn_b_out"]))
    p.add("g", col(f["L3_attn_ln_gamma"]))
    p.add("b", col(f["L3_attn_ln_beta"]))

    p = out["L3_xattn"] = Pack()
    p.add("wq", strips(f["L3_xattn_Wq"], PLAIN))
    p.add("wk", strips(f["L3_xattn_Wk"], PLAIN))
    p.add("wv", f["L3_xattn_Wv"])
    p.add("wo", f["L3_xattn_Wo"])
    p.add("q_add", strips(row(f["L3_xattn_bq"]), PLAIN))
    p.add("k_add", strips(row(f["L3_xattn_bk"]), PLAIN))
    p.add("bv", row(f["L3_xattn_bv"]))
    p.add("bo", row(f["L3_xattn_bo"]))

    p = out["L3_ffn"] = Pack()
    down = np.zeros((8, 384, 128), np.float32)
    down[:, 0:352] = f["L3_ffn_down_w"].transpose(0, 2, 1)
    p.add("down", down.reshape(8, 3, 128, 128).transpose(2, 0, 1, 3))
    p.add("router", f["L3_ffn_router_w"].T)

    p = out["L3_ffn_gate_up"] = Pack()
    p.add("gate", f["L3_ffn_gate_w"].transpose(2, 0, 1))
    p.add("up", f["L3_ffn_up_w"].transpose(2, 0, 1))
    return out



BIG_Q, BIG_K, BIG_V, BIG_O = 16 * N, 16 * 592, 5 * 16 * 128 + 128, 8 * N
SLOT = 4288

SCORE_BANK, EXPO_BANK, VALUE_BANK, TURN_BANK, OUT_BANK = 0, 2, 4, 6, 7

SIGNALS = [
    "step_v", "alpha_ready", "rope_in", "variance", "deviation", "normed", "turned", "features", "ctx_ready", "filled",
    "projected", "taken_v", "taken_s", "latent", "latent_kept", "rotated", "squared", "mean_square", "root",
    "divided", "rounded", "operand_ready", "score", "maximum", "guard_ready", "guard_turned", "guarded", "expo", "relu",
    "probs", "valued", "finished", "out", "added", "keep_loaded", "keep_turned", "keep_ready",
    "logits", "shifted", "exps", "gates", "gates_turned", "gates_kept", "up", "hidden", "down", "summed",
    "converted", "ka_tensor", "ka_vector", "ka_scalar", "ka_moved",
]


class Core:

    def __init__(self, nc, ctx, dram, layouts):
        self.nc, self.dram, self.layouts = nc, dram, layouts
        self.const_at = constants().at

        def sb(name, shape, dt=F32):
            return ctx.enter_context(nc.sbuf_tensor(name, shape, dt))

        self.consts = sb("consts", [128, constants().width])
        self.x = sb("x", [128, NT, D])
        self.h = sb("h", [128, NT, D])
        self.xn = sb("xn", [128, NT, D])
        self.xt = sb("xt", [128, N])
        self.ctx_rows, self.ctx_n = self.xn[:, 0, :], self.xn[:, 1, :]
        self.ctx_raw_t = sb("ctx_raw_t", [128, 128])
        self.ctx_norm_t = sb("ctx_norm_t", [128, 80])
        self.ctx_t = sb("ctx_t", [128, 80])
        self.mask_rows = sb("mask_rows", [128, NT * NC], U8)
        self.mask_vec = sb("mask_vec", [1, 128])
        self.v = sb("v", [128, BIG_V])
        self.o = sb("o", [128, BIG_O])
        self.slot = [sb("weights_even", [128, SLOT]), sb("weights_odd", [128, SLOT])]
        self.guard_thin = sb("guard_thin", [128, 2, NT, 128])
        self.guard_wide = sb("guard_wide", [128, 2, NT, 65])
        self.max_ctx = sb("max_ctx", [128, 2, NT])
        self.p = sb("p", [128, 4, N])
        self.recip = sb("recip", [64, N])
        self.tmp = sb("tmp", [128, 2, N])
        self.keep_rows = self.tmp[:, 0, 0:NT * NC]
        self.stats = sb("stats", [128, NT, 6])
        self.mv = sb("mv", [128, NT, 2])
        self.small = sb("small", [128, 16, NT])
        self.ka = sb("ka", [128, 512])
        self.scale_o = sb("scale_o", [64, 2])
        self.identity_b = sb("identity_b", [128, 128], BF16)
        self.mask_at = masks().at
        self.masks_b = {n: sb(n + "_b", [128, wide], BF16) for n, (_, wide, _) in self.mask_at.items()}
        self.ps = ctx.enter_context(nc.psum_tensor("ps", [128, 8, BANK], F32))

        self.sets = [{s: ctx.enter_context(nc.semaphore(f"{s}_{half}")) for s in SIGNALS}
                     for half in ("even", "odd")]
        self.loaded = {k: ctx.enter_context(nc.semaphore(f"loaded_{k}")) for k in layouts}
        self.x_loaded = ctx.enter_context(nc.semaphore("x_loaded"))
        self.consts_loaded = ctx.enter_context(nc.semaphore("consts_loaded"))
        self.consts_made = ctx.enter_context(nc.semaphore("consts_made"))
        self.loop_sems = ([s for half in self.sets for s in half.values()]
                          + list(self.loaded.values()) + [self.x_loaded])

    @contextmanager
    def operands(self, thin, number):
        with ExitStack() as ctx:
            def sb(name, wide, dt=F32):
                return ctx.enter_context(self.nc.sbuf_tensor(f"{name}_{number}", [128, wide], dt))

            self.q_parts = sb("q_parts", 4 * N, F32R)
            self.k_parts = sb("k_parts", 4 * N, F32R)
            self.q_guarded = sb("q_guarded", 2 * N, F32R)
            self.spare = sb("spare", 5 * N)
            self.gate_up = sb("gate_up", 16 * 352)
            if not thin:
                ctx.close()
                self.q, self.k = sb("q", BIG_Q), sb("k", BIG_K)
            yield

    def c(self, name, rows=None):
        at, wide, r = self.const_at[name]
        return self.consts[0:rows or r, at:at + wide]


class Sublayer:

    def __init__(self, core, key, number):
        self.core, self.key, self.number = core, key, number
        self.s = core.sets[number % 2]
        self.slot = core.slot[number % 2]
        self.at = core.layouts[key]

    def w(self, name):
        at, wide, rows = self.at[name]
        return self.slot[0:rows, at:at + wide]


def chained(eng, sem):
    done = [0]

    def link(ins):
        ins.then_inc(sem, 1)
        done[0] += 1
        eng.wait_ge(sem, done[0])
    return link



class Norm:

    def __init__(self, sub, kind="ln", source=None, again=None, gain=None, offset=None, keep=None):
        self.sub, self.kind, self.again, self.keep = sub, kind, again, keep
        self.source = source if source is not None else sub.core.x
        self.gain, self.offset = gain, offset
        self.roots = 2 if again is not None else 1

    def vector(self, e, link):
        co, s, src = self.sub.core, self.sub.s, self.source
        mean, var = co.mv[:, :, 0], co.mv[:, :, 1]
        sm = co.small
        for i in range(NT):
            last = e.bn_stats(co.stats[:, i, :], src[:, i, :])
        link(last)
        for i in range(NT):
            last = e.bn_aggr(co.mv[:, i, :], co.stats[:, i, :])
        link(last)
        if self.kind == "rms":
            link(e.tensor_tensor(sm[:, 4, :], mean, mean, ALU.mult))
            link(e.tensor_tensor(sm[:, 5, :], sm[:, 4, :], var, ALU.add))
            e.tensor_scalar(sm[:, 0, :], sm[:, 5, :], RMS_EPS, None, ALU.add).then_inc(s["variance"], 1)
        else:
            e.tensor_scalar(sm[:, 0, :], var, LN_EPS, None, ALU.add).then_inc(s["variance"], 1)
        e.wait_ge(s["deviation"], 1)
        link(e.reciprocal(sm[:, 2, :], sm[:, 1, :]))
        scale = sm[:, 2, :]
        if self.again is not None:
            link(e.tensor_tensor(sm[:, 3, :], var, scale, ALU.mult))
            link(e.tensor_tensor(sm[:, 4, :], sm[:, 3, :], scale, ALU.mult))
            e.tensor_scalar(sm[:, 0, :], sm[:, 4, :], self.again, None, ALU.add).then_inc(s["variance"], 1)
            e.wait_ge(s["deviation"], 2)
            link(e.reciprocal(sm[:, 5, :], sm[:, 1, :]))
            link(e.tensor_tensor(sm[:, 6, :], sm[:, 5, :], scale, ALU.mult))
            if self.keep is not None:
                for i in range(NT):
                    e.tensor_scalar(self.keep[:, i, :], src[:, i, :], mean[:, i:i + 1], scale[:, i:i + 1],
                                    ALU.subtract, ALU.mult)
            scale = sm[:, 6, :]
        for i in range(NT):
            if self.kind == "rms":
                ins = e.tensor_scalar(co.xn[:, i, :], src[:, i, :], scale[:, i:i + 1], None, ALU.mult)
            else:
                ins = e.tensor_scalar(co.xn[:, i, :], src[:, i, :], mean[:, i:i + 1], scale[:, i:i + 1],
                                      ALU.subtract, ALU.mult)
            ins.then_inc(s["normed"], 1)

    def scalar(self, e):
        co, s, sm = self.sub.core, self.sub.s, self.sub.core.small
        for n in range(self.roots):
            e.wait_ge(s["variance"], n + 1)
            e.activation(sm[:, 1, :], sm[:, 0, :], ACT.Sqrt).then_inc(s["deviation"], 1)
        e.wait_ge(s["turned"], 1)
        wide = co.ps[:, TURN_BANK, :]
        if self.gain is None:
            ins = e.activation(co.xt[:, :], wide, ACT.Copy)
        else:
            ins = e.activation(co.xt[:, :], wide, ACT.Identity, scale=self.gain,
                               bias=self.offset if self.offset is not None else 0.0)
        ins.then_inc(s["features"], 1)

    def tensor(self, e):
        co, s = self.sub.core, self.sub.s
        for i in range(NT):
            e.wait_ge(s["normed"], i + 1)
            last = e.transpose(co.ps[:, TURN_BANK, i * 128:i * 128 + 128], co.xn[:, i, :], co.c("identity"))
        last.then_inc(s["turned"], 1)



class Attention:
    def __init__(self, sub, wide, heads=HEADS, own=True, ctx=False, pattern="full", scale=1.0, grouped=False,
                 relu=False, alibi=False, ctx_mask=False, rope=False, latent=False, ctx_rope=False, alpha=False,
                 value_scale=False):
        self.sub, self.wide, self.heads, self.own, self.ctx, self.pattern = sub, wide, heads, own, ctx, pattern
        self.scale, self.grouped, self.relu, self.alibi, self.ctx_mask = scale, grouped, relu, alibi, ctx_mask
        self.rope, self.latent, self.ctx_rope, self.alpha = rope, latent, ctx_rope, alpha
        self.value_scale = value_scale
        self.kw = (N if own else 0) + ((80 if wide else 128) if ctx else 0)
        self.units = heads if wide else heads // 4
        self.per_unit = 1 if wide else 4
        self.per_group = 1 if wide else 8
        self.vw = heads * 128
        self.key_tiles = (list(range(NT)) if own else []) + (["ctx"] if ctx else [])
        self.jobs = self.projections()
        self.plan()

    def rows(self, pos, guard=False):
        if self.wide:
            return slice(0, 65 if guard else 64)
        return slice(STRIP * (pos % 4), STRIP * (pos % 4) + STRIP)

    def q_col(self, pos):
        return (pos if self.wide else pos // 4) * N

    def k_col(self, pos, tile):
        chunk = pos if self.wide else 0 if self.grouped else pos // 4
        at = (N if self.own else 0) if tile == "ctx" else tile * 128
        return chunk * self.kw + at

    def v_cols(self, pos, tile):
        at = (len(self.key_tiles) - 1 if tile == "ctx" else tile) * self.vw + pos * 128
        return slice(at, at + 128)

    def projections(self):
        jobs = []
        chunks = self.heads // 2 if self.wide else 4
        if not self.rope:
            jobs += [("q", c) for c in range(chunks)]
            if self.own:
                jobs += [("k", c) for c in range(chunks)]
        if self.ctx:
            jobs += [("kc", c) for c in range(chunks)]
        for t in self.key_tiles:
            jobs += [("v", t, half) for half in range(self.heads // 8 if self.wide else 1)]
        return jobs

    def takers(self, j):
        job = self.jobs[j]
        if self.ctx_rope and job[0] == "kc":
            return {"v": None}
        if self.wide and job[0] in ("q", "k", "kc"):
            return {"v": 0, "s": 1}
        if job[0] != "v":
            return {"s": None, "v": None}
        return {"vs"[j % 2]: None}

    def plan(self):
        ev, self.n = [], {}

        def score_tiles(u):
            if self.relu or u >= self.units:
                return []
            heads = range(u * self.per_unit, (u + 1) * self.per_unit)
            return [(p, t) for p in heads for t in self.key_tiles_of_scores()]

        def expo_tiles(u):
            heads = range(u * self.per_unit, (u + 1) * self.per_unit)
            return [(p, t) for p in heads for t in self.key_tiles]

        def value(pt):
            ev.append(("value",) + pt)
            if pt[1] == self.key_tiles[-1] and pt[0] % self.per_group == self.per_group - 1:
                ev.append(("finish", pt[0] // self.per_group))

        for st in score_tiles(0):
            ev.append(("score",) + st)
        if not self.relu:
            ev.append(("guard", 0))
        before = None
        for u in range(self.units):
            tiles, ahead = expo_tiles(u), score_tiles(u + 1)
            done = 0
            for i, t in enumerate(tiles):
                ev.append(("expo",) + t)
                want = -(-(i + 1) * len(ahead) // max(1, len(tiles) - 1))
                while done < min(want, len(ahead)):
                    ev.append(("score",) + ahead[done])
                    done += 1
                if i == len(tiles) - 1 and ahead:
                    ev.append(("guard", u + 1))
                if before:
                    value(before)
                before = t
        value(before)
        count, self.steps = {}, []
        self.upto = {}
        for e in ev:
            k = e[0]
            self.steps.append(e + (count.get(k, 0),))
            count[k] = count.get(k, 0) + 1
            if k in ("score", "expo"):
                self.upto[(k, e[1] // self.per_unit)] = count[k]
            if k == "value":
                self.upto[(k, e[1] // self.per_group)] = count[k]

    def key_tiles_of_scores(self):
        return (list(range(NT)) if self.own else []) + (["ctx"] if self.ctx else [])

    def score_keys(self, qt):
        if self.pattern == "causal":
            return 0, 128 * (qt + 1), 128 * qt, self.sub.core.masks_b["causal"][:, :]
        if self.pattern == "local":
            first = max(0, 128 * qt - STRIP)
            n = 128 * (qt + 1) - first
            return first, n, 0, self.sub.core.masks_b["local"][:, 160 - n:160]
        return 0, N, None, None

    def expo_queries(self, kt):
        if kt == "ctx" or self.pattern == "full":
            return 0, N, None
        if self.pattern == "causal":
            return 128 * kt, N - 128 * kt, self.sub.core.masks_b["causal_t"][:, :]
        n = min(160, N - 128 * kt)
        return 128 * kt, n, self.sub.core.masks_b["local_t"][:, 0:n]


    def fill(self, e):
        co, s = self.sub.core, self.sub.s
        tiles = len(self.key_tiles)
        if self.wide:
            v = co.v[:, 0:tiles * self.vw].rearrange("p (t c) -> p t c", c=128)
            e.memset(v[:, :, 64:128], 1.0).then_inc(s["filled"], 1)
            e.wait_ge(s["filled"], 1)
            e.memset(co.k[64:65, 0:self.heads * self.kw], 1.0).then_inc(s["filled"], 1)
            return
        e.memset(co.v[:, 0:tiles * self.vw + 128], 0.0).then_inc(s["filled"], 1)
        e.wait_ge(s["filled"], 1)
        for t in range(tiles):
            for g in range(2):
                at = t * self.vw + g * 1024
                ones = co.v[:, at:at + 8 * 136].rearrange("p (h r) -> p h r", r=136)[:, :, 64:72]
                last = e.memset(ones, 1.0)
        last.then_inc(s["filled"], 1)

    def project_tensor(self, e):
        co, s, w = self.sub.core, self.sub.s, self.sub.w
        e.wait_ge(s["features"], 1)
        ctx_t = self.ctx_source()
        if self.ctx and ctx_t is co.ctx_t:
            e.wait_ge(s["ctx_ready"], 1)
        ksrc = co.xt[:, :]
        if self.latent:
            e.matmul(co.ps[0:32, OUT_BANK, :], w("down"), co.xt[:, :], start=True, stop=True)\
                .then_inc(s["latent"], 1)
            e.wait_ge(s["latent_kept"], 1)
            ksrc = co.recip[0:32, :]
        if self.rope:
            self.rope_tensor(e, ksrc)
        taken_v = taken_s = 0
        history = []
        for j, job in enumerate(self.jobs):
            if j >= 6:
                e.wait_ge(s["taken_v"], history[j - 6][0])
                e.wait_ge(s["taken_s"], history[j - 6][1])
            elif j == 0 and self.rope:
                e.wait_ge(s["operand_ready"], 5)
            bank = co.ps[:, j % 6, :]
            kind = job[0]
            if kind in ("q", "k"):
                c = job[1]
                more = kind + "_add" in self.sub.at
                last = e.matmul(bank, w("w" + kind)[:, c * 128:c * 128 + 128], co.xt[:, :], start=True,
                                stop=not more)
                if more:
                    add = w(kind + "_add")
                    last = e.matmul(bank, add[:, c * 128:c * 128 + 128],
                                    co.c("ones_and_position")[0:add.shape[0], :], start=False, stop=True)
            elif kind == "kc":
                c = job[1]
                n = NC if self.wide else 128
                last = e.matmul(bank[:, 0:n], w("wk")[:, c * 128:c * 128 + 128], ctx_t[:, 0:n], start=True,
                                stop=not self.ctx_mask)
                if self.ctx_mask:
                    e.matmul(bank[:, 0:n], w("k_add")[:, c * 128:c * 128 + 128], co.c("ones")[:, 0:n],
                             start=False, stop=False)
                    last = e.matmul(bank[:, 0:n], co.c("mask_row"), co.mask_vec[:, 0:n], start=False, stop=True)
                if self.ctx_rope:
                    last = e.matmul(bank[:, 128:128 + NC], w("wk_swapped")[:, c * 128:c * 128 + 128],
                                    ctx_t[:, 0:NC], start=True, stop=True, skip_group_check=True)
            else:
                _, t, half = job
                m = NC if t == "ctx" else 128
                lhs = ctx_t[:, 0:NC] if t == "ctx" else ksrc[:, t * 128:t * 128 + 128]
                n = 512 if self.wide else 128
                biased = "bv" in self.sub.at
                last = e.matmul(bank[0:m, 0:n], lhs, w("wv")[:, half * n:half * n + n], start=True,
                                stop=not biased)
                if biased:
                    last = e.matmul(bank[0:m, 0:n], co.c("ones")[:, 0:m], w("bv"), start=False, stop=True)
            last.then_inc(s["projected"], 1)
            taken_v += "v" in self.takers(j)
            taken_s += "s" in self.takers(j)
            history.append((taken_v, taken_s))
        e.wait_ge(s["taken_v"], taken_v)
        e.wait_ge(s["taken_s"], taken_s)
        e.wait_ge(s["filled"], 2)

    def ctx_source(self):
        co = self.sub.core
        return co.ctx_t if "g_ctx" in self.sub.at else co.ctx_raw_t

    def take(self, e, job, part, copy):
        co, w = self.sub.core, self.sub.w
        bank = co.ps[:, self.jobs.index(job) % 6, :]
        kind = job[0]
        if kind in ("q", "k", "kc"):
            c = job[1]
            n = N if kind != "kc" else NC if self.wide else 128
            if self.wide:
                pos = 2 * c + part
                dst, at = (co.q, self.q_col(pos)) if kind == "q" else \
                    (co.k, self.k_col(pos, "ctx" if kind == "kc" else 0))
                return copy(dst[0:64, at:at + n], bank[64 * part:64 * part + 64, 0:n])
            rounded = co.tmp[:, self.jobs.index(job) % 2, 0:n]
            side = "q" if kind == "q" else "k"
            by = lambda part: co.ka[:, 480 + 4 * part + c:481 + 4 * part + c] if self.alpha and side == "q" \
                else co.c(side + "_" + "ab"[part])
            if part == "round":
                return e.activation(rounded.bitcast(F32R), bank[:, 0:n], ACT.Identity, scale=by(1),
                                    bias=co.c(side + "_bias"))
            dst, at = (co.q_parts, self.q_col(4 * c)) if kind == "q" else \
                (co.k_parts, self.k_col(4 * c, "ctx" if kind == "kc" else 0))
            return e.scalar_tensor_tensor(out=dst[:, at:at + n], in0=bank[:, 0:n], scalar=by(0),
                                          in1=rounded, op0=ALU.mult, op1=ALU.add)
        _, t, half = job
        m = NC if t == "ctx" else 128
        if self.wide:
            at = self.v_cols(half * 8, t).start
            dst = co.v[0:m, at:at + 8 * 128].rearrange("p (h c) -> p h c", c=128)[:, :, 0:64]
            return copy(dst, bank[0:m, 0:512].rearrange("p (h c) -> p h c", c=64))
        at = self.v_cols(0, t).start
        for g in range(2):
            dst = co.v[0:m, at + g * 1024:at + g * 1024 + 8 * 136].rearrange("p (h r) -> p h r", r=136)
            last = copy(dst[:, :, 0:8], bank[0:m, g * 64:g * 64 + 64].rearrange("p (h c) -> p h c", c=8))
        return last

    def project_vector(self, e, link):
        co, s, w = self.sub.core, self.sub.s, self.sub.w
        if self.alpha:
            for part in (0, 1):
                e.tensor_tensor(co.ka[:, 480 + 4 * part:484 + 4 * part], w("alpha"), co.c("alpha_" + "ab"[part]),
                                ALU.mult).then_inc(s["alpha_ready"], 1)
            e.wait_ge(s["alpha_ready"], 2)
        if self.rope:
            self.rope_vector(e, link)

        taken_s = 0
        for j, job in enumerate(self.jobs):
            taken_s += "s" in self.takers(j)
            if "v" not in self.takers(j):
                continue
            if self.takers(j) == {"s": None, "v": None}:
                e.wait_ge(s["taken_s"], taken_s)
                self.take(e, job, "add", None).then_inc(s["taken_v"], 1)
                continue
            e.wait_ge(s["projected"], j + 1)
            if job[0] == "v":
                e.wait_ge(s["filled"], 2)
            if not (self.ctx_rope and job[0] == "kc"):
                self.take(e, job, 0, e.tensor_copy).then_inc(s["taken_v"], 1)
                continue
            bank, t = co.ps[:, j % 6, :], co.tmp
            e.wait_ge(s["taken_v"], sum("v" in self.takers(i) for i in range(j)))
            link(e.tensor_tensor(t[:, 0, 0:NC], bank[:, 0:NC], w("cos"), ALU.mult))
            link(e.tensor_tensor(t[:, 1, 0:NC], bank[:, 128:128 + NC], w("sin"), ALU.mult))
            for part in range(2):
                at = self.k_col(2 * job[1] + part, "ctx")
                r = slice(64 * part, 64 * part + 64)
                last = e.tensor_tensor(co.k[0:64, at:at + NC], t[r, 0, 0:NC], t[r, 1, 0:NC], ALU.add)
            last.then_inc(s["taken_v"], 1)

    def project_scalar(self, e):
        co, s, w = self.sub.core, self.sub.s, self.sub.w
        if self.latent:
            e.wait_ge(s["latent"], 1)
            e.activation(co.recip[0:32, :], co.ps[0:32, OUT_BANK, :], ACT.Copy).then_inc(s["latent_kept"], 1)
        if self.rope:
            self.rope_scalar(e)
        if self.alpha:
            e.wait_ge(s["alpha_ready"], 2)

        for j, job in enumerate(self.jobs):
            if "s" not in self.takers(j):
                continue
            e.wait_ge(s["projected"], j + 1)
            if self.takers(j) == {"s": None, "v": None}:
                if j >= 2:
                    e.wait_ge(s["taken_v"], sum("v" in self.takers(i) for i in range(j - 1)))
                self.take(e, job, "round", None).then_inc(s["taken_s"], 1)
                continue
            if job[0] == "v":
                e.wait_ge(s["filled"], 2)
            self.take(e, job, 1, lambda out, in_: e.activation(out, in_, ACT.Copy)).then_inc(s["taken_s"], 1)


    def rope_operand(self, j):
        co = self.sub.core
        return co.q_parts[:, j * N:j * N + N] if j < 4 else co.k_parts[:, 0:N]

    def rope_product(self, j):
        return self.sub.core.spare[:, j * N:(j + 1) * N]

    def rope_tensor(self, e, ksrc):
        co, s, w = self.sub.core, self.sub.s, self.sub.w

        def rotate(j):
            if j >= 3:
                e.wait_ge(s["rotated"], j - 2)
            for half, name in ((0, ""), (1, "_swapped")):
                lhs = w("wq" + name)[:, j * 128:j * 128 + 128] if j < 4 else w("wk" + name)
                last = e.matmul(co.ps[:, 2 * (j % 3) + half, :], lhs, co.xt[:, :] if j < 4 else ksrc,
                                start=True, stop=True)
            last.then_inc(s["rope_in"], 1)

        rotate(0)
        for j in range(5):
            if j < 4:
                rotate(j + 1)
            e.wait_ge(s["squared"], j + 1)
            if j >= 1:
                e.wait_ge(s["root"], j)
            e.matmul(co.ps[:, TURN_BANK, :], co.c("strip_mean"), co.o[:, (j % 2) * N:(j % 2) * N + N],
                     start=True, stop=True).then_inc(s["mean_square"], 1)

    def rope_vector(self, e, link):
        co, s, w = self.sub.core, self.sub.s, self.sub.w
        t = co.o[:, 2 * N:4 * N].rearrange("p (a n) -> p a n", a=2)

        def rotate(j):
            e.wait_ge(s["rope_in"], j + 1)
            if j >= 1:
                e.wait_ge(s["rotated"], j)
            link(e.tensor_tensor(t[:, 0, :], co.ps[:, 2 * (j % 3), :], w("cos"), ALU.mult))
            link(e.tensor_tensor(t[:, 1, :], co.ps[:, 2 * (j % 3) + 1, :], w("sin"), ALU.mult))
            e.tensor_tensor(self.rope_product(j), t[:, 0, :], t[:, 1, :], ALU.add).then_inc(s["rotated"], 1)

        def split(j):
            e.wait_ge(s["rounded"], j + 1)
            e.scalar_tensor_tensor(out=self.rope_operand(j), in0=self.rope_product(j),
                                   scalar=co.c("q_a" if j < 4 else "k_a"), in1=co.tmp[:, j % 2, :],
                                   op0=ALU.mult, op1=ALU.add).then_inc(s["operand_ready"], 1)

        rotate(0)
        for j in range(5):
            if j < 4:
                rotate(j + 1)
            e.wait_ge(s["root"], j + 1)
            root = co.o[:, (4 + j % 2) * N:(5 + j % 2) * N]
            link(e.reciprocal(root, root))
            e.tensor_tensor(self.rope_product(j), self.rope_product(j), root, ALU.mult)\
                .then_inc(s["divided"], 1)
            if j >= 1:
                split(j - 1)
        split(4)

    def rope_scalar(self, e):
        co, s = self.sub.core, self.sub.s

        def round_(j):
            e.wait_ge(s["divided"], j + 1)
            if j >= 2:
                e.wait_ge(s["operand_ready"], j - 1)
            side = "q" if j < 4 else "k"
            e.activation(co.tmp[:, j % 2, :].bitcast(F32R), self.rope_product(j), ACT.Identity,
                         scale=co.c(side + "_b"), bias=co.c(side + "_bias")).then_inc(s["rounded"], 1)

        for j in range(5):
            e.wait_ge(s["rotated"], j + 1)
            if j >= 2:
                e.wait_ge(s["mean_square"], j - 1)
            e.activation(co.o[:, (j % 2) * N:(j % 2) * N + N], self.rope_product(j), ACT.Square)\
                .then_inc(s["squared"], 1)
            if j >= 1:
                round_(j - 1)
            e.wait_ge(s["mean_square"], j + 1)
            e.activation(co.o[:, (4 + j % 2) * N:(5 + j % 2) * N], co.ps[:, TURN_BANK, :], ACT.Sqrt,
                         bias=co.c("rms_eps")).then_inc(s["root"], 1)
        round_(4)


    def guard(self):
        return self.sub.core.guard_wide if self.wide else self.sub.core.guard_thin

    def guard_col(self, pos):
        return 64 if self.wide else STRIP * (pos % 4) + MAX_ROW

    def attend_tensor(self, e):
        co, s = self.sub.core, self.sub.s
        ps = co.ps
        q, k = (co.q, co.k) if self.wide else (co.q_parts, co.k_parts)
        for step in self.steps:
            kind, n = step[0], step[-1]
            if kind == "score":
                _, pos, t, _ = step
                r, qc = self.rows(pos), self.q_col(pos)
                bank = ps[:, SCORE_BANK + n % 2, :]
                if n >= 2:
                    e.wait_ge(s["maximum"], n - 1)
                if t == "ctx":
                    kc = self.k_col(pos, "ctx")
                    for i in range(NT):
                        m = NC if self.wide else 80
                        last = e.matmul(bank[:, i * 80:i * 80 + m], q[r, qc + i * 128:qc + i * 128 + 128],
                                        k[r, kc:kc + m], start=True, stop=True, skip_group_check=True)
                else:
                    first, m, mc, mask = self.score_keys(t)
                    kc = self.k_col(pos, 0) + first
                    last = e.matmul(bank[:, 0:m], q[r, qc + t * 128:qc + t * 128 + 128], k[r, kc:kc + m],
                                    start=True, stop=mask is None, skip_group_check=True)
                    if mask is not None:
                        last = e.matmul(bank[:, mc:mc + mask.shape[1]], co.identity_b[:, :], mask,
                                        start=False, stop=True, skip_group_check=True)
                last.then_inc(s["score"], 1)
            elif kind == "guard":
                u = step[1]
                e.wait_ge(s["maximum"], self.upto[("score", u)])
                if self.own and self.ctx:
                    e.wait_ge(s["guard_ready"], (u + 1) * self.per_unit)
                if n >= 1:
                    e.wait_ge(s["guarded"], n)
                g = self.guard()
                m = g.shape[3]
                for i in range(NT):
                    last = e.transpose(ps[0:m, TURN_BANK, i * 128:i * 128 + 128], g[:, u % 2, i, :],
                                       co.c("identity"))
                last.then_inc(s["guard_turned"], 1)
            elif kind == "expo":
                _, pos, t, _ = step
                u = pos // self.per_unit
                first, m, mask = self.expo_queries(t)
                keys = NC if t == "ctx" and self.wide else 128
                bank = ps[0:keys, EXPO_BANK + n % 2, 0:m]
                if n >= 2:
                    e.wait_ge(s["relu" if self.relu else "probs"], n - 1)
                if not self.relu:
                    e.wait_ge(s["guarded"], u + 1)
                r, kc = self.rows(pos, guard=True), self.k_col(pos, t)
                if self.wide or self.relu:
                    moving = q[r, self.q_col(pos) + first:self.q_col(pos) + first + m]
                else:
                    at = u % 2 * N + first
                    moving = co.q_guarded[r, at:at + m]
                last = e.matmul(bank, k[r, kc:kc + keys], moving, start=True, stop=mask is None,
                                skip_group_check=True)
                if mask is not None:
                    last = e.matmul(bank[:, 0:mask.shape[1]], co.identity_b[:, :], mask, start=False, stop=True,
                                    skip_group_check=True)
                last.then_inc(s["expo"], 1)
            elif kind == "value":
                _, pos, t, _ = step
                g = pos // self.per_group
                first, m, _ = self.expo_queries(t)
                keys = NC if t == "ctx" else 128
                e.wait_ge(s["probs"], n + 1)
                opens = t == self.key_tiles[0] and pos % self.per_group == 0
                closes = t == self.key_tiles[-1] and pos % self.per_group == self.per_group - 1
                if opens and g >= 2:
                    e.wait_ge(s["finished"], g - 1)
                e.matmul(ps[:, VALUE_BANK + g % 2, first:first + m], co.v[0:keys, self.v_cols(pos, t)],
                         co.p[0:keys, n % 4, 0:m], start=opens, stop=closes, skip_group_check=True)\
                    .then_inc(s["valued"], 1)

    def attend_vector(self, e, link):
        co, s = self.sub.core, self.sub.s
        ps = co.ps
        if self.relu:
            e.wait_ge(s["keep_ready"], 1)
        for step in self.steps:
            kind, n = step[0], step[-1]
            if kind == "score":
                _, pos, t, _ = step
                u = pos // self.per_unit
                e.wait_ge(s["score"], n + 1)
                bank = ps[:, SCORE_BANK + n % 2, :]
                g = self.guard()[:, u % 2, :, self.guard_col(pos)]
                if t == "ctx":
                    out = co.max_ctx[:, n % 2, :] if self.own else g
                    ins = e.tensor_reduce(out, bank[:, 0:NT * 80].rearrange("p (i k) -> p i k", k=80)[:, :, 0:NC], AX.X,
                                          ALU.max, negate=True)
                    ins.then_inc(s["maximum"], 1)
                    if self.own:
                        e.wait_ge(s["maximum"], n + 1)
                        e.tensor_tensor(g, g, out, ALU.min).then_inc(s["guard_ready"], 1)
                else:
                    _, m, _, _ = self.score_keys(t)
                    e.tensor_reduce(g[:, t:t + 1], bank[:, 0:m], AX.X, ALU.max, negate=True)\
                        .then_inc(s["maximum"], 1)
            elif kind == "guard":
                u = step[1]
                e.wait_ge(s["guard_turned"], u + 1)
                if self.wide:
                    qc = self.q_col(u)
                    e.tensor_copy(co.q[64:65, qc:qc + N], ps[64:65, TURN_BANK, :]).then_inc(s["guarded"], 1)
                else:
                    if u >= 2:
                        e.wait_ge(s["expo"], self.upto[("expo", u - 2)])
                    e.tensor_tensor(co.q_guarded[:, u % 2 * N:u % 2 * N + N],
                                    co.q_parts[:, u * N:u * N + N].bitcast(F32),
                                    ps[:, TURN_BANK, :], ALU.add).then_inc(s["guarded"], 1)
            elif kind == "expo" and self.relu:
                e.wait_ge(s["relu"], n + 1)
                r = co.tmp[0:NC, n % 2, :]
                masked = co.spare[0:NC, (1 + n % 2) * N:(2 + n % 2) * N]
                link(e.tensor_tensor(masked, r, co.spare[0:NC, 0:N], ALU.mult))
                if n >= 4:
                    e.wait_ge(s["valued"], n - 3)
                e.tensor_tensor(co.p[0:NC, n % 4, :], masked, r, ALU.mult).then_inc(s["probs"], 1)
            elif kind == "finish":
                g = step[1]
                e.wait_ge(s["valued"], self.upto[("value", g)])
                if self.value_scale and g == 0:
                    e.wait_ge(s["ka_moved"], 32)
                if g >= 1:
                    e.wait_ge(s["finished"], g)
                bank = ps[:, VALUE_BANK + g % 2, :]
                if self.relu:
                    link(e.tensor_scalar(co.recip[:, :], bank[64:128, :], 1e-32, None, ALU.add))
                    link(e.reciprocal(co.recip[:, :], co.recip[:, :]))
                else:
                    link(e.reciprocal(co.recip[:, :], bank[64:128, :]))
                out = co.o[64 * (g % 2):64 * (g % 2) + 64, (g // 2) * N:(g // 2) * N + N]
                if self.value_scale:
                    ins = e.scalar_tensor_tensor(out=out, in0=bank[0:64, :], scalar=co.scale_o[:, g:g + 1],
                                                 in1=co.recip[:, :], op0=ALU.mult, op1=ALU.mult)
                else:
                    ins = e.tensor_tensor(out, bank[0:64, :], co.recip[:, :], ALU.mult)
                ins.then_inc(s["finished"], 1)

    def attend_scalar(self, e):
        co, s, w = self.sub.core, self.sub.s, self.sub.w
        for step in self.steps:
            if step[0] != "expo":
                continue
            _, pos, t, n = step
            _, m, _ = self.expo_queries(t)
            keys = NC if t == "ctx" else 128
            e.wait_ge(s["expo"], n + 1)
            bank = co.ps[0:keys, EXPO_BANK + n % 2, 0:m]
            if self.relu:
                if n >= 2:
                    e.wait_ge(s["probs"], n - 1)
                e.activation(co.tmp[0:keys, n % 2, :], bank, ACT.Relu, scale=self.scale,
                             bias=w("sn_bias")[0:keys, 0:1]).then_inc(s["relu"], 1)
            else:
                if n >= 4:
                    e.wait_ge(s["valued"], n - 3)
                e.activation(co.p[0:keys, n % 4, 0:m], bank, ACT.Exp, scale=self.scale).then_inc(s["probs"], 1)


    def output_tensor(self, e):
        co, s, w = self.sub.core, self.sub.s, self.sub.w
        groups = self.heads // self.per_group
        e.wait_ge(s["finished"], groups)
        biased = "bo" in self.sub.at
        for i in range(NT):
            out = co.ps[:, OUT_BANK, i * 128:i * 128 + 128]
            for c in range(groups // 2):
                last = e.matmul(out, co.o[:, c * N + i * 128:c * N + i * 128 + 128],
                                w("wo")[:, c * 128:c * 128 + 128], start=c == 0,
                                stop=c == groups // 2 - 1 and not biased, skip_group_check=True)
            if biased:
                last = e.matmul(out, co.c("ones")[:, 0:128], w("bo"), start=False, stop=True,
                                skip_group_check=True)
        last.then_inc(s["out"], 1)

    def output_vector(self, e, link, into):
        co, s = self.sub.core, self.sub.s
        e.wait_ge(s["out"], 1)
        flat = into[:, :, :].rearrange("p i d -> p (i d)")
        link(e.tensor_tensor(flat, flat, co.ps[:, OUT_BANK, :], ALU.add))


def attention_sublayer(core, load_next, clear, key, number, norm, keep_h=False, add_h=False, **kinds):
    sub = Sublayer(core, key, number)
    s, w = sub.s, sub.w
    at = Attention(sub, **kinds)
    nm = Norm(sub, gain=w("g") if "g" in sub.at else None, offset=w("b") if "b" in sub.at else None,
              keep=core.h if keep_h else None, source=core.h if add_h else None, **norm)
    into = core.h if keep_h or add_h else core.x
    own_ctx = kinds.get("ctx") and "g_ctx" in sub.at

    with core.nc.Block() as block:

        @block.sync
        def _(sp):
            load_next(sp)
            if at.value_scale:
                ka_sync(sub, sp)

        @block.gpsimd
        def _(pool):
            clear(pool)
            at.fill(pool)

        @block.vector
        def _(dve):
            link = chained(dve, s["step_v"])
            dve.wait_ge(core.loaded[key], 16)
            nm.vector(dve, link)
            if own_ctx:
                dve.tensor_scalar(core.ctx_t[:, 0:NC], core.ctx_norm_t[:, 0:NC], w("g_ctx"), w("b_ctx"),
                                  ALU.mult, ALU.add).then_inc(s["ctx_ready"], 1)
            if at.relu:
                keep_vector(sub, dve)
            if at.value_scale:
                ka_vector(sub, dve, link)
            at.project_vector(dve, link)
            at.attend_vector(dve, link)
            at.output_vector(dve, link, into)
            if add_h:
                flat = lambda a: a[:, :, :].rearrange("p i d -> p (i d)")
                dve.tensor_tensor(flat(core.x), flat(core.x), flat(core.h), ALU.add).then_inc(s["added"], 1)

        @block.scalar
        def _(act):
            act.wait_ge(core.loaded[key], 16)
            nm.scalar(act)
            if at.relu:
                keep_scalar(sub, act)
            if at.value_scale:
                ka_scalar(sub, act)
            at.project_scalar(act)
            at.attend_scalar(act)

        @block.tensor
        def _(pe):
            pe.wait_ge(core.loaded[key], 16)
            nm.tensor(pe)
            if at.relu:
                keep_tensor(sub, pe)
            if at.value_scale:
                ka_tensor(sub, pe)
            at.project_tensor(pe)
            at.attend_tensor(pe)
            at.output_tensor(pe)



def keep_vector(sub, e):
    co, s = sub.core, sub.s
    e.wait_ge(co.x_loaded, 64)
    e.tensor_scalar(co.keep_rows[:, :], co.mask_rows[:, :], -1.0, 1.0, ALU.mult, ALU.add)\
        .then_inc(s["keep_loaded"], 1)


def keep_tensor(sub, e):
    co, s = sub.core, sub.s
    e.wait_ge(s["keep_loaded"], 1)
    for i in range(NT):
        last = e.transpose(co.ps[0:NC, OUT_BANK, i * 128:i * 128 + 128], co.keep_rows[:, i * NC:i * NC + NC],
                           co.c("identity"))
    last.then_inc(s["keep_turned"], 1)


def keep_scalar(sub, e):
    co, s = sub.core, sub.s
    e.wait_ge(s["keep_turned"], 1)
    e.activation(co.spare[0:NC, 0:N], co.ps[0:NC, OUT_BANK, :], ACT.Copy).then_inc(s["keep_ready"], 1)



KA_QK, KA_AX, KA_PHI, KA_PSI, KA_TURNED, KA_PHI2, KA_PSI2, KA_OUT = 16, 32, 96, 160, 240, 304, 320, 336
KA_STATS, KA_VAR = 400, 440


def ka_tensor(sub, e):
    co, s, w = sub.core, sub.s, sub.w
    ps, ka = co.ps[:, OUT_BANK, :], co.ka
    e.wait_ge(s["ka_vector"], 1)
    for h in range(HEADS):
        last = e.matmul(ps[0:16, h:h + 1], w("wqk_mean")[:, 16 * h:16 * h + 16], ka[:, 1:2], start=True,
                        stop=True, skip_group_check=True)
    last.then_inc(s["ka_tensor"], 1)
    e.wait_ge(s["ka_scalar"], 1)
    for t in range(4):
        e.matmul(ps[0:16, KA_AX + 16 * t:KA_AX + 16 * t + 16], w("ka_a")[:, 16 * t:16 * t + 16],
                 ka[0:16, KA_QK:KA_QK + 16], start=True, stop=True, skip_group_check=True)
        last = e.matmul(ps[0:8, KA_PHI + 16 * t:KA_PHI + 16 * t + 16], w("ka_phi1")[:, 8 * t:8 * t + 8],
                        ka[0:16, KA_QK:KA_QK + 16], start=True, stop=True, skip_group_check=True)
    last.then_inc(s["ka_tensor"], 1)
    e.wait_ge(s["ka_vector"], 2)
    e.wait_ge(s["ka_scalar"], 2)
    for t in range(4):
        e.matmul(ps[0:16, KA_PSI + 16 * t:KA_PSI + 16 * t + 16], ka[0:16, KA_AX + 16 * t:KA_AX + 16 * t + 16],
                 w("ka_psi1")[:, 16 * t:16 * t + 16], start=True, stop=True, skip_group_check=True)
        last = e.matmul(ps[0:16, KA_PHI2 + 2 * t:KA_PHI2 + 2 * t + 2], ka[0:8, KA_PHI + 16 * t:KA_PHI + 16 * t + 16],
                        w("ka_phi2")[:, 2 * t:2 * t + 2], start=True, stop=True, skip_group_check=True)
    last.then_inc(s["ka_tensor"], 1)
    e.wait_ge(s["ka_scalar"], 4)
    for t in range(4):
        last = e.transpose(ps[0:16, KA_TURNED + 16 * t:KA_TURNED + 16 * t + 16],
                           ka[0:16, KA_PSI + 16 * t:KA_PSI + 16 * t + 16], co.c("identity")[0:16, 0:16])
    last.then_inc(s["ka_tensor"], 1)
    e.wait_ge(s["ka_vector"], 5)
    for t in range(4):
        last = e.matmul(ps[0:16, KA_PSI2 + 2 * t:KA_PSI2 + 2 * t + 2],
                        ka[0:16, KA_TURNED + 16 * t:KA_TURNED + 16 * t + 16], w("ka_psi2")[:, 2 * t:2 * t + 2],
                        start=True, stop=True, skip_group_check=True)
    last.then_inc(s["ka_tensor"], 1)


def ka_vector(sub, e, link):
    co, s, w = sub.core, sub.s, sub.w
    ps, ka = co.ps[:, OUT_BANK, :], co.ka
    e.wait_ge(s["features"], 1)
    link(e.tensor_reduce(ka[:, 0:1], co.xt[:, :], AX.X, ALU.add))
    e.tensor_scalar(ka[:, 1:2], ka[:, 0:1], 1.0 / N, None, ALU.mult).then_inc(s["ka_vector"], 1)
    e.wait_ge(s["ka_tensor"], 2)
    e.tensor_copy(ka[0:16, KA_AX:KA_AX + 64], ps[0:16, KA_AX:KA_AX + 64]).then_inc(s["ka_vector"], 1)
    e.wait_ge(s["ka_tensor"], 3)
    psi = ka[0:16, KA_PSI:KA_PSI + 64]
    link(e.tensor_tensor(psi, ps[0:16, KA_PSI:KA_PSI + 64], w("ka_bpsi1"), ALU.add))
    link(e.tensor_tensor(ka[0:16, KA_PHI2:KA_PHI2 + 8], ps[0:16, KA_PHI2:KA_PHI2 + 8], w("ka_bphi2"), ALU.add))
    stats, mv = ka[0:16, KA_STATS:KA_STATS + 24], ka[0:16, KA_STATS + 24:KA_STATS + 32]
    for t in range(4):
        last = e.bn_stats(stats[:, 6 * t:6 * t + 6], psi[:, 16 * t:16 * t + 16])
    link(last)
    for t in range(4):
        last = e.bn_aggr(mv[:, 2 * t:2 * t + 2], stats[:, 6 * t:6 * t + 6])
    link(last)
    var, root = ka[0:16, KA_VAR:KA_VAR + 4], ka[0:16, KA_VAR + 4:KA_VAR + 8]
    e.tensor_scalar(var, mv[:, 1:8:2], LN_EPS, None, ALU.add).then_inc(s["ka_vector"], 1)
    e.wait_ge(s["ka_scalar"], 3)
    link(e.reciprocal(root, root))
    for t in range(4):
        last = e.tensor_scalar(psi[:, 16 * t:16 * t + 16], psi[:, 16 * t:16 * t + 16], mv[:, 2 * t:2 * t + 1],
                               root[:, t:t + 1], ALU.subtract, ALU.mult)
    link(last)
    link(e.tensor_tensor(psi, psi, w("ka_g"), ALU.mult))
    e.tensor_tensor(psi, psi, w("ka_b"), ALU.add).then_inc(s["ka_vector"], 1)
    e.wait_ge(s["ka_tensor"], 4)
    e.tensor_copy(ka[0:16, KA_TURNED:KA_TURNED + 64], ps[0:16, KA_TURNED:KA_TURNED + 64])\
        .then_inc(s["ka_vector"], 1)
    e.wait_ge(s["ka_tensor"], 5)
    psi2, out = ka[0:16, KA_PSI2:KA_PSI2 + 8], ka[0:16, KA_OUT:KA_OUT + 8]
    link(e.tensor_tensor(psi2, ps[0:16, KA_PSI2:KA_PSI2 + 8], w("ka_bpsi2"), ALU.add))
    link(e.tensor_tensor(out, ka[0:16, KA_PHI2:KA_PHI2 + 8], psi2, ALU.mult))
    link(e.tensor_scalar(out, out, w("ka_temp"), None, ALU.mult))
    link(e.tensor_tensor(out, out, w("ka_mix"), ALU.mult))
    e.tensor_scalar(out, out, 1.0, w("gamma"), ALU.add, ALU.mult).then_inc(s["ka_vector"], 1)


def ka_scalar(sub, e):
    co, s, w = sub.core, sub.s, sub.w
    ps, ka = co.ps[:, OUT_BANK, :], co.ka
    e.wait_ge(s["ka_tensor"], 1)
    e.activation(ka[0:16, KA_QK:KA_QK + 16], ps[0:16, 0:16], ACT.Copy).then_inc(s["ka_scalar"], 1)
    e.wait_ge(s["ka_vector"], 2)
    for t in range(4):
        last = e.activation(ka[0:8, KA_PHI + 16 * t:KA_PHI + 16 * t + 16],
                            ps[0:8, KA_PHI + 16 * t:KA_PHI + 16 * t + 16], ACT.Silu,
                            bias=w("ka_bphi1")[:, t:t + 1], scale=1.0)
    last.then_inc(s["ka_scalar"], 1)
    e.wait_ge(s["ka_vector"], 3)
    e.activation(ka[0:16, KA_VAR + 4:KA_VAR + 8], ka[0:16, KA_VAR:KA_VAR + 4], ACT.Sqrt)\
        .then_inc(s["ka_scalar"], 1)
    e.wait_ge(s["ka_vector"], 4)
    e.activation(ka[0:16, KA_PSI:KA_PSI + 64], ka[0:16, KA_PSI:KA_PSI + 64], ACT.Gelu)\
        .then_inc(s["ka_scalar"], 1)


def ka_sync(sub, e):
    co, s = sub.core, sub.s
    e.wait_ge(s["ka_vector"], 6)
    e.dma_start(co.scratch, co.ka[0:16, KA_OUT:KA_OUT + 8]).then_inc(s["ka_moved"], 16)
    e.wait_ge(s["ka_moved"], 16)
    with co.nc.allow_non_contiguous_dma("128 words"):
        e.dma_start(co.scale_o[:, :], co.scratch.rearrange("(g h) d -> (h d) g", g=2)).then_inc(s["ka_moved"], 16)
    e.wait_ge(s["ka_moved"], 32)



def context_stage(core, load_next, number, x_in, ctx_in, mask_in, vec_in, b):
    s = core.sets[number % 2]
    sm = core.small

    with core.nc.Block() as block:

        @block.sync
        def _(sp):
            one = lambda a: a[bass.ds(b, 1)].rearrange("o p c -> (o p) c")
            sp.dma_start(core.ctx_rows[0:NC, :], one(ctx_in)).then_inc(core.x_loaded, 16)
            sp.dma_start(core.x[:, :, :].rearrange("p i d -> p (i d)"), one(x_in)).then_inc(core.x_loaded, 16)
            sp.dma_start(core.mask_rows[:, :].bitcast(I32), one(mask_in)).then_inc(core.x_loaded, 16)
            sp.dma_start(core.mask_vec[:, 0:NC], one(vec_in)).then_inc(core.x_loaded, 16)
            load_next(sp)

        @block.vector
        def _(dve):
            link = chained(dve, s["step_v"])
            dve.wait_ge(core.x_loaded, 64)
            rows, stats, mv = core.ctx_rows[0:NC, :], core.stats[0:NC, 0, :], core.mv[0:NC, 0, :]
            link(dve.bn_stats(stats, rows))
            link(dve.bn_aggr(mv, stats))
            dve.tensor_scalar(sm[0:NC, 0, 0:1], mv[:, 1:2], LN_EPS, None, ALU.add).then_inc(s["variance"], 1)
            dve.wait_ge(s["deviation"], 1)
            link(dve.reciprocal(sm[0:NC, 2, 0:1], sm[0:NC, 1, 0:1]))
            dve.tensor_scalar(core.ctx_n[0:NC, :], rows, mv[:, 0:1], sm[0:NC, 2, 0:1], ALU.subtract, ALU.mult)\
                .then_inc(s["normed"], 1)

        @block.scalar
        def _(act):
            act.wait_ge(s["variance"], 1)
            act.activation(sm[0:NC, 1, 0:1], sm[0:NC, 0, 0:1], ACT.Sqrt).then_inc(s["deviation"], 1)
            act.wait_ge(s["turned"], 1)
            act.activation(core.ctx_raw_t[:, 0:NC], core.ps[:, TURN_BANK, 0:NC], ACT.Copy)
            act.activation(core.ctx_norm_t[:, 0:NC], core.ps[:, TURN_BANK, 128:128 + NC], ACT.Copy)

        @block.tensor
        def _(pe):
            pe.wait_ge(core.x_loaded, 64)
            pe.wait_ge(s["normed"], 1)
            eye = core.c("identity")[0:NC, 0:NC]
            pe.transpose(core.ps[:, TURN_BANK, 0:NC], core.ctx_rows[0:NC, :], eye)
            pe.transpose(core.ps[:, TURN_BANK, 128:128 + NC], core.ctx_n[0:NC, :], eye).then_inc(s["turned"], 1)


class Experts:

    def __init__(self, sub, kind, experts, hidden, up, gate, down, b1=None, b2=None, routed=0, top=None):
        self.sub, self.kind, self.experts, self.up, self.gate, self.down = sub, kind, experts, up, gate, down
        self.chunks = [min(128, hidden - at) for at in range(0, hidden, 128)]
        self.hidden, self.b1, self.b2, self.routed, self.top = hidden, b1, b2, routed, top
        co = sub.core
        self.row = 24
        area = co.ka[:, 0:NT * 24 * 4].rearrange("p (a i c) -> p a i c", a=4, i=NT)
        self.exps, self.replaced, self.gates, self.misc = area[:, 0], area[:, 1], area[:, 2], area[:, 3]

    def route_tensor(self, e):
        co, s, w = self.sub.core, self.sub.s, self.sub.w
        for i in range(NT):
            out = co.ps[:, OUT_BANK, 32 * i:32 * i + self.routed]
            biased = "router_b" in self.sub.at
            last = e.matmul(out, co.xt[:, i * 128:i * 128 + 128], w("router"), start=True, stop=not biased,
                            skip_group_check=True)
            if biased:
                last = e.matmul(out, co.c("ones")[:, 0:128], w("router_b"), start=False, stop=True,
                                skip_group_check=True)
        last.then_inc(s["logits"], 1)

    def turn_gates_tensor(self, e):
        co, s = self.sub.core, self.sub.s
        e.wait_ge(s["gates"], 1)
        for i in range(NT):
            last = e.transpose(co.ps[0:self.experts, TURN_BANK, i * 128:i * 128 + 128],
                               self.gates[:, i, 0:self.experts], co.c("identity"))
        last.then_inc(s["gates_turned"], 1)

    def route_vector(self, e, link):
        co, s = self.sub.core, self.sub.s
        r, k = self.routed, self.top
        low, total, tops = self.misc[:, :, 0:1], self.misc[:, :, 1:2], self.misc[:, :, 8:16]
        e.memset(self.exps[:, :, r:self.row], -1.0)
        link(e.memset(self.misc[:, :, 0:self.row], -1.0))
        e.wait_ge(s["logits"], 1)
        logits = co.ps[:, OUT_BANK, 0:NT * 32].rearrange("p (i c) -> p i c", i=NT)[:, :, 0:r]
        e.tensor_reduce(low[:, :, 0], logits, AX.X, ALU.max, negate=True).then_inc(s["shifted"], 1)
        e.wait_ge(s["exps"], 1)
        for i in range(NT):
            last = e.max(tops[:, i, :], self.exps[:, i, 0:r])
        link(last)
        link(e.memset(tops[:, :, k:8], -1.0))
        link(e.reciprocal(total[:, :, 0], total[:, :, 0]))
        for i in range(NT):
            last = e.match_replace(self.replaced[:, i, 0:r + 8 - k], tops[:, i, :],
                                   self.exps[:, i, 0:r + 8 - k], -2.0)
        link(last)
        for i in range(NT):
            last = e.scalar_tensor_tensor(out=self.gates[:, i, 0:r], in0=self.replaced[:, i, 0:r], scalar=-1.5,
                                          in1=self.exps[:, i, 0:r], op0=ALU.is_lt, op1=ALU.mult)
        link(last)
        if self.experts > r:
            e.memset(self.gates[:, :, r:self.experts], 1.0)
        for i in range(NT):
            last = e.tensor_scalar(self.gates[:, i, 0:r], self.gates[:, i, 0:r], total[:, i, :], None, ALU.mult)
        last.then_inc(s["gates"], 1)

    def route_scalar(self, e):
        co, s = self.sub.core, self.sub.s
        e.wait_ge(s["shifted"], 1)
        for i in range(NT):
            last = e.activation(self.exps[:, i, 0:self.routed], co.ps[:, OUT_BANK, 32 * i:32 * i + self.routed],
                                ACT.Exp, bias=self.misc[:, i, 0:1], scale=1.0, accum_out=self.misc[:, i, 1:2])
        last.then_inc(s["exps"], 1)

    def pairs(self):
        return [(x, c) for x in range(self.experts) for c in range(len(self.chunks))]

    def hidden_tile(self, x, c):
        at = ((x % 2) * len(self.chunks) + c) * N
        return self.sub.core.o[0:self.chunks[c], at:at + N]

    def tensor(self, e):
        co, s, w = self.sub.core, self.sub.s, self.sub.w
        n = len(self.chunks)
        e.wait_ge(s["features"], 1)
        if self.top is not None:
            self.route_tensor(e)

        def up(x):
            for c, m in enumerate(self.chunks):
                job = x * n + c
                if job >= 2:
                    e.wait_ge(s["hidden"], job - 1)
                cols = slice(x * self.hidden + 128 * c, x * self.hidden + 128 * c + m)
                for b, weights in enumerate((self.up, self.gate) if self.gate is not None else (self.up,)):
                    last = e.matmul(co.ps[0:m, 2 * (job % 2) + b, :], weights[:, cols], co.xt[:, :],
                                    start=True, stop=True)
                last.then_inc(s["up"], 1)

        up(0)
        if self.b2 is not None:
            self.turn_gates_tensor(e)
            e.wait_ge(s["gates_kept"], 1)
            for i in range(NT):
                last = e.matmul(co.ps[:, OUT_BANK, i * 128:i * 128 + 128],
                                co.tmp[0:self.experts, 0, i * 128:i * 128 + 128], self.b2, start=True,
                                stop=True, skip_group_check=True)
            last.then_inc(s["out"], 1)
        for x in range(self.experts):
            if x + 1 < self.experts:
                up(x + 1)
            e.wait_ge(s["hidden"], (x + 1) * n)
            if x >= 2:
                e.wait_ge(s["summed"], (x - 1) * NT)
            for i in range(NT):
                for c in range(n):
                    last = e.matmul(co.ps[:, 4 + x % 2, i * 128:i * 128 + 128],
                                    self.hidden_tile(x, c)[:, i * 128:i * 128 + 128],
                                    self.down[0:self.chunks[c], (x * n + c) * 128:(x * n + c) * 128 + 128],
                                    start=c == 0, stop=c == n - 1, skip_group_check=True)
            last.then_inc(s["down"], 1)

    def scalar(self, e):
        co, s = self.sub.core, self.sub.s
        if self.top is not None:
            self.route_scalar(e)
        for job, (x, c) in enumerate(self.pairs()):
            m = self.chunks[c]
            e.wait_ge(s["up"], job + 1)
            if self.kind == "relu":
                if x >= 2:
                    e.wait_ge(s["down"], x - 1)
                e.activation(self.hidden_tile(x, c), co.ps[0:m, 2 * (job % 2), :], ACT.Relu,
                             bias=self.b1[:, x:x + 1], scale=1.0).then_inc(s["hidden"], 1)
                if x == 0 and self.b2 is not None:
                    e.wait_ge(s["gates_turned"], 1)
                    e.activation(co.tmp[0:self.experts, 0, :], co.ps[0:self.experts, TURN_BANK, :], ACT.Copy)\
                        .then_inc(s["gates_kept"], 1)
            else:
                if job >= 2:
                    e.wait_ge(s["hidden"], job - 1)
                e.activation(co.tmp[0:m, job % 2, :], co.ps[0:m, 2 * (job % 2) + 1, :], ACT.Silu)\
                    .then_inc(s["relu"], 1)

    def vector(self, e, link):
        co, s = self.sub.core, self.sub.s
        if self.top is not None:
            self.route_vector(e, link)
        if self.b2 is not None:
            e.wait_ge(s["out"], 1)
            flat = co.x[:, :, :].rearrange("p i d -> p (i d)")
            link(e.tensor_tensor(flat, flat, co.ps[:, OUT_BANK, :], ALU.add))
        n = len(self.chunks)

        def hidden(x):
            for c, m in enumerate(self.chunks):
                job = x * n + c
                e.wait_ge(s["relu"], job + 1)
                if x >= 2:
                    e.wait_ge(s["down"], x - 1)
                e.tensor_tensor(self.hidden_tile(x, c), co.tmp[0:m, job % 2, :],
                                co.ps[0:m, 2 * (job % 2), :], ALU.mult).then_inc(s["hidden"], 1)

        if self.kind == "silu":
            hidden(0)
        for x in range(self.experts):
            if self.kind == "silu" and x + 1 < self.experts:
                hidden(x + 1)
            e.wait_ge(s["down"], x + 1)
            if x >= 1:
                e.wait_ge(s["summed"], x * NT)
            for i in range(NT):
                out = co.ps[:, 4 + x % 2, i * 128:i * 128 + 128]
                if self.top is None:
                    ins = e.tensor_tensor(co.x[:, i, :], co.x[:, i, :], out, ALU.add)
                else:
                    ins = e.scalar_tensor_tensor(out=co.x[:, i, :], in0=out, scalar=self.gates[:, i, x:x + 1],
                                                 in1=co.x[:, i, :], op0=ALU.mult, op1=ALU.add)
                ins.then_inc(s["summed"], 1)
        e.wait_ge(s["summed"], self.experts * NT)


def experts_sublayer(core, load_next, clear, key, number):
    sub = Sublayer(core, key, number)
    s, w = sub.s, sub.w
    nm = Norm(sub)
    if key == "L0_ffn":
        ex = Experts(sub, "relu", 16, 128, w("w1"), None, w("w2"), b1=w("b1"), b2=w("b2"), routed=15, top=3)
    elif key == "L3_ffn":
        gate = core.gate_up[:, 0:8 * 352]
        up = core.gate_up[:, 8 * 352:16 * 352]
        ex = Experts(sub, "silu", 8, 352, up, gate, w("down"), routed=8, top=2)
    else:
        at = sub.at
        real = lambda n: core.q[:, at[n][0]:at[n][0] + at[n][1]]
        ex = Experts(sub, "silu", 1, 384, real("up"), real("gate"), real("down"))
    whole = key == "L3_ffn"

    with core.nc.Block() as block:

        @block.sync
        def _(sp):
            load_next(sp)

        @block.gpsimd
        def _(pool):
            clear(pool)

        @block.vector
        def _(dve):
            link = chained(dve, s["step_v"])
            dve.wait_ge(core.loaded[key], 16)
            if key == "L1_ffn":
                n = sum(wide for _, wide, _ in sub.at.values())
                dve.tensor_scalar(core.q[:, 0:n], sub.slot[:, 0:n].bitcast(I32), 1.0 / 127.0, None, ALU.mult)\
                    .then_inc(s["converted"], 1)
            nm.vector(dve, link)
            ex.vector(dve, link)

        @block.scalar
        def _(act):
            act.wait_ge(core.loaded[key], 16)
            nm.scalar(act)
            ex.scalar(act)

        @block.tensor
        def _(pe):
            pe.wait_ge(core.loaded[key], 16)
            if whole:
                pe.wait_ge(core.loaded["L3_ffn_gate_up"], 16)
            nm.tensor(pe)
            if key == "L1_ffn":
                pe.wait_ge(s["converted"], 1)
            ex.tensor(pe)


def fourier_sublayer(core, load_next, clear, key, number):
    sub = Sublayer(core, key, number)
    s, w = sub.s, sub.w
    nm = Norm(sub)
    at_real, at_imag, mat = core.tmp[:, 0, 0:128], core.tmp[:, 0, 128:256], core.tmp[:, 0, 256:384]

    with core.nc.Block() as block:

        @block.sync
        def _(sp):
            load_next(sp)

        @block.gpsimd
        def _(pool):
            clear(pool)

        @block.vector
        def _(dve):
            link = chained(dve, s["step_v"])
            nm.vector(dve, link)
            dve.wait_ge(s["up"], 1)
            dve.tensor_copy(core.tmp[:, 0, 0:256], core.ps[:, 0, 0:256]).then_inc(s["hidden"], 1)
            dve.wait_ge(s["up"], 2)
            dve.tensor_scalar(mat, core.ps[:, 1, 0:128], 1.0 / 128, None, ALU.mult).then_inc(s["hidden"], 1)
            dve.wait_ge(s["out"], 1)
            flat = core.x[:, :, :].rearrange("p i d -> p (i d)")
            link(dve.tensor_tensor(flat, flat, core.ps[:, OUT_BANK, :], ALU.add))

        @block.scalar
        def _(act):
            nm.scalar(act)

        @block.tensor
        def _(pe):
            pe.wait_ge(core.loaded[key], 16)
            group = dict(skip_group_check=True)
            pe.matmul(core.ps[:, 0, 0:128], w("real"), core.c("dft_cos"), start=True, stop=False, **group)
            pe.matmul(core.ps[:, 0, 0:128], w("imag"), core.c("dft_sin"), start=False, stop=True, **group)
            pe.matmul(core.ps[:, 0, 128:256], w("imag"), core.c("dft_cos"), start=True, stop=False, **group)
            pe.matmul(core.ps[:, 0, 128:256], w("real"), core.c("dft_minus_sin"), start=False, stop=True,
                      **group).then_inc(s["up"], 1)
            nm.tensor(pe)
            pe.wait_ge(s["hidden"], 1)
            pe.matmul(core.ps[:, 1, 0:128], at_real, core.c("dft_cos"), start=True, stop=False, **group)
            pe.matmul(core.ps[:, 1, 0:128], at_imag, core.c("dft_minus_sin"), start=False, stop=True, **group)\
                .then_inc(s["up"], 1)
            pe.wait_ge(s["hidden"], 2)
            pe.wait_ge(s["features"], 1)
            for i in range(NT):
                out = core.ps[:, OUT_BANK, i * 128:i * 128 + 128]
                pe.matmul(out, core.xt[:, i * 128:i * 128 + 128], mat, start=True, stop=False, **group)
                last = pe.matmul(out, core.c("ones")[:, 0:128], w("bo"), start=False, stop=True, **group)
            last.then_inc(s["out"], 1)



SUBLAYERS = [
    ("L0_attn", 0, dict(wide=False, pattern="causal", scale=8 ** -0.5, alibi=True, norm={})),
    ("L0_xattn", 1, dict(wide=False, own=False, ctx=True, scale=8 ** -0.5, relu=True, norm={})),
    ("L0_ffn", 2, None),
    ("L1_attn", 3, dict(wide=False, alpha=True, value_scale=True, norm={})),
    ("L1_xattn", 4, dict(wide=True, ctx=True, scale=1 / 8, norm=dict(again=LN_EPS))),
    ("L1_ffn", 5, None),
    ("L2_attn_g", 6, dict(wide=False, pattern="causal", scale=8 ** -0.5, grouped=True, rope=True, latent=True,
                          norm=dict(again=RMS_EPS), keep_h=True)),
    ("L2_attn_l", 6, dict(wide=False, pattern="local", scale=8 ** -0.5, grouped=True, rope=True,
                          norm=dict(kind="rms"), add_h=True)),
    ("L2_xattn", 7, dict(wide=True, heads=8, ctx=True, scale=1 / 8, ctx_rope=True, norm=dict(again=LN_EPS))),
    ("L2_ffn", 8, None),
    ("L3_attn", 9, dict(wide=True, pattern="causal", scale=1 / 8, norm=dict(again=LN_EPS))),
    ("L3_xattn", 10, dict(wide=False, own=False, ctx=True, scale=8 ** -0.5, ctx_mask=True, norm={})),
    ("L3_ffn", 11, None),
]


def build(nc, dram, layouts, out, scratch):
    with ExitStack() as ctx:
        core = Core(nc, ctx, dram, layouts)
        core.scratch = scratch
        todo = [x for x in SUBLAYERS if STAGES[0] <= x[1] <= STAGES[1]]

        with nc.Block() as block:

            @block.sync
            def _(sp):
                sp.dma_start(core.consts[:, :], dram["consts"]).then_inc(core.consts_loaded, 16)
                sp.dma_start(core.o[:, 0:masks().width], dram["masks"]).then_inc(core.consts_loaded, 16)

            @block.gpsimd
            def _(pool):
                pool.memset(core.guard_thin[:, :, :, :], 0.0)
                pool.memset(core.guard_wide[:, :, :, :], 0.0)
                pool.memset(core.ctx_raw_t[:, 64:128], 0.0)
                pool.memset(core.mask_vec[:, 64:128], 0.0)

            @block.vector
            def _(dve):
                dve.wait_ge(core.consts_loaded, 32)
                dve.tensor_copy(core.identity_b[:, :], core.c("identity"))
                for name, mask in core.masks_b.items():
                    at, wide, _ = core.mask_at[name]
                    dve.tensor_copy(mask[:, :], core.o[:, at:at + wide])

        def loader(n):
            def load(sp):
                if n >= len(todo):
                    return
                key = todo[n][0]
                wide = sum(cols for _, cols, _ in layouts[key].values())
                slot = core.slot[(n + 1) % 2][:, 0:wide]
                sp.dma_start(slot.bitcast(I32) if key == "L1_ffn" else slot, dram[key])\
                    .then_inc(core.loaded[key], 16)
                if key == "L3_ffn":
                    sp.dma_start(core.gate_up[:, :], dram["L3_ffn_gate_up"])\
                        .then_inc(core.loaded["L3_ffn_gate_up"], 16)
            return load

        def clearer(number):
            def clear(pool):
                nums = [x.num for x in core.sets[(number + 1) % 2].values()]
                assert nums == list(range(nums[0], nums[-1] + 1))
                pool.sem_clear(range(nums[0], nums[-1] + 1))
            return clear

        with nc.Fori(0, BATCHES) as b:
            context_stage(core, loader(0), 0, dram["x"], dram["ctx"], dram["mask"], dram["mask_vec"], b)
            room = ExitStack()
            for n, (key, _, kinds) in enumerate(todo):
                number = n + 1
                args = (core, loader(n + 1), clearer(number), key, number)
                if n == 0 or key != "L3_ffn":
                    room.close()
                    room.enter_context(core.operands(bool(kinds and not kinds["wide"]) or key == "L3_ffn", number))
                if kinds is not None:
                    attention_sublayer(*args, **kinds)
                elif key == "L2_ffn":
                    fourier_sublayer(*args)
                else:
                    experts_sublayer(*args)
            room.close()
            with nc.Block() as block:

                @block.sync
                def _(sp):
                    sp.dma_start(out[bass.ds(b, 1)].rearrange("o p c -> (o p) c"),
                                 core.x[:, :, :].rearrange("p i d -> p (i d)")).then_inc(core.x_loaded, 16)
                    sp.wait_ge(core.x_loaded, 80)
            nums = sorted(x.num for x in core.loop_sems)
            assert nums == list(range(nums[0], nums[-1] + 1))
            nc.gpsimd.sem_clear(range(nums[0], nums[-1] + 1))
            nc.all_engine_barrier()


def kernel(**inputs):
    import concourse.bacc as _bacc
    from concourse.bass_utils import run_bass_kernel_spmd as _run

    nc = _bacc.Bacc("TRN2", target_bir_lowering=False, num_devices=1)
    tiles = lambda a: np.ascontiguousarray(a.reshape(B, NT, 128, -1).transpose(0, 2, 1, 3).reshape(B, 128, -1))
    x = np.asarray(inputs["x"] if X_OVERRIDE is None else X_OVERRIDE)
    arrays = {
        "x": tiles(x),
        "ctx": np.ascontiguousarray(inputs["ctx_1024"]),
        "mask": tiles(np.asarray(inputs["mask_BxSxS2_bk1"]).view(np.uint8)).view(np.int32),
        "mask_vec": np.ascontiguousarray(np.asarray(inputs["mask_Bx1x1xS2_fk0"]).reshape(B, 1, NC)),
        "consts": constants().array(),
        "masks": masks().array(),
    }
    layouts = {}
    for key, pack in packs(inputs).items():
        arrays[key] = pack.array()
        layouts[key] = pack.at
    dram = {k: nc.dram_tensor(f"in_{k}", a.shape, mybir.dt.from_np(a.dtype), kind="ExternalInput").ap()
            for k, a in arrays.items()}
    out = nc.dram_tensor("out_x", (B, 128, NT * D), F32, kind="ExternalOutput").ap()
    scratch = nc.dram_tensor("scratch", (16, 8), F32, kind="Internal").ap()
    build(nc, dram, layouts, out, scratch)
    r = _run(nc, [{f"in_{k}": a for k, a in arrays.items()}], core_ids=[0])
    y = np.asarray(r.results[0]["out_x"])
    return np.ascontiguousarray(y.reshape(B, 128, NT, D).transpose(0, 2, 1, 3).reshape(B, N, D))
```

```python
from contextlib import ExitStack, contextmanager

import numpy as np

import concourse.bass as bass
from concourse import mybir

F32 = mybir.dt.float32
F32R = mybir.dt.float32r
BF16 = mybir.dt.bfloat16
I32 = mybir.dt.int32
U8 = mybir.dt.uint8
ALU = mybir.AluOpType
ACT = mybir.ActivationFunctionType
AX = mybir.AxisListType

B, N, D = 4, 512, 128
NC = 77
NT = N // 128
HEADS = 16
STRIP = 32
BANK = 512
COPIES = 3
MAX_ROW, BY_KEY, BY_QUERY, MASKED = 24, 25, 27, 29
NEG = -1e30
LN_EPS = 1e-5
RMS_EPS = 1e-6

STAGES = (0, 11)
BATCHES = B
X_OVERRIDE = None


PLAIN = [4 * c + s for c in range(4) for s in range(4)]
GROUPED = [4 * s + c for c in range(4) for s in range(4)]


class Pack:

    def __init__(self):
        self.at, self.width, self.parts = {}, 0, []

    def add(self, name, a):
        a = np.asarray(a)
        a = a.reshape(a.shape[0], -1)
        self.at[name] = (self.width, a.shape[1], a.shape[0])
        self.width += a.shape[1]
        self.parts.append(a)

    def array(self):
        out = np.zeros((128, self.width), self.parts[0].dtype)
        for (col, wide, rows), a in zip(self.at.values(), self.parts):
            out[:rows, col:col + wide] = a
        return out


def strips(w, order, extra=None):
    rows = w.shape[0]
    out = np.zeros((rows, len(order), STRIP), w.dtype)
    for n in range(COPIES):
        out[:, :, 8 * n:8 * n + 8] = w.reshape(rows, -1, 8)[:, order, :]
    for feature, v in (extra or {}).items():
        out[:, :, feature] = v[:, order]
    return out.reshape(rows, -1)


def split_columns():
    cols = {}
    for name, low, ones in (("q", (slice(16, 24), BY_KEY + 1, BY_QUERY + 1), (MASKED, MASKED + 1)),
                            ("k", (slice(8, 16), MASKED + 1), (MAX_ROW, BY_QUERY, BY_QUERY + 1))):
        a, b, bias = np.zeros((4, STRIP), np.float32), np.ones((4, STRIP), np.float32), \
            np.zeros((4, STRIP), np.float32)
        for f in low:
            a[:, f], b[:, f] = 1, -1
        for f in ones:
            bias[:, f] = 1
        cols[name] = [v.reshape(128, 1) for v in (a, b, bias)]
    return cols


def strip_column(head_values, order, extra):
    n = len(order)
    out = np.zeros((n, STRIP), np.float32)
    if head_values is not None:
        out[:, 0:8 * COPIES] = np.tile(head_values.reshape(-1, 8)[order], (1, COPIES))
    for row, v in extra.items():
        out[:, row] = v if np.isscalar(v) else np.asarray(v)[order]
    return np.ascontiguousarray(out.reshape(n // 4, 128).T)


def by_head(w, order):
    return w.reshape(w.shape[0], -1, 8)[:, order, :].reshape(w.shape[0], -1)


def swap_pairs(w):
    return w.reshape(w.shape[0], -1, 2)[:, :, ::-1].reshape(w.shape[0], -1)


def chunks_of_rows(w):
    n = w.shape[0] // 128
    return w.reshape(n, 128, -1).transpose(1, 0, 2).reshape(128, -1)


def row(v):
    return np.asarray(v, np.float32).reshape(1, -1)


def col(v):
    return np.asarray(v, np.float32).reshape(-1, 1)


def rope_tables(base):
    inv = (1.0 / np.float32(base) ** (np.arange(0, 8, 2, dtype=np.float32) / np.float32(8))).astype(np.float32)
    f = np.arange(N, dtype=np.float32)[:, None] * inv[None, :]
    cos, sin = np.cos(f), np.sin(f)
    c, s = np.zeros((4, STRIP, N), np.float32), np.zeros((4, STRIP, N), np.float32)
    for d in range(8 * COPIES):
        c[:, d] = cos[:, d % 8 // 2]
        s[:, d] = sin[:, d % 8 // 2] * (-1.0 if d % 2 == 0 else 1.0)
    return c.reshape(128, N), s.reshape(128, N)


def context_rope_tables():
    half = 32
    inv = (1.0 / np.float32(10000.0) ** (np.arange(0, 64, 2, dtype=np.float32) / np.float32(64))).astype(np.float32)
    theta = np.arange(NC, dtype=np.float32)[:, None] * inv[None, :]
    c = np.concatenate([np.cos(theta)] * 2, 1).T
    s = np.concatenate([-np.sin(theta), np.sin(theta)], 1).T
    assert c.shape[0] == 2 * half
    return np.concatenate([c, c], 0), np.concatenate([s, s], 0)


def alibi_slopes():
    start = 2 ** (-2 ** (-(np.log2(HEADS) - 3)))
    return np.array([start * start ** i for i in range(HEADS)], np.float32)


def masks():
    p = Pack()
    i = np.arange(128)
    p.add("causal", np.where(i[None, :] <= i[:, None], 0, NEG).astype(np.float32))
    p.add("causal_t", np.where(i[None, :] >= i[:, None], 0, NEG).astype(np.float32))
    wide = np.arange(128 + STRIP)
    gap = i[:, None] + 32 - wide[None, :]
    p.add("local", np.where((gap >= 0) & (gap < 32), 0, NEG).astype(np.float32))
    gap = wide[None, :] - i[:, None]
    p.add("local_t", np.where((gap >= 0) & (gap < 32), 0, NEG).astype(np.float32))
    return p


def constants():
    p = Pack()
    i = np.arange(128)
    p.add("identity", np.eye(128, dtype=np.float32))
    same = (i[:, None] // STRIP == i[None, :] // STRIP) & (i[:, None] % STRIP < 8) & (i[None, :] % STRIP < 8 * COPIES)
    p.add("strip_mean", np.where(same, 1 / 8, 0).astype(np.float32))
    p.add("rms_eps", np.full((128, 1), RMS_EPS, np.float32))
    p.add("ones", np.ones((1, N), np.float32))
    p.add("ones_and_position", np.stack([np.ones(N), np.arange(N)]).astype(np.float32))
    for name, cols in split_columns().items():
        for part, v in zip(("a", "b", "bias"), cols):
            p.add(f"{name}_{part}", v)
    at = np.arange(128) % STRIP
    scale = np.where(at < 8 * COPIES, np.float32(8 ** -0.5 / 0.72), np.float32(1)).reshape(128, 1)
    for part in (0, 1):
        p.add("alpha_" + "ab"[part], np.repeat(split_columns()["q"][part] * scale, 4, axis=1))
    m = np.zeros((1, 4, STRIP), np.float32)
    m[:, :, MASKED:MASKED + 2] = -1e9 * np.sqrt(8.0)
    p.add("mask_row", m.reshape(1, -1))
    a = 2 * np.pi * ((i[:, None] * i[None, :]) % 128) / 128
    p.add("dft_cos", np.cos(a).astype(np.float32))
    p.add("dft_sin", np.sin(a).astype(np.float32))
    p.add("dft_minus_sin", -np.sin(a).astype(np.float32))
    return p


def packs(w):
    f = {k: np.asarray(v) for k, v in w.items()}
    out = {}

    p = out["L0_attn"] = Pack()
    p.add("wq", strips(f["L0_attn_Wq"], PLAIN))
    p.add("wk", strips(f["L0_attn_Wk"], PLAIN))
    p.add("wv", f["L0_attn_Wv"])
    p.add("wo", f["L0_attn_Wo"])
    slope = alibi_slopes() * np.float32(np.sqrt(8.0))
    none, one = np.zeros(HEADS, np.float32), np.ones(HEADS, np.float32)
    nothing = np.zeros((1, 128), np.float32)
    p.add("q_add", strips(np.concatenate([row(f["L0_attn_bq"]), nothing]), PLAIN,
                          {BY_KEY: np.stack([-slope, none]), BY_KEY + 1: np.stack([-slope, none]),
                           BY_QUERY: np.stack([none, slope]), BY_QUERY + 1: np.stack([none, slope])}))
    p.add("k_add", strips(np.concatenate([row(f["L0_attn_bk"]), nothing]), PLAIN,
                          {BY_KEY: np.stack([none, one]), BY_KEY + 1: np.stack([none, one])}))
    p.add("bv", row(f["L0_attn_bv"]))
    p.add("bo", row(f["L0_attn_bo"]))

    p = out["L0_xattn"] = Pack()
    p.add("wq", strips(f["L0_xattn_Wq"].T, PLAIN))
    p.add("wk", strips(f["L0_xattn_Wk"].T, PLAIN))
    p.add("wv", f["L0_xattn_Wv"].T)
    p.add("wo", f["L0_xattn_Wo"].T)
    p.add("sn_bias", np.broadcast_to(f["L0_xattn_sn_bias"].reshape(1, 1), (128, 1)))

    p = out["L0_ffn"] = Pack()
    p.add("w1", np.concatenate([f["L0_ffn_eW1"], f["L0_ffn_sW1"][None]]).transpose(1, 0, 2))
    p.add("w2", np.concatenate([f["L0_ffn_eW2"], f["L0_ffn_sW2"][None]]).transpose(1, 0, 2))
    p.add("b1", np.concatenate([f["L0_ffn_eb1"], f["L0_ffn_sb1"][None]]).T)
    p.add("b2", np.concatenate([f["L0_ffn_eb2"], f["L0_ffn_sb2"][None]]))
    p.add("router", f["L0_ffn_router_W"])
    p.add("router_b", row(f["L0_ffn_router_b"]))

    p = out["L1_attn"] = Pack()
    wqkv = f["L1_attn_Wqkv"]
    p.add("wq", strips(wqkv[:, 0:128], PLAIN))
    p.add("wk", strips(wqkv[:, 128:256], PLAIN))
    p.add("wv", wqkv[:, 256:384])
    p.add("wo", f["L1_attn_Wproj"])
    p.add("bo", row(f["L1_attn_bproj"]))
    p.add("alpha", strip_column(np.repeat(f["L1_attn_alpha"], 8), PLAIN, {BY_QUERY: 1.0, BY_QUERY + 1: 1.0}))
    beta = row(f["L1_attn_beta"])
    p.add("q_add", strips(nothing, PLAIN, {BY_QUERY: beta, BY_QUERY + 1: beta}))
    p.add("wqk_mean", wqkv[:, 0:256].reshape(128, 2, 16, 8).transpose(0, 2, 1, 3))
    p.add("ka_a", f["L1_attn_A"].transpose(1, 0, 2))
    p.add("ka_phi1", f["L1_attn_Wphi1"].transpose(1, 0, 2))
    p.add("ka_bphi1", f["L1_attn_bphi1"].T)
    p.add("ka_phi2", f["L1_attn_Wphi2"].transpose(1, 0, 2))
    p.add("ka_psi1", f["L1_attn_Wpsi1"].transpose(1, 0, 2))
    p.add("ka_psi2", f["L1_attn_Wpsi2"].transpose(1, 0, 2))
    over_heads = lambda a: np.broadcast_to(np.asarray(a).reshape(1, -1), (16, np.asarray(a).size))
    p.add("ka_bpsi1", over_heads(f["L1_attn_bpsi1"]))
    p.add("ka_g", over_heads(f["L1_attn_ln_g"]))
    p.add("ka_b", over_heads(f["L1_attn_ln_b"]))
    p.add("ka_bphi2", over_heads(f["L1_attn_bphi2"]))
    p.add("ka_bpsi2", over_heads(f["L1_attn_bpsi2"]))
    p.add("ka_mix", over_heads(np.repeat(f["L1_attn_mixing"], 2)))
    p.add("ka_temp", over_heads(f["L1_attn_temp_scale"]))
    p.add("gamma", f["L1_attn_gamma"].reshape(16, 1))

    p = out["L1_xattn"] = Pack()
    p.add("wq", f["L1_xattn_Wq"])
    p.add("wk", f["L1_xattn_Wkv"][:, 0:1024])
    p.add("wv", f["L1_xattn_Wkv"][:, 1024:2048])
    p.add("wo", chunks_of_rows(f["L1_xattn_Wo"]))
    p.add("g_ctx", col(f["L1_xattn_ln1_g"]))
    p.add("b_ctx", col(f["L1_xattn_ln1_b"]))
    p.add("g", col(f["L1_xattn_ln2_g"]))
    p.add("b", col(f["L1_xattn_ln2_b"]))

    p = out["L1_ffn"] = Pack()
    p.add("gate", f["L1_ffn_w_gate"].T)
    p.add("up", f["L1_ffn_w_up"].T)
    p.add("down", chunks_of_rows(f["L1_ffn_w_down"].T))

    for kind, base, key in (("g", 1e6, "L2_attn_g"), ("l", 1e4, "L2_attn_l")):
        p = out[key] = Pack()
        wq = f[f"L2_attn_{kind}_wq"]
        p.add("wq", strips(wq, GROUPED))
        p.add("wq_swapped", strips(swap_pairs(wq), GROUPED))
        kv = list(range(4))
        if kind == "g":
            p.add("down", f["L2_attn_g_kv_down"])
            wk, wv = f["L2_attn_g_k_up"], f["L2_attn_g_v_up"]
        else:
            wk, wv = f["L2_attn_l_wk"], f["L2_attn_l_wv"]
        p.add("wk", strips(wk, kv))
        p.add("wk_swapped", strips(swap_pairs(wk), kv))
        p.add("wv", by_head(wv, [h // 4 for h in GROUPED]))
        p.add("wo", f[f"L2_attn_{kind}_wo"].reshape(16, 8, 128)[GROUPED].reshape(128, 128))
        p.add("g", col(f["L2_attn_norm1_w" if kind == "g" else "L2_attn_norm2_w"]))
        c, s = rope_tables(base)
        p.add("cos", c)
        p.add("sin", s)

    p = out["L2_xattn"] = Pack()
    wk = f["L2_xattn_Wkv"][:, 0:512]
    p.add("wq", f["L2_xattn_Wq"])
    p.add("wk", wk)
    p.add("wk_swapped", wk.reshape(128, 8, 2, 32)[:, :, ::-1, :].reshape(128, 512))
    p.add("wv", f["L2_xattn_Wkv"][:, 512:1024])
    p.add("wo", chunks_of_rows(f["L2_xattn_Wo"]))
    p.add("g_ctx", col(f["L2_xattn_gamma_x"]))
    p.add("b_ctx", col(f["L2_xattn_beta_x"]))
    p.add("g", col(f["L2_xattn_gamma_l"]))
    p.add("b", col(f["L2_xattn_beta_l"]))
    c, s = context_rope_tables()
    p.add("cos", c)
    p.add("sin", s)

    p = out["L2_ffn"] = Pack()
    p.add("real", f["L2_ffn_w_freq_real"])
    p.add("imag", f["L2_ffn_w_freq_imag"])
    p.add("bo", row(f["L2_ffn_bias"]))

    p = out["L3_attn"] = Pack()
    w3 = f["L3_attn_w_qkv"].T
    p.add("wq", w3[:, 0:1024])
    p.add("wk", w3[:, 1024:2048])
    p.add("wv", w3[:, 2048:3072])
    p.add("wo", chunks_of_rows(f["L3_attn_w_out"].T))
    p.add("bo", row(f["L3_attn_b_out"]))
    p.add("g", col(f["L3_attn_ln_gamma"]))
    p.add("b", col(f["L3_attn_ln_beta"]))

    p = out["L3_xattn"] = Pack()
    p.add("wq", strips(f["L3_xattn_Wq"], PLAIN))
    p.add("wk", strips(f["L3_xattn_Wk"], PLAIN))
    p.add("wv", f["L3_xattn_Wv"])
    p.add("wo", f["L3_xattn_Wo"])
    p.add("q_add", strips(row(f["L3_xattn_bq"]), PLAIN))
    p.add("k_add", strips(row(f["L3_xattn_bk"]), PLAIN))
    p.add("bv", row(f["L3_xattn_bv"]))
    p.add("bo", row(f["L3_xattn_bo"]))

    p = out["L3_ffn"] = Pack()
    down = np.zeros((8, 384, 128), np.float32)
    down[:, 0:352] = f["L3_ffn_down_w"].transpose(0, 2, 1)
    p.add("down", down.reshape(8, 3, 128, 128).transpose(2, 0, 1, 3))
    p.add("router", f["L3_ffn_router_w"].T)

    p = out["L3_ffn_gate_up"] = Pack()
    p.add("gate", f["L3_ffn_gate_w"].transpose(2, 0, 1))
    p.add("up", f["L3_ffn_up_w"].transpose(2, 0, 1))
    return out



BIG_V, BIG_O = 5 * 16 * 128 + 128, 8 * N
ONES_STEPS = 8
RING, KEYS = 6, N + 128
SLOT = 4288

VALUE_LAG, FINISH_LAG, SCORES_BY = 2, 1, 0.75

SCORE_BANK, EXPO_BANK, VALUE_BANK, TURN_BANK, OUT_BANK = 0, 2, 4, 6, 7
OUT_BANKS = (OUT_BANK, TURN_BANK, SCORE_BANK, SCORE_BANK + 1)

SIGNALS = [
    "step_v", "alpha_ready", "rope_in", "variance", "deviation", "normed", "turned", "features", "ctx_ready", "filled",
    "pair_projected", "ctx_rotated", "high", "low", "copied", "projected", "taken_v", "taken_s", "latent", "latent_kept", "rotated", "squared", "mean_square", "root",
    "divided", "rounded", "operand_ready", "score", "maximum", "guard_ready", "guard_turned", "guarded", "expo", "relu",
    "probs", "valued", "lifted", "finished", "out", "added", "keep_loaded", "keep_turned", "keep_ready",
    "logits", "shifted", "exps", "gates", "gates_turned", "gates_kept", "up", "hidden", "down", "summed",
    "converted", "ka_tensor", "ka_vector", "ka_scalar", "ka_moved",
]


class Core:

    def __init__(self, nc, ctx, dram, layouts):
        self.nc, self.dram, self.layouts = nc, dram, layouts
        self.const_at = constants().at

        def sb(name, shape, dt=F32):
            return ctx.enter_context(nc.sbuf_tensor(name, shape, dt))

        self.consts = sb("consts", [128, constants().width])
        self.x = sb("x", [128, NT, D])
        self.h = sb("h", [128, NT, D])
        self.xn = sb("xn", [128, NT, D])
        self.xt = sb("xt", [128, N])
        self.ctx_rows, self.ctx_n = self.xn[:, 0, :], self.xn[:, 1, :]
        self.ctx_raw_t = sb("ctx_raw_t", [128, 128])
        self.ctx_norm_t = sb("ctx_norm_t", [128, 80])
        self.ctx_t = sb("ctx_t", [128, 128])
        self.mask_rows = sb("mask_rows", [128, NT * NC], U8)
        self.mask_vec = sb("mask_vec", [1, 128])
        self.v = sb("v", [128, BIG_V])
        self.o = sb("o", [128, BIG_O])
        self.slot = [sb("weights_even", [128, SLOT]), sb("weights_odd", [128, SLOT])]
        self.guard_thin = sb("guard_thin", [128, 2, NT, 128])
        self.guard_wide = sb("guard_wide", [128, 2, NT, 65])
        self.ctx_rotated = sb("ctx_rotated", [128, 128])
        self.max_ctx = sb("max_ctx", [128, 2, NT])
        self.p = sb("p", [128, 4, N])
        self.sums = sb("sums", [128, 2, N])
        self.tmp = sb("tmp", [128, 2, N])
        self.keep_rows = self.tmp[:, 0, 0:NT * NC]
        self.stats = sb("stats", [128, NT, 6])
        self.mv = sb("mv", [128, NT, 2])
        self.small = sb("small", [128, 16, NT])
        self.ka = sb("ka", [128, 512])
        self.table_cells = sb("table_cells", [1, 32])
        self.scale_o = sb("scale_o", [128, 2])
        self.identity_b = sb("identity_b", [128, 128], BF16)
        self.mask_at = masks().at
        self.masks_b = {n: sb(n + "_b", [128, wide], BF16) for n, (_, wide, _) in self.mask_at.items()}
        self.ps = ctx.enter_context(nc.psum_tensor("ps", [128, 8, BANK], F32))

        self.sets = [{s: ctx.enter_context(nc.semaphore(f"{s}_{half}")) for s in SIGNALS}
                     for half in ("even", "odd")]
        self.loaded = {k: ctx.enter_context(nc.semaphore(f"loaded_{k}")) for k in layouts}
        self.x_loaded = ctx.enter_context(nc.semaphore("x_loaded"))
        self.consts_loaded = ctx.enter_context(nc.semaphore("consts_loaded"))
        self.consts_made = ctx.enter_context(nc.semaphore("consts_made"))
        self.loop_sems = ([s for half in self.sets for s in half.values()]
                          + list(self.loaded.values()) + [self.x_loaded])

    @contextmanager
    def operands(self, use, number):
        with ExitStack() as ctx:
            def sb(name, wide, dt=F32):
                return ctx.enter_context(self.nc.sbuf_tensor(f"{name}_{number}", [128, wide], dt))

            if use == "thin":
                self.q_parts = sb("q_parts", 4 * N, F32R)
                self.k_parts = sb("k_parts", 4 * N, F32R)
                self.q_guarded = sb("q_guarded", 2 * N, F32R)
                self.spare = sb("spare", 5 * N)
                self.gate_up = sb("gate_up", 16 * 352)
            elif use == "wide":
                self.q_high = sb("q_high", RING * N, F32R)
                self.q_low = sb("q_low", RING * N, F32R)
                self.k_both = sb("k_both", RING * KEYS, F32R)
                self.k_high = sb("k_high", RING * KEYS, F32R)
            else:
                self.converted = sb("converted", SLOT)
            yield

    def load_table(self, e, function, cell):
        e.activation(self.table_cells[:, cell:cell + 1], self.c("ones")[:, 0:1], function)

    def c(self, name, rows=None):
        at, wide, r = self.const_at[name]
        return self.consts[0:rows or r, at:at + wide]


class Sublayer:

    def __init__(self, core, key, number):
        self.core, self.key, self.number = core, key, number
        self.s = core.sets[number % 2]
        self.slot = core.slot[number % 2]
        self.at = core.layouts[key]

    def w(self, name):
        at, wide, rows = self.at[name]
        return self.slot[0:rows, at:at + wide]


def chained(eng, sem):
    done = [0]

    def link(ins):
        ins.then_inc(sem, 1)
        done[0] += 1
        eng.wait_ge(sem, done[0])
    return link



class Norm:

    def __init__(self, sub, kind="ln", source=None, again=None, gain=None, offset=None, keep=None,
                 next_table=ACT.Exp):
        self.next_table = next_table
        self.sub, self.kind, self.again, self.keep = sub, kind, again, keep
        self.source = source if source is not None else sub.core.x
        self.gain, self.offset = gain, offset
        self.roots = 2 if again is not None else 1

    def vector(self, e, link):
        co, s, src = self.sub.core, self.sub.s, self.source
        mean, var = co.mv[:, :, 0], co.mv[:, :, 1]
        sm = co.small
        for i in range(NT):
            last = e.bn_stats(co.stats[:, i, :], src[:, i, :])
        link(last)
        for i in range(NT):
            last = e.bn_aggr(co.mv[:, i, :], co.stats[:, i, :])
        link(last)
        if self.kind == "rms":
            link(e.tensor_tensor(sm[:, 4, :], mean, mean, ALU.mult))
            link(e.tensor_tensor(sm[:, 5, :], sm[:, 4, :], var, ALU.add))
            e.tensor_scalar(sm[:, 0, :], sm[:, 5, :], RMS_EPS, None, ALU.add).then_inc(s["variance"], 1)
        else:
            e.tensor_scalar(sm[:, 0, :], var, LN_EPS, None, ALU.add).then_inc(s["variance"], 1)
        e.wait_ge(s["deviation"], 1)
        link(e.reciprocal(sm[:, 2, :], sm[:, 1, :]))
        scale = sm[:, 2, :]
        if self.again is not None:
            link(e.tensor_tensor(sm[:, 3, :], var, scale, ALU.mult))
            link(e.tensor_tensor(sm[:, 4, :], sm[:, 3, :], scale, ALU.mult))
            e.tensor_scalar(sm[:, 0, :], sm[:, 4, :], self.again, None, ALU.add).then_inc(s["variance"], 1)
            e.wait_ge(s["deviation"], 2)
            link(e.reciprocal(sm[:, 5, :], sm[:, 1, :]))
            link(e.tensor_tensor(sm[:, 6, :], sm[:, 5, :], scale, ALU.mult))
            if self.keep is not None:
                for i in range(NT):
                    e.tensor_scalar(self.keep[:, i, :], src[:, i, :], mean[:, i:i + 1], scale[:, i:i + 1],
                                    ALU.subtract, ALU.mult)
            scale = sm[:, 6, :]
        for i in range(NT):
            if self.kind == "rms":
                ins = e.tensor_scalar(co.xn[:, i, :], src[:, i, :], scale[:, i:i + 1], None, ALU.mult)
            else:
                ins = e.tensor_scalar(co.xn[:, i, :], src[:, i, :], mean[:, i:i + 1], scale[:, i:i + 1],
                                      ALU.subtract, ALU.mult)
            ins.then_inc(s["normed"], 1)

    def scalar(self, e):
        co, s, sm = self.sub.core, self.sub.s, self.sub.core.small
        for n in range(self.roots):
            e.wait_ge(s["variance"], n + 1)
            e.activation(sm[:, 1, :], sm[:, 0, :], ACT.Sqrt).then_inc(s["deviation"], 1)
        if self.next_table is not None:
            self.sub.core.load_table(e, self.next_table, 2 * self.sub.number)
        e.wait_ge(s["turned"], 1)
        wide = co.ps[:, TURN_BANK, :]
        if self.gain is None:
            ins = e.activation(co.xt[:, :], wide, ACT.Copy)
        else:
            ins = e.activation(co.xt[:, :], wide, ACT.Identity, scale=self.gain,
                               bias=self.offset if self.offset is not None else 0.0)
        ins.then_inc(s["features"], 1)

    def tensor(self, e):
        co, s = self.sub.core, self.sub.s
        for i in range(NT):
            e.wait_ge(s["normed"], i + 1)
            last = e.transpose(co.ps[:, TURN_BANK, i * 128:i * 128 + 128], co.xn[:, i, :], co.c("identity"))
        last.then_inc(s["turned"], 1)



class Attention:
    def __init__(self, sub, wide, heads=HEADS, own=True, ctx=False, pattern="full", scale=1.0, grouped=False,
                 relu=False, alibi=False, ctx_mask=False, rope=False, latent=False, ctx_rope=False, alpha=False,
                 value_scale=False):
        self.sub, self.wide, self.heads, self.own, self.ctx, self.pattern = sub, wide, heads, own, ctx, pattern
        self.scale, self.grouped, self.relu, self.alibi, self.ctx_mask = scale, grouped, relu, alibi, ctx_mask
        self.rope, self.latent, self.ctx_rope, self.alpha = rope, latent, ctx_rope, alpha
        self.value_scale = value_scale
        self.kw = KEYS if wide else (N if own else 0) + (128 if ctx else 0)
        self.units = heads if wide else heads // 4
        self.per_unit = 1 if wide else 4
        self.per_group = 1 if wide else 8
        self.vw = heads * 128
        self.key_tiles = (list(range(NT)) if own else []) + (["ctx"] if ctx else [])
        self.jobs = self.projections()
        self.plan()

    def rows(self, pos):
        return slice(STRIP * (pos % 4), STRIP * (pos % 4) + STRIP)

    def q_col(self, pos):
        return (pos % RING if self.wide else pos // 4) * N

    def k_col(self, pos, tile):
        chunk = pos % RING if self.wide else 0 if self.grouped else pos // 4
        at = (N if self.own else 0) if tile == "ctx" else tile * 128
        return chunk * self.kw + at

    def v_cols(self, pos, tile):
        at = (len(self.key_tiles) - 1 if tile == "ctx" else tile) * self.vw + pos * 128
        return slice(at, at + 128)

    def projections(self):
        jobs = []
        for t in self.key_tiles:
            jobs += [("v", t, half) for half in range(self.heads // 8 if self.wide else 1)]
        if self.wide:
            self.pair_kinds = ["q"] + (["k"] if self.own else []) + (["kc"] if self.ctx else [])
            for i, kind in enumerate(self.pair_kinds):
                jobs.insert(3 * i, ("pair", kind, 0, i))
            return jobs
        first = []
        if not self.rope:
            first += [("q", c) for c in range(4)]
            if self.own:
                first += [("k", c) for c in range(4)]
        if self.ctx:
            first += [("kc", c) for c in range(4)]
        return first + jobs

    def ring(self, job):
        return sum(x[0] != "pair" for x in self.jobs[:self.jobs.index(job)])

    def takers(self, job):
        if job[0] != "v":
            return "sv"
        return "vs"[self.ring(job) % 2]

    def taken(self, count, who):
        return sum(who in self.takers(x) for x in [x for x in self.jobs if x[0] != "pair"][:count])

    def plan(self):
        ev, self.n = [], {}

        def score_tiles(u):
            if self.relu or u >= self.units:
                return []
            heads = range(u * self.per_unit, (u + 1) * self.per_unit)
            return [(p, t) for p in heads for t in self.key_tiles_of_scores()]

        def expo_tiles(u):
            heads = range(u * self.per_unit, (u + 1) * self.per_unit)
            return [(p, t) for p in heads for t in self.key_tiles]

        def value(pt):
            ev.append(("value",) + pt)
            if pt[1] == self.key_tiles[-1] and pt[0] % self.per_group == self.per_group - 1:
                ending.append([FINISH_LAG, pt[0] // self.per_group])

        for st in score_tiles(0):
            ev.append(("score",) + st)
        if not self.relu:
            ev.append(("guard", 0))
        waiting, ending = [], []
        for u in range(self.units):
            tiles, ahead = expo_tiles(u), score_tiles(u + 1)
            done, guarded = 0, not ahead
            for i, t in enumerate(tiles):
                ev.append(("expo",) + t)
                pair = 1 if u == 0 else (u + 3) // 2 if u % 2 else self.units
                if self.wide and 2 * pair < self.units and i < len(self.pair_kinds):
                    ev.append(("pair", self.pair_kinds[i], pair, len(self.pair_kinds) * pair + i))
                if not guarded and (i == len(tiles) - 1 or done == len(ahead)):
                    while done < len(ahead):
                        ev.append(("score",) + ahead[done])
                        done += 1
                    ev.append(("guard", u + 1))
                    guarded = True
                want = int(np.ceil((i + 1) * len(ahead) / (SCORES_BY * len(tiles))))
                while done < min(want, len(ahead)):
                    ev.append(("score",) + ahead[done])
                    done += 1
                waiting.append(t)
                if len(waiting) > VALUE_LAG:
                    value(waiting.pop(0))
                for x in list(ending):
                    x[0] -= 1
                    if x[0] == -1:
                        ev.append(("lift", x[1]))
                        if x[1] % 2 == 0:
                            ending.remove(x)
                    if x[0] < -1:
                        ev.append(("divide", x[1] // 2, -2 - x[0]))
                        if x[0] == -1 - NT:
                            ending.remove(x)
        for t in waiting:
            value(t)
        for left, g in ending:
            if left >= 0:
                ev.append(("lift", g))
            if g % 2:
                ev += [("divide", g // 2, i) for i in range(max(0, -1 - left), NT)]
        count, self.steps = {}, []
        self.upto = {}
        for e in ev:
            k = e[0]
            if k in ("pair", "lift", "divide"):
                self.steps.append(e)
                continue
            self.steps.append(e + (count.get(k, 0),))
            count[k] = count.get(k, 0) + 1
            if k in ("score", "expo"):
                self.upto[(k, e[1] // self.per_unit)] = count[k]
            if k == "value":
                self.upto[(k, e[1] // self.per_group)] = count[k]

    def key_tiles_of_scores(self):
        return (list(range(NT)) if self.own else []) + (["ctx"] if self.ctx else [])

    def score_keys(self, qt):
        if self.pattern == "causal":
            return 0, 128 * (qt + 1), 128 * qt, self.sub.core.masks_b["causal"][:, :]
        if self.pattern == "local":
            first = max(0, 128 * qt - STRIP)
            n = 128 * (qt + 1) - first
            return first, n, 0, self.sub.core.masks_b["local"][:, 160 - n:160]
        return 0, N, None, None

    def expo_queries(self, kt):
        if kt == "ctx" or self.pattern == "full":
            return 0, N, None
        if self.pattern == "causal":
            return 128 * kt, N - 128 * kt, self.sub.core.masks_b["causal_t"][:, :]
        n = min(160, N - 128 * kt)
        return 128 * kt, n, self.sub.core.masks_b["local_t"][:, 0:n]


    def fill(self, e):
        co, s = self.sub.core, self.sub.s
        tiles = len(self.key_tiles)
        if self.wide:
            v = co.v[:, 0:tiles * self.vw].rearrange("p (h two c) -> p h two c", two=2, c=128)
            e.memset(v[:, :, 0, 64:128], 1.0).then_inc(s["filled"], 1)
            e.wait_ge(s["filled"], 1)
            e.memset(v[:, :, 1, 0:64], 1.0).then_inc(s["filled"], 1)
            for i in range(ONES_STEPS):
                e.wait_ge(s["filled"], 2 + i)
                wide = RING * KEYS // ONES_STEPS
                e.tensor_copy(co.k_high[64:65, i * wide:i * wide + wide], co.c("ones")[:, 0:wide])\
                    .then_inc(s["filled"], 1)
            return
        e.memset(co.v[:, 0:tiles * self.vw + 128], 0.0).then_inc(s["filled"], 1)
        e.wait_ge(s["filled"], 1)
        for t in range(tiles):
            for g in range(2):
                at = t * self.vw + g * 1024
                ones = co.v[:, at:at + 8 * 136].rearrange("p (h r) -> p h r", r=136)
                ones = ones[:, :, 64:72] if g == 0 else ones[:, :, 0:8]
                last = e.memset(ones, 1.0)
        last.then_inc(s["filled"], 1)

    def project_tensor(self, e):
        co, s, w = self.sub.core, self.sub.s, self.sub.w
        e.wait_ge(s["features"], 1)
        ctx_t = self.ctx_source()
        if self.ctx and ctx_t is co.ctx_t:
            e.wait_ge(s["ctx_ready"], 1)
        ksrc = co.xt[:, :]
        if self.latent:
            e.matmul(co.ps[0:32, OUT_BANK, :], w("down"), co.xt[:, :], start=True, stop=True)\
                .then_inc(s["latent"], 1)
            e.wait_ge(s["latent_kept"], 1)
            ksrc = co.sums[0:32, 0, :]
        if self.rope:
            self.rope_tensor(e, ksrc)
        for job in self.jobs:
            if job[0] == "pair":
                self.pair_tensor(e, job)
                continue
            j = self.ring(job)
            if j >= 6:
                e.wait_ge(s["taken_v"], self.taken(j - 5, "v"))
                if self.taken(j - 5, "s"):
                    e.wait_ge(s["taken_s"], self.taken(j - 5, "s"))
            elif j == 0 and self.rope:
                e.wait_ge(s["operand_ready"], 5)
            bank = co.ps[:, j % 6, :]
            kind = job[0]
            if kind in ("q", "k"):
                c = job[1]
                more = kind + "_add" in self.sub.at
                last = e.matmul(bank, w("w" + kind)[:, c * 128:c * 128 + 128], co.xt[:, :], start=True,
                                stop=not more)
                if more:
                    add = w(kind + "_add")
                    last = e.matmul(bank, add[:, c * 128:c * 128 + 128],
                                    co.c("ones_and_position")[0:add.shape[0], :], start=False, stop=True)
            elif kind == "kc":
                c = job[1]
                n = 128
                last = e.matmul(bank[:, 0:n], w("wk")[:, c * 128:c * 128 + 128], ctx_t[:, 0:n], start=True,
                                stop=not self.ctx_mask)
                if self.ctx_mask:
                    e.matmul(bank[:, 0:n], w("k_add")[:, c * 128:c * 128 + 128], co.c("ones")[:, 0:n],
                             start=False, stop=False)
                    last = e.matmul(bank[:, 0:n], co.c("mask_row"), co.mask_vec[:, 0:n], start=False, stop=True)
            else:
                _, t, half = job
                m = NC if t == "ctx" else 128
                lhs = ctx_t[:, 0:NC] if t == "ctx" else ksrc[:, t * 128:t * 128 + 128]
                n = 512 if self.wide else 128
                biased = "bv" in self.sub.at
                last = e.matmul(bank[0:m, 0:n], lhs, w("wv")[:, half * n:half * n + n], start=True,
                                stop=not biased)
                if biased:
                    last = e.matmul(bank[0:m, 0:n], co.c("ones")[:, 0:m], w("bv"), start=False, stop=True)
            last.then_inc(s["projected"], 1)
        e.wait_ge(s["taken_v"], self.taken(99, "v"))
        e.wait_ge(s["taken_s"], self.taken(99, "s"))
        e.wait_ge(s["filled"], 2 + ONES_STEPS if self.wide else 2)

    def ctx_source(self):
        co = self.sub.core
        return co.ctx_t if "g_ctx" in self.sub.at else co.ctx_raw_t

    def take(self, e, job, part, copy):
        co, w = self.sub.core, self.sub.w
        bank = co.ps[:, self.ring(job) % 6, :]
        kind = job[0]
        if kind in ("q", "k", "kc"):
            c = job[1]
            n = N if kind != "kc" else 128
            rounded = co.tmp[:, self.ring(job) % 2, 0:n]
            side = "q" if kind == "q" else "k"
            by = lambda part: co.ka[:, 480 + 4 * part + c:481 + 4 * part + c] if self.alpha and side == "q" \
                else co.c(side + "_" + "ab"[part])
            if part == "round":
                return e.activation(rounded.bitcast(F32R), bank[:, 0:n], ACT.Identity, scale=by(1),
                                    bias=co.c(side + "_bias"))
            dst, at = (co.q_parts, self.q_col(4 * c)) if kind == "q" else \
                (co.k_parts, self.k_col(4 * c, "ctx" if kind == "kc" else 0))
            return e.scalar_tensor_tensor(out=dst[:, at:at + n], in0=bank[:, 0:n], scalar=by(0),
                                          in1=rounded, op0=ALU.mult, op1=ALU.add)
        _, t, half = job
        m = NC if t == "ctx" else 128
        if self.wide:
            at = self.v_cols(half * 8, t).start
            dst = co.v[0:m, at:at + 8 * 128].rearrange("p (h two c) -> p h two c", two=4, c=64)[:, :, 0:4:3, :]
            return copy(dst, bank[0:m, 0:512].rearrange("p (h two c) -> p h two c", two=2, c=64))
        at = self.v_cols(0, t).start
        for g in range(2):
            dst = co.v[0:m, at + g * 1024:at + g * 1024 + 8 * 136].rearrange("p (h r) -> p h r", r=136)
            last = copy(dst[:, :, 64 * g:64 * g + 8], bank[0:m, g * 64:g * 64 + 64].rearrange("p (h c) -> p h c", c=8))
        return last

    def project_vector(self, e, link):
        co, s, w = self.sub.core, self.sub.s, self.sub.w
        if self.alpha:
            for part in (0, 1):
                e.tensor_tensor(co.ka[:, 480 + 4 * part:484 + 4 * part], w("alpha"), co.c("alpha_" + "ab"[part]),
                                ALU.mult).then_inc(s["alpha_ready"], 1)
            e.wait_ge(s["alpha_ready"], 2)
        if self.rope:
            self.rope_vector(e, link)

        for job in self.jobs:
            if job[0] == "pair":
                self.pair_vector(e, link, job)
                continue
            j = self.ring(job)
            if self.takers(job) == "sv":
                e.wait_ge(s["taken_s"], self.taken(j + 1, "s"))
                self.take(e, job, "add", None).then_inc(s["taken_v"], 1)
            elif self.takers(job) == "v":
                e.wait_ge(s["projected"], j + 1)
                e.wait_ge(s["filled"], 2)
                self.take(e, job, None, e.tensor_copy).then_inc(s["taken_v"], 1)

    def project_scalar(self, e):
        co, s, w = self.sub.core, self.sub.s, self.sub.w
        if self.latent:
            e.wait_ge(s["latent"], 1)
            e.activation(co.sums[0:32, 0, :], co.ps[0:32, OUT_BANK, :], ACT.Copy).then_inc(s["latent_kept"], 1)
        if self.rope:
            self.rope_scalar(e)
        if self.alpha:
            e.wait_ge(s["alpha_ready"], 2)

        for job in self.jobs:
            if job[0] == "pair":
                self.pair_scalar(e, job)
                continue
            j = self.ring(job)
            if "s" not in self.takers(job):
                continue
            e.wait_ge(s["projected"], j + 1)
            if self.takers(job) == "sv":
                if j >= 2:
                    e.wait_ge(s["taken_v"], self.taken(j - 1, "v"))
                self.take(e, job, "round", None).then_inc(s["taken_s"], 1)
            else:
                e.wait_ge(s["filled"], 2)
                self.take(e, job, None, lambda out, in_: e.activation(out, in_, ACT.Copy))\
                    .then_inc(s["taken_s"], 1)


    def pair_at(self, kind, part):
        return slice(64 * part, 64 * part + 64), slice(64 - 64 * part, 128 - 64 * part), \
            N if kind != "kc" else 128

    def pair_cols(self, kind, pair, part):
        pos = 2 * pair + part
        if kind == "q":
            return slice(self.q_col(pos), self.q_col(pos) + N)
        at = self.k_col(pos, "ctx" if kind == "kc" else 0)
        return slice(at, at + (128 if kind == "kc" else N))

    def pair_tensor(self, e, job):
        co, s, w = self.sub.core, self.sub.s, self.sub.w
        _, kind, pair, j = job
        if j >= 1:
            e.wait_ge(s["low"], 2 * j)
        bank = co.ps[:, OUT_BANK, :]
        at = slice(pair * 128, pair * 128 + 128)
        src = co.xt[:, :] if kind != "kc" else self.ctx_source()[:, :]
        last = e.matmul(bank[:, 0:src.shape[1]], w("wq" if kind == "q" else "wk")[:, at], src, start=True,
                        stop=True, skip_group_check=True)
        if kind == "kc" and self.ctx_rope:
            last = e.matmul(bank[:, 128:256], w("wk_swapped")[:, at], src, start=True, stop=True,
                            skip_group_check=True)
        last.then_inc(s["pair_projected"], 1)

    def pair_source(self, kind):
        co = self.sub.core
        return co.ctx_rotated[:, :] if kind == "kc" and self.ctx_rope else co.ps[:, OUT_BANK, :]

    def pair_room(self, e, pair):
        s = self.sub.s
        before = 2 * pair + 1 - RING
        if before >= 0:
            e.wait_ge(s["expo"], self.upto[("expo", before)])
            e.wait_ge(s["score"], self.upto[("score", before)])

    def pair_scalar(self, e, job):
        co, s = self.sub.core, self.sub.s
        _, kind, pair, j = job
        self.pair_room(e, pair)
        if kind == "kc" and self.ctx_rope:
            e.wait_ge(s["ctx_rotated"], pair + 1)
        else:
            e.wait_ge(s["pair_projected"], j + 1)
        for part in range(2):
            rows, _, n = self.pair_at(kind, part)
            dst = co.q_high if kind == "q" else co.k_both
            e.activation(dst[rows, self.pair_cols(kind, pair, part)], self.pair_source(kind)[rows, 0:n], ACT.Copy)\
                .then_inc(s["high"], 1)

    def pair_vector(self, e, link, job):
        co, s, w = self.sub.core, self.sub.s, self.sub.w
        _, kind, pair, j = job
        if kind == "kc" and self.ctx_rope:
            bank, turned = co.ps[:, OUT_BANK, :], co.tmp
            e.wait_ge(s["pair_projected"], j + 1)
            if pair:
                e.wait_ge(s["low"], 2 * (j - len(self.pair_kinds)) + 2)
            link(e.tensor_tensor(turned[:, 0, 0:NC], bank[:, 0:NC], w("cos"), ALU.mult))
            link(e.tensor_tensor(turned[:, 1, 0:NC], bank[:, 128:128 + NC], w("sin"), ALU.mult))
            e.tensor_tensor(co.ctx_rotated[:, 0:NC], turned[:, 0, 0:NC], turned[:, 1, 0:NC], ALU.add)\
                .then_inc(s["ctx_rotated"], 1)
        self.pair_room(e, pair)
        for part in range(2):
            rows, other, n = self.pair_at(kind, part)
            cols = self.pair_cols(kind, pair, part)
            e.wait_ge(s["high"], 2 * j + part + 1)
            high = (co.q_high if kind == "q" else co.k_both)[rows, cols].bitcast(F32)
            low = co.q_low[0:64, cols] if kind == "q" else co.k_both[other, cols]
            e.tensor_tensor(low, self.pair_source(kind)[rows, 0:n], high, ALU.subtract).then_inc(s["low"], 1)

    def pair_pool(self, e, job):
        co, s = self.sub.core, self.sub.s
        _, kind, pair, j = job
        self.pair_room(e, pair)
        for part in range(2):
            rows, other, _ = self.pair_at(kind, part)
            cols = self.pair_cols(kind, pair, part)
            e.wait_ge(s["high"], 2 * j + part + 1)
            if j or part:
                e.wait_ge(s["copied"], 2 * j + part)
            else:
                e.wait_ge(s["filled"], 2 + ONES_STEPS)
            if kind == "q":
                ins = e.tensor_copy(co.q_high[other, cols], co.q_high[rows, cols])
            else:
                ins = e.tensor_copy(co.k_high[0:64, cols], co.k_both[rows, cols])
            ins.then_inc(s["copied"], 1)

    def attend_pool(self, e):
        for step in self.jobs + self.steps:
            if step[0] == "pair":
                self.pair_pool(e, step)


    def rope_operand(self, j):
        co = self.sub.core
        return co.q_parts[:, j * N:j * N + N] if j < 4 else co.k_parts[:, 0:N]

    def rope_product(self, j):
        return self.sub.core.spare[:, j * N:(j + 1) * N]

    def rope_tensor(self, e, ksrc):
        co, s, w = self.sub.core, self.sub.s, self.sub.w

        def rotate(j):
            if j >= 3:
                e.wait_ge(s["rotated"], j - 2)
            for half, name in ((0, ""), (1, "_swapped")):
                lhs = w("wq" + name)[:, j * 128:j * 128 + 128] if j < 4 else w("wk" + name)
                last = e.matmul(co.ps[:, 2 * (j % 3) + half, :], lhs, co.xt[:, :] if j < 4 else ksrc,
                                start=True, stop=True)
            last.then_inc(s["rope_in"], 1)

        rotate(0)
        for j in range(5):
            if j < 4:
                rotate(j + 1)
            e.wait_ge(s["squared"], j + 1)
            if j >= 1:
                e.wait_ge(s["root"], j)
            e.matmul(co.ps[:, TURN_BANK, :], co.c("strip_mean"), co.o[:, (j % 2) * N:(j % 2) * N + N],
                     start=True, stop=True).then_inc(s["mean_square"], 1)

    def rope_vector(self, e, link):
        co, s, w = self.sub.core, self.sub.s, self.sub.w
        t = co.o[:, 2 * N:4 * N].rearrange("p (a n) -> p a n", a=2)

        def rotate(j):
            e.wait_ge(s["rope_in"], j + 1)
            if j >= 1:
                e.wait_ge(s["rotated"], j)
            link(e.tensor_tensor(t[:, 0, :], co.ps[:, 2 * (j % 3), :], w("cos"), ALU.mult))
            link(e.tensor_tensor(t[:, 1, :], co.ps[:, 2 * (j % 3) + 1, :], w("sin"), ALU.mult))
            e.tensor_tensor(self.rope_product(j), t[:, 0, :], t[:, 1, :], ALU.add).then_inc(s["rotated"], 1)

        def split(j):
            e.wait_ge(s["rounded"], j + 1)
            e.scalar_tensor_tensor(out=self.rope_operand(j), in0=self.rope_product(j),
                                   scalar=co.c("q_a" if j < 4 else "k_a"), in1=co.tmp[:, j % 2, :],
                                   op0=ALU.mult, op1=ALU.add).then_inc(s["operand_ready"], 1)

        rotate(0)
        for j in range(5):
            if j < 4:
                rotate(j + 1)
            e.wait_ge(s["root"], j + 1)
            root = co.o[:, (4 + j % 2) * N:(5 + j % 2) * N]
            link(e.reciprocal(root, root))
            e.tensor_tensor(self.rope_product(j), self.rope_product(j), root, ALU.mult)\
                .then_inc(s["divided"], 1)
            if j >= 1:
                split(j - 1)
        split(4)

    def rope_scalar(self, e):
        co, s = self.sub.core, self.sub.s

        def round_(j):
            e.wait_ge(s["divided"], j + 1)
            if j >= 2:
                e.wait_ge(s["operand_ready"], j - 1)
            side = "q" if j < 4 else "k"
            e.activation(co.tmp[:, j % 2, :].bitcast(F32R), self.rope_product(j), ACT.Identity,
                         scale=co.c(side + "_b"), bias=co.c(side + "_bias")).then_inc(s["rounded"], 1)

        for j in range(5):
            e.wait_ge(s["rotated"], j + 1)
            if j >= 2:
                e.wait_ge(s["mean_square"], j - 1)
            e.activation(co.o[:, (j % 2) * N:(j % 2) * N + N], self.rope_product(j), ACT.Square)\
                .then_inc(s["squared"], 1)
            if j >= 1:
                round_(j - 1)
            e.wait_ge(s["mean_square"], j + 1)
            e.activation(co.o[:, (4 + j % 2) * N:(5 + j % 2) * N], co.ps[:, TURN_BANK, :], ACT.Sqrt,
                         bias=co.c("rms_eps")).then_inc(s["root"], 1)
        round_(4)


    def guard(self):
        return self.sub.core.guard_wide if self.wide else self.sub.core.guard_thin

    def guard_col(self, pos):
        return 64 if self.wide else STRIP * (pos % 4) + MAX_ROW

    def attend_tensor(self, e):
        co, s = self.sub.core, self.sub.s
        ps = co.ps
        for step in self.steps:
            kind, n = step[0], step[-1]
            if kind == "pair":
                self.pair_tensor(e, step)
            elif kind == "score":
                _, pos, t, _ = step
                if self.wide:
                    r, q, k = slice(0, 128), co.q_high, co.k_both
                    if pos % 2 == 0:
                        e.wait_ge(s["low"], 2 * len(self.pair_kinds) * (pos // 2 + 1))
                        e.wait_ge(s["copied"], 2 * len(self.pair_kinds) * (pos // 2 + 1))
                else:
                    r, q, k = self.rows(pos), co.q_parts, co.k_parts
                qc = self.q_col(pos)
                bank = ps[:, SCORE_BANK + n % 2, :]
                if n >= 2:
                    e.wait_ge(s["maximum"], n - 1)
                if t == "ctx":
                    kc = self.k_col(pos, "ctx")
                    for i in range(NT):
                        last = e.matmul(bank[:, i * 80:i * 80 + 80], q[r, qc + i * 128:qc + i * 128 + 128],
                                        k[r, kc:kc + 80], start=True, stop=True, skip_group_check=True)
                else:
                    first, m, mc, mask = self.score_keys(t)
                    kc = self.k_col(pos, 0) + first
                    last = e.matmul(bank[:, 0:m], q[r, qc + t * 128:qc + t * 128 + 128], k[r, kc:kc + m],
                                    start=True, stop=mask is None, skip_group_check=True)
                    if mask is not None:
                        last = e.matmul(bank[:, mc:mc + mask.shape[1]], co.identity_b[:, :], mask,
                                        start=False, stop=True, skip_group_check=True)
                last.then_inc(s["score"], 1)
            elif kind == "guard":
                u = step[1]
                e.wait_ge(s["maximum"], self.upto[("score", u)])
                if self.own and self.ctx:
                    e.wait_ge(s["guard_ready"], (u + 1) * self.per_unit)
                if n >= 1:
                    e.wait_ge(s["guarded"], n)
                g = self.guard()
                m = g.shape[3]
                for i in range(NT):
                    last = e.transpose(ps[0:m, TURN_BANK, i * 128:i * 128 + 128], g[:, u % 2, i, :],
                                       co.c("identity"))
                last.then_inc(s["guard_turned"], 1)
            elif kind == "expo":
                _, pos, t, _ = step
                u = pos // self.per_unit
                first, m, mask = self.expo_queries(t)
                bank = ps[:, EXPO_BANK + n % 2, 0:m]
                if n >= 2:
                    e.wait_ge(s["relu" if self.relu else "probs"], n - 1)
                if not self.relu:
                    e.wait_ge(s["guarded"], u + 1)
                kc, qc = self.k_col(pos, t), self.q_col(pos) + first
                if self.wide:
                    e.matmul(bank, co.k_both[:, kc:kc + 128], co.q_high[:, qc:qc + m], start=True, stop=False,
                             skip_group_check=True)
                    last = e.matmul(bank, co.k_high[0:65, kc:kc + 128], co.q_low[0:65, qc:qc + m], start=False,
                                    stop=mask is None, skip_group_check=True)
                else:
                    r = self.rows(pos)
                    if self.relu:
                        moving = co.q_parts[r, qc:qc + m]
                    else:
                        moving = co.q_guarded[r, u % 2 * N + first:u % 2 * N + first + m]
                    last = e.matmul(bank, co.k_parts[r, kc:kc + 128], moving, start=True, stop=mask is None,
                                    skip_group_check=True)
                if mask is not None:
                    last = e.matmul(bank[:, 0:mask.shape[1]], co.identity_b[:, :], mask, start=False, stop=True,
                                    skip_group_check=True)
                last.then_inc(s["expo"], 1)
            elif kind == "value":
                _, pos, t, _ = step
                g = pos // self.per_group
                first, m, _ = self.expo_queries(t)
                keys = NC if t == "ctx" else 128
                e.wait_ge(s["probs"], n + 1)
                opens = t == self.key_tiles[0] and pos % self.per_group == 0
                closes = t == self.key_tiles[-1] and pos % self.per_group == self.per_group - 1
                if opens and g >= 2:
                    e.wait_ge(s["lifted"], 2 * g - 2)
                e.matmul(ps[:, VALUE_BANK + g % 2, first:first + m], co.v[0:keys, self.v_cols(pos, t)],
                         co.p[0:keys, n % 4, 0:m], start=opens, stop=closes, skip_group_check=True)\
                    .then_inc(s["valued"], 1)

    def attend_vector(self, e, link):
        co, s = self.sub.core, self.sub.s
        ps = co.ps
        if self.relu:
            e.wait_ge(s["keep_ready"], 1)
        for step in self.steps:
            kind, n = step[0], step[-1]
            if kind == "pair":
                self.pair_vector(e, link, step)
            elif kind == "score":
                _, pos, t, _ = step
                u = pos // self.per_unit
                e.wait_ge(s["score"], n + 1)
                bank = ps[:, SCORE_BANK + n % 2, :]
                g = self.guard()[:, u % 2, :, self.guard_col(pos)]
                if t == "ctx":
                    out = co.max_ctx[:, n % 2, :] if self.own else g
                    ins = e.tensor_reduce(out, bank[:, 0:NT * 80].rearrange("p (i k) -> p i k", k=80)[:, :, 0:NC], AX.X,
                                          ALU.max, negate=True)
                    ins.then_inc(s["maximum"], 1)
                    if self.own:
                        e.wait_ge(s["maximum"], n + 1)
                        e.tensor_tensor(g, g, out, ALU.min).then_inc(s["guard_ready"], 1)
                else:
                    _, m, _, _ = self.score_keys(t)
                    e.tensor_reduce(g[:, t:t + 1], bank[:, 0:m], AX.X, ALU.max, negate=True)\
                        .then_inc(s["maximum"], 1)
            elif kind == "guard":
                u = step[1]
                e.wait_ge(s["guard_turned"], u + 1)
                if self.wide:
                    qc = self.q_col(u)
                    e.tensor_copy(co.q_low[64:65, qc:qc + N], ps[64:65, TURN_BANK, :]).then_inc(s["guarded"], 1)
                else:
                    if u >= 2:
                        e.wait_ge(s["expo"], self.upto[("expo", u - 2)])
                    e.tensor_tensor(co.q_guarded[:, u % 2 * N:u % 2 * N + N],
                                    co.q_parts[:, u * N:u * N + N].bitcast(F32),
                                    ps[:, TURN_BANK, :], ALU.add).then_inc(s["guarded"], 1)
            elif kind == "expo" and self.relu:
                e.wait_ge(s["relu"], n + 1)
                r = co.tmp[0:NC, n % 2, :]
                masked = co.spare[0:NC, (1 + n % 2) * N:(2 + n % 2) * N]
                link(e.tensor_tensor(masked, r, co.spare[0:NC, 0:N], ALU.mult))
                if n >= 4:
                    e.wait_ge(s["valued"], n - 3)
                e.tensor_tensor(co.p[0:NC, n % 4, :], masked, r, ALU.mult).then_inc(s["probs"], 1)
            elif kind == "divide":
                _, pair, i = step
                e.wait_ge(s["lifted"], 4 * pair + 4)
                sums = co.sums[:, pair % 2, i * 128:i * 128 + 128]
                out = co.o[:, pair * N + i * 128:pair * N + i * 128 + 128]
                if self.relu:
                    link(e.tensor_scalar(sums, sums, 1e-32, None, ALU.add))
                link(e.reciprocal(sums, sums))
                if self.value_scale:
                    e.wait_ge(s["ka_moved"], 32)
                    ins = e.scalar_tensor_tensor(out=out, in0=out, scalar=co.scale_o[:, 0:1], in1=sums,
                                                 op0=ALU.mult, op1=ALU.mult)
                else:
                    ins = e.tensor_tensor(out, out, sums, ALU.mult)
                ins.then_inc(s["finished"], 1)

    def attend_scalar(self, e):
        co, s, w = self.sub.core, self.sub.s, self.sub.w
        for step in self.steps:
            if step[0] == "pair":
                self.pair_scalar(e, step)
            elif step[0] == "lift":
                g = step[1]
                e.wait_ge(s["valued"], self.upto[("value", g)])
                if g >= 4:
                    e.wait_ge(s["finished"], NT * (g // 2 - 1))
                rows, other, _ = self.pair_at(None, g % 2)
                bank = co.ps[:, VALUE_BANK + g % 2, :]
                e.activation(co.sums[rows, g // 2 % 2, :], bank[other, :], ACT.Copy).then_inc(s["lifted"], 1)
                e.activation(co.o[rows, g // 2 * N:g // 2 * N + N], bank[rows, :], ACT.Copy)\
                    .then_inc(s["lifted"], 1)
            if step[0] != "expo":
                continue
            _, pos, t, n = step
            _, m, _ = self.expo_queries(t)
            keys = NC if t == "ctx" else 128
            e.wait_ge(s["expo"], n + 1)
            bank = co.ps[0:keys, EXPO_BANK + n % 2, 0:m]
            if self.relu:
                if n >= 2:
                    e.wait_ge(s["probs"], n - 1)
                e.activation(co.tmp[0:keys, n % 2, :], bank, ACT.Relu, scale=self.scale,
                             bias=w("sn_bias")[0:keys, 0:1]).then_inc(s["relu"], 1)
            else:
                if n >= 4:
                    e.wait_ge(s["valued"], n - 3)
                e.activation(co.p[0:keys, n % 4, 0:m], bank, ACT.Exp, scale=self.scale).then_inc(s["probs"], 1)


    def output_tensor(self, e):
        co, s, w = self.sub.core, self.sub.s, self.sub.w
        pairs = self.heads // self.per_group // 2
        biased = "bo" in self.sub.at
        for i in range(NT):
            e.wait_ge(s["finished"], NT * (pairs - 1) + i + 1)
            out = co.ps[:, OUT_BANKS[i], 0:128]
            for c in range(pairs):
                last = e.matmul(out, co.o[:, c * N + i * 128:c * N + i * 128 + 128],
                                w("wo")[:, c * 128:c * 128 + 128], start=c == 0,
                                stop=c == pairs - 1 and not biased, skip_group_check=True)
            if biased:
                last = e.matmul(out, co.c("ones")[:, 0:128], w("bo"), start=False, stop=True,
                                skip_group_check=True)
            last.then_inc(s["out"], 1)

    def output_vector(self, e, link, into):
        co, s = self.sub.core, self.sub.s
        for i in range(NT):
            e.wait_ge(s["out"], i + 1)
            link(e.tensor_tensor(into[:, i, :], into[:, i, :], co.ps[:, OUT_BANKS[i], 0:128], ALU.add))


def attention_sublayer(core, load_next, clear, key, number, norm, keep_h=False, add_h=False, **kinds):
    sub = Sublayer(core, key, number)
    s, w = sub.s, sub.w
    at = Attention(sub, **kinds)
    nm = Norm(sub, gain=w("g") if "g" in sub.at else None, offset=w("b") if "b" in sub.at else None,
              keep=core.h if keep_h else None, source=core.h if add_h else None, **norm)
    into = core.h if keep_h or add_h else core.x
    own_ctx = kinds.get("ctx") and "g_ctx" in sub.at

    with core.nc.Block() as block:

        @block.sync
        def _(sp):
            load_next(sp)
            if at.value_scale:
                ka_sync(sub, sp)

        @block.gpsimd
        def _(pool):
            clear(pool)
            at.fill(pool)
            at.attend_pool(pool)

        @block.vector
        def _(dve):
            link = chained(dve, s["step_v"])
            dve.wait_ge(core.loaded[key], 16)
            nm.vector(dve, link)
            if own_ctx:
                dve.tensor_scalar(core.ctx_t[:, 0:NC], core.ctx_norm_t[:, 0:NC], w("g_ctx"), w("b_ctx"),
                                  ALU.mult, ALU.add).then_inc(s["ctx_ready"], 1)
            if at.relu:
                keep_vector(sub, dve)
            if at.value_scale:
                ka_vector(sub, dve, link)
            at.project_vector(dve, link)
            at.attend_vector(dve, link)
            at.output_vector(dve, link, into)
            if add_h:
                flat = lambda a: a[:, :, :].rearrange("p i d -> p (i d)")
                dve.tensor_tensor(flat(core.x), flat(core.x), flat(core.h), ALU.add).then_inc(s["added"], 1)

        @block.scalar
        def _(act):
            act.wait_ge(core.loaded[key], 16)
            nm.scalar(act)
            if at.relu:
                keep_scalar(sub, act)
            if at.value_scale:
                ka_scalar(sub, act)
            at.project_scalar(act)
            at.attend_scalar(act)
            core.load_table(act, ACT.Sqrt, 2 * number + 1)

        @block.tensor
        def _(pe):
            pe.wait_ge(core.loaded[key], 16)
            nm.tensor(pe)
            if at.relu:
                keep_tensor(sub, pe)
            if at.value_scale:
                ka_tensor(sub, pe)
            at.project_tensor(pe)
            at.attend_tensor(pe)
            at.output_tensor(pe)



def keep_vector(sub, e):
    co, s = sub.core, sub.s
    e.wait_ge(co.x_loaded, 64)
    e.tensor_scalar(co.keep_rows[:, :], co.mask_rows[:, :], -1.0, 1.0, ALU.mult, ALU.add)\
        .then_inc(s["keep_loaded"], 1)


def keep_tensor(sub, e):
    co, s = sub.core, sub.s
    e.wait_ge(s["keep_loaded"], 1)
    for i in range(NT):
        last = e.transpose(co.ps[0:NC, OUT_BANK, i * 128:i * 128 + 128], co.keep_rows[:, i * NC:i * NC + NC],
                           co.c("identity"))
    last.then_inc(s["keep_turned"], 1)


def keep_scalar(sub, e):
    co, s = sub.core, sub.s
    e.wait_ge(s["keep_turned"], 1)
    e.activation(co.spare[0:NC, 0:N], co.ps[0:NC, OUT_BANK, :], ACT.Copy).then_inc(s["keep_ready"], 1)



KA_QK, KA_AX, KA_PHI, KA_PSI, KA_TURNED, KA_PHI2, KA_PSI2, KA_OUT = 16, 32, 96, 160, 240, 304, 320, 336
KA_STATS, KA_VAR = 400, 440


def ka_tensor(sub, e):
    co, s, w = sub.core, sub.s, sub.w
    ps, ka = co.ps[:, OUT_BANK, :], co.ka
    e.wait_ge(s["ka_vector"], 1)
    for h in range(HEADS):
        last = e.matmul(ps[0:16, h:h + 1], w("wqk_mean")[:, 16 * h:16 * h + 16], ka[:, 1:2], start=True,
                        stop=True, skip_group_check=True)
    last.then_inc(s["ka_tensor"], 1)
    e.wait_ge(s["ka_scalar"], 1)
    for t in range(4):
        e.matmul(ps[0:16, KA_AX + 16 * t:KA_AX + 16 * t + 16], w("ka_a")[:, 16 * t:16 * t + 16],
                 ka[0:16, KA_QK:KA_QK + 16], start=True, stop=True, skip_group_check=True)
        last = e.matmul(ps[0:8, KA_PHI + 16 * t:KA_PHI + 16 * t + 16], w("ka_phi1")[:, 8 * t:8 * t + 8],
                        ka[0:16, KA_QK:KA_QK + 16], start=True, stop=True, skip_group_check=True)
    last.then_inc(s["ka_tensor"], 1)
    e.wait_ge(s["ka_vector"], 2)
    e.wait_ge(s["ka_scalar"], 2)
    for t in range(4):
        e.matmul(ps[0:16, KA_PSI + 16 * t:KA_PSI + 16 * t + 16], ka[0:16, KA_AX + 16 * t:KA_AX + 16 * t + 16],
                 w("ka_psi1")[:, 16 * t:16 * t + 16], start=True, stop=True, skip_group_check=True)
        last = e.matmul(ps[0:16, KA_PHI2 + 2 * t:KA_PHI2 + 2 * t + 2], ka[0:8, KA_PHI + 16 * t:KA_PHI + 16 * t + 16],
                        w("ka_phi2")[:, 2 * t:2 * t + 2], start=True, stop=True, skip_group_check=True)
    last.then_inc(s["ka_tensor"], 1)
    e.wait_ge(s["ka_scalar"], 4)
    for t in range(4):
        last = e.transpose(ps[0:16, KA_TURNED + 16 * t:KA_TURNED + 16 * t + 16],
                           ka[0:16, KA_PSI + 16 * t:KA_PSI + 16 * t + 16], co.c("identity")[0:16, 0:16])
    last.then_inc(s["ka_tensor"], 1)
    e.wait_ge(s["ka_vector"], 5)
    for t in range(4):
        last = e.matmul(ps[0:16, KA_PSI2 + 2 * t:KA_PSI2 + 2 * t + 2],
                        ka[0:16, KA_TURNED + 16 * t:KA_TURNED + 16 * t + 16], w("ka_psi2")[:, 2 * t:2 * t + 2],
                        start=True, stop=True, skip_group_check=True)
    last.then_inc(s["ka_tensor"], 1)


def ka_vector(sub, e, link):
    co, s, w = sub.core, sub.s, sub.w
    ps, ka = co.ps[:, OUT_BANK, :], co.ka
    e.wait_ge(s["features"], 1)
    link(e.tensor_reduce(ka[:, 0:1], co.xt[:, :], AX.X, ALU.add))
    e.tensor_scalar(ka[:, 1:2], ka[:, 0:1], 1.0 / N, None, ALU.mult).then_inc(s["ka_vector"], 1)
    e.wait_ge(s["ka_tensor"], 2)
    e.tensor_copy(ka[0:16, KA_AX:KA_AX + 64], ps[0:16, KA_AX:KA_AX + 64]).then_inc(s["ka_vector"], 1)
    e.wait_ge(s["ka_tensor"], 3)
    psi = ka[0:16, KA_PSI:KA_PSI + 64]
    link(e.tensor_tensor(psi, ps[0:16, KA_PSI:KA_PSI + 64], w("ka_bpsi1"), ALU.add))
    link(e.tensor_tensor(ka[0:16, KA_PHI2:KA_PHI2 + 8], ps[0:16, KA_PHI2:KA_PHI2 + 8], w("ka_bphi2"), ALU.add))
    stats, mv = ka[0:16, KA_STATS:KA_STATS + 24], ka[0:16, KA_STATS + 24:KA_STATS + 32]
    for t in range(4):
        last = e.bn_stats(stats[:, 6 * t:6 * t + 6], psi[:, 16 * t:16 * t + 16])
    link(last)
    for t in range(4):
        last = e.bn_aggr(mv[:, 2 * t:2 * t + 2], stats[:, 6 * t:6 * t + 6])
    link(last)
    var, root = ka[0:16, KA_VAR:KA_VAR + 4], ka[0:16, KA_VAR + 4:KA_VAR + 8]
    e.tensor_scalar(var, mv[:, 1:8:2], LN_EPS, None, ALU.add).then_inc(s["ka_vector"], 1)
    e.wait_ge(s["ka_scalar"], 3)
    link(e.reciprocal(root, root))
    for t in range(4):
        last = e.tensor_scalar(psi[:, 16 * t:16 * t + 16], psi[:, 16 * t:16 * t + 16], mv[:, 2 * t:2 * t + 1],
                               root[:, t:t + 1], ALU.subtract, ALU.mult)
    link(last)
    link(e.tensor_tensor(psi, psi, w("ka_g"), ALU.mult))
    e.tensor_tensor(psi, psi, w("ka_b"), ALU.add).then_inc(s["ka_vector"], 1)
    e.wait_ge(s["ka_tensor"], 4)
    e.tensor_copy(ka[0:16, KA_TURNED:KA_TURNED + 64], ps[0:16, KA_TURNED:KA_TURNED + 64])\
        .then_inc(s["ka_vector"], 1)
    e.wait_ge(s["ka_tensor"], 5)
    psi2, out = ka[0:16, KA_PSI2:KA_PSI2 + 8], ka[0:16, KA_OUT:KA_OUT + 8]
    link(e.tensor_tensor(psi2, ps[0:16, KA_PSI2:KA_PSI2 + 8], w("ka_bpsi2"), ALU.add))
    link(e.tensor_tensor(out, ka[0:16, KA_PHI2:KA_PHI2 + 8], psi2, ALU.mult))
    link(e.tensor_scalar(out, out, w("ka_temp"), None, ALU.mult))
    link(e.tensor_tensor(out, out, w("ka_mix"), ALU.mult))
    e.tensor_scalar(out, out, 1.0, w("gamma"), ALU.add, ALU.mult).then_inc(s["ka_vector"], 1)


def ka_scalar(sub, e):
    co, s, w = sub.core, sub.s, sub.w
    ps, ka = co.ps[:, OUT_BANK, :], co.ka
    e.wait_ge(s["ka_tensor"], 1)
    e.activation(ka[0:16, KA_QK:KA_QK + 16], ps[0:16, 0:16], ACT.Copy).then_inc(s["ka_scalar"], 1)
    e.wait_ge(s["ka_vector"], 2)
    for t in range(4):
        last = e.activation(ka[0:8, KA_PHI + 16 * t:KA_PHI + 16 * t + 16],
                            ps[0:8, KA_PHI + 16 * t:KA_PHI + 16 * t + 16], ACT.Silu,
                            bias=w("ka_bphi1")[:, t:t + 1], scale=1.0)
    last.then_inc(s["ka_scalar"], 1)
    e.wait_ge(s["ka_vector"], 3)
    e.activation(ka[0:16, KA_VAR + 4:KA_VAR + 8], ka[0:16, KA_VAR:KA_VAR + 4], ACT.Sqrt)\
        .then_inc(s["ka_scalar"], 1)
    e.wait_ge(s["ka_vector"], 4)
    e.activation(ka[0:16, KA_PSI:KA_PSI + 64], ka[0:16, KA_PSI:KA_PSI + 64], ACT.Gelu)\
        .then_inc(s["ka_scalar"], 1)


def ka_sync(sub, e):
    co, s = sub.core, sub.s
    e.wait_ge(s["ka_vector"], 6)
    e.dma_start(co.scratch, co.ka[0:16, KA_OUT:KA_OUT + 8]).then_inc(s["ka_moved"], 16)
    e.wait_ge(s["ka_moved"], 16)
    with co.nc.allow_non_contiguous_dma("128 words"):
        e.dma_start(co.scale_o[:, 0:1], co.scratch.rearrange("h (d one) -> (h d) one", one=1)).then_inc(s["ka_moved"], 16)
    e.wait_ge(s["ka_moved"], 32)



def context_stage(core, load_next, number, x_in, ctx_in, mask_in, vec_in, b):
    s = core.sets[number % 2]
    sm = core.small

    with core.nc.Block() as block:

        @block.sync
        def _(sp):
            one = lambda a: a[bass.ds(b, 1)].rearrange("o p c -> (o p) c")
            sp.dma_start(core.ctx_rows[0:NC, :], one(ctx_in)).then_inc(core.x_loaded, 16)
            sp.dma_start(core.x[:, :, :].rearrange("p i d -> p (i d)"), one(x_in)).then_inc(core.x_loaded, 16)
            sp.dma_start(core.mask_rows[:, :].bitcast(I32), one(mask_in)).then_inc(core.x_loaded, 16)
            sp.dma_start(core.mask_vec[:, 0:NC], one(vec_in)).then_inc(core.x_loaded, 16)
            load_next(sp)

        @block.vector
        def _(dve):
            link = chained(dve, s["step_v"])
            dve.wait_ge(core.x_loaded, 64)
            rows, stats, mv = core.ctx_rows[0:NC, :], core.stats[0:NC, 0, :], core.mv[0:NC, 0, :]
            link(dve.bn_stats(stats, rows))
            link(dve.bn_aggr(mv, stats))
            dve.tensor_scalar(sm[0:NC, 0, 0:1], mv[:, 1:2], LN_EPS, None, ALU.add).then_inc(s["variance"], 1)
            dve.wait_ge(s["deviation"], 1)
            link(dve.reciprocal(sm[0:NC, 2, 0:1], sm[0:NC, 1, 0:1]))
            dve.tensor_scalar(core.ctx_n[0:NC, :], rows, mv[:, 0:1], sm[0:NC, 2, 0:1], ALU.subtract, ALU.mult)\
                .then_inc(s["normed"], 1)

        @block.scalar
        def _(act):
            act.wait_ge(s["variance"], 1)
            act.activation(sm[0:NC, 1, 0:1], sm[0:NC, 0, 0:1], ACT.Sqrt).then_inc(s["deviation"], 1)
            act.wait_ge(s["turned"], 1)
            act.activation(core.ctx_raw_t[:, 0:NC], core.ps[:, TURN_BANK, 0:NC], ACT.Copy)
            act.activation(core.ctx_norm_t[:, 0:NC], core.ps[:, TURN_BANK, 128:128 + NC], ACT.Copy)

        @block.tensor
        def _(pe):
            pe.wait_ge(core.x_loaded, 64)
            pe.wait_ge(s["normed"], 1)
            eye = core.c("identity")[0:NC, 0:NC]
            pe.transpose(core.ps[:, TURN_BANK, 0:NC], core.ctx_rows[0:NC, :], eye)
            pe.transpose(core.ps[:, TURN_BANK, 128:128 + NC], core.ctx_n[0:NC, :], eye).then_inc(s["turned"], 1)


class Experts:

    def __init__(self, sub, kind, experts, hidden, up, gate, down, b1=None, b2=None, routed=0, top=None):
        self.sub, self.kind, self.experts, self.up, self.gate, self.down = sub, kind, experts, up, gate, down
        self.chunks = [min(128, hidden - at) for at in range(0, hidden, 128)]
        self.hidden, self.b1, self.b2, self.routed, self.top = hidden, b1, b2, routed, top
        co = sub.core
        self.row = 24
        area = co.ka[:, 0:NT * 24 * 4].rearrange("p (a i c) -> p a i c", a=4, i=NT)
        self.exps, self.replaced, self.gates, self.misc = area[:, 0], area[:, 1], area[:, 2], area[:, 3]

    def route_tensor(self, e):
        co, s, w = self.sub.core, self.sub.s, self.sub.w
        for i in range(NT):
            out = co.ps[:, OUT_BANK, 32 * i:32 * i + self.routed]
            biased = "router_b" in self.sub.at
            last = e.matmul(out, co.xt[:, i * 128:i * 128 + 128], w("router"), start=True, stop=not biased,
                            skip_group_check=True)
            if biased:
                last = e.matmul(out, co.c("ones")[:, 0:128], w("router_b"), start=False, stop=True,
                                skip_group_check=True)
        last.then_inc(s["logits"], 1)

    def turn_gates_tensor(self, e):
        co, s = self.sub.core, self.sub.s
        e.wait_ge(s["gates"], 1)
        for i in range(NT):
            last = e.transpose(co.ps[0:self.experts, TURN_BANK, i * 128:i * 128 + 128],
                               self.gates[:, i, 0:self.experts], co.c("identity"))
        last.then_inc(s["gates_turned"], 1)

    def route_vector(self, e, link):
        co, s = self.sub.core, self.sub.s
        r, k = self.routed, self.top
        low, total, tops = self.misc[:, :, 0:1], self.misc[:, :, 1:2], self.misc[:, :, 8:16]
        e.memset(self.exps[:, :, r:self.row], -1.0)
        link(e.memset(self.misc[:, :, 0:self.row], -1.0))
        e.wait_ge(s["logits"], 1)
        logits = co.ps[:, OUT_BANK, 0:NT * 32].rearrange("p (i c) -> p i c", i=NT)[:, :, 0:r]
        e.tensor_reduce(low[:, :, 0], logits, AX.X, ALU.max, negate=True).then_inc(s["shifted"], 1)
        e.wait_ge(s["exps"], 1)
        for i in range(NT):
            last = e.max(tops[:, i, :], self.exps[:, i, 0:r])
        link(last)
        link(e.memset(tops[:, :, k:8], -1.0))
        link(e.reciprocal(total[:, :, 0], total[:, :, 0]))
        for i in range(NT):
            last = e.match_replace(self.replaced[:, i, 0:r + 8 - k], tops[:, i, :],
                                   self.exps[:, i, 0:r + 8 - k], -2.0)
        link(last)
        for i in range(NT):
            last = e.scalar_tensor_tensor(out=self.gates[:, i, 0:r], in0=self.replaced[:, i, 0:r], scalar=-1.5,
                                          in1=self.exps[:, i, 0:r], op0=ALU.is_lt, op1=ALU.mult)
        link(last)
        if self.experts > r:
            e.memset(self.gates[:, :, r:self.experts], 1.0)
        for i in range(NT):
            last = e.tensor_scalar(self.gates[:, i, 0:r], self.gates[:, i, 0:r], total[:, i, :], None, ALU.mult)
        last.then_inc(s["gates"], 1)

    def route_scalar(self, e):
        co, s = self.sub.core, self.sub.s
        e.wait_ge(s["shifted"], 1)
        for i in range(NT):
            last = e.activation(self.exps[:, i, 0:self.routed], co.ps[:, OUT_BANK, 32 * i:32 * i + self.routed],
                                ACT.Exp, bias=self.misc[:, i, 0:1], scale=1.0, accum_out=self.misc[:, i, 1:2])
        last.then_inc(s["exps"], 1)

    def pairs(self):
        return [(x, c) for x in range(self.experts) for c in range(len(self.chunks))]

    def hidden_tile(self, x, c):
        at = ((x % 2) * len(self.chunks) + c) * N
        return self.sub.core.o[0:self.chunks[c], at:at + N]

    def tensor(self, e):
        co, s, w = self.sub.core, self.sub.s, self.sub.w
        n = len(self.chunks)
        e.wait_ge(s["features"], 1)
        if self.top is not None:
            self.route_tensor(e)

        def up(x):
            for c, m in enumerate(self.chunks):
                job = x * n + c
                if job >= 2:
                    e.wait_ge(s["hidden"], job - 1)
                cols = slice(x * self.hidden + 128 * c, x * self.hidden + 128 * c + m)
                for b, weights in enumerate((self.up, self.gate) if self.gate is not None else (self.up,)):
                    last = e.matmul(co.ps[0:m, 2 * (job % 2) + b, :], weights[:, cols], co.xt[:, :],
                                    start=True, stop=True)
                last.then_inc(s["up"], 1)

        up(0)
        if self.b2 is not None:
            self.turn_gates_tensor(e)
            e.wait_ge(s["gates_kept"], 1)
            for i in range(NT):
                last = e.matmul(co.ps[:, OUT_BANK, i * 128:i * 128 + 128],
                                co.tmp[0:self.experts, 0, i * 128:i * 128 + 128], self.b2, start=True,
                                stop=True, skip_group_check=True)
            last.then_inc(s["out"], 1)
        for x in range(self.experts):
            if x + 1 < self.experts:
                up(x + 1)
            e.wait_ge(s["hidden"], (x + 1) * n)
            if x >= 2:
                e.wait_ge(s["summed"], (x - 1) * NT)
            for i in range(NT):
                for c in range(n):
                    last = e.matmul(co.ps[:, 4 + x % 2, i * 128:i * 128 + 128],
                                    self.hidden_tile(x, c)[:, i * 128:i * 128 + 128],
                                    self.down[0:self.chunks[c], (x * n + c) * 128:(x * n + c) * 128 + 128],
                                    start=c == 0, stop=c == n - 1, skip_group_check=True)
            last.then_inc(s["down"], 1)

    def scalar(self, e):
        co, s = self.sub.core, self.sub.s
        if self.top is not None:
            self.route_scalar(e)
        for job, (x, c) in enumerate(self.pairs()):
            m = self.chunks[c]
            e.wait_ge(s["up"], job + 1)
            if self.kind == "relu":
                if x >= 2:
                    e.wait_ge(s["down"], x - 1)
                e.activation(self.hidden_tile(x, c), co.ps[0:m, 2 * (job % 2), :], ACT.Relu,
                             bias=self.b1[:, x:x + 1], scale=1.0).then_inc(s["hidden"], 1)
                if x == 0 and self.b2 is not None:
                    e.wait_ge(s["gates_turned"], 1)
                    e.activation(co.tmp[0:self.experts, 0, :], co.ps[0:self.experts, TURN_BANK, :], ACT.Copy)\
                        .then_inc(s["gates_kept"], 1)
            else:
                if job >= 2:
                    e.wait_ge(s["hidden"], job - 1)
                e.activation(co.tmp[0:m, job % 2, :], co.ps[0:m, 2 * (job % 2) + 1, :], ACT.Silu)\
                    .then_inc(s["relu"], 1)

    def vector(self, e, link):
        co, s = self.sub.core, self.sub.s
        if self.top is not None:
            self.route_vector(e, link)
        if self.b2 is not None:
            e.wait_ge(s["out"], 1)
            flat = co.x[:, :, :].rearrange("p i d -> p (i d)")
            link(e.tensor_tensor(flat, flat, co.ps[:, OUT_BANK, :], ALU.add))
        n = len(self.chunks)

        def hidden(x):
            for c, m in enumerate(self.chunks):
                job = x * n + c
                e.wait_ge(s["relu"], job + 1)
                if x >= 2:
                    e.wait_ge(s["down"], x - 1)
                e.tensor_tensor(self.hidden_tile(x, c), co.tmp[0:m, job % 2, :],
                                co.ps[0:m, 2 * (job % 2), :], ALU.mult).then_inc(s["hidden"], 1)

        if self.kind == "silu":
            hidden(0)
        for x in range(self.experts):
            if self.kind == "silu" and x + 1 < self.experts:
                hidden(x + 1)
            e.wait_ge(s["down"], x + 1)
            if x >= 1:
                e.wait_ge(s["summed"], x * NT)
            for i in range(NT):
                out = co.ps[:, 4 + x % 2, i * 128:i * 128 + 128]
                if self.top is None:
                    ins = e.tensor_tensor(co.x[:, i, :], co.x[:, i, :], out, ALU.add)
                else:
                    ins = e.scalar_tensor_tensor(out=co.x[:, i, :], in0=out, scalar=self.gates[:, i, x:x + 1],
                                                 in1=co.x[:, i, :], op0=ALU.mult, op1=ALU.add)
                ins.then_inc(s["summed"], 1)
        e.wait_ge(s["summed"], self.experts * NT)


def experts_sublayer(core, load_next, clear, key, number):
    sub = Sublayer(core, key, number)
    s, w = sub.s, sub.w
    nm = Norm(sub)
    if key == "L0_ffn":
        ex = Experts(sub, "relu", 16, 128, w("w1"), None, w("w2"), b1=w("b1"), b2=w("b2"), routed=15, top=3)
    elif key == "L3_ffn":
        gate = core.gate_up[:, 0:8 * 352]
        up = core.gate_up[:, 8 * 352:16 * 352]
        ex = Experts(sub, "silu", 8, 352, up, gate, w("down"), routed=8, top=2)
    else:
        at = sub.at
        real = lambda n: core.converted[:, at[n][0]:at[n][0] + at[n][1]]
        ex = Experts(sub, "silu", 1, 384, real("up"), real("gate"), real("down"))
    whole = key == "L3_ffn"

    with core.nc.Block() as block:

        @block.sync
        def _(sp):
            load_next(sp)

        @block.gpsimd
        def _(pool):
            clear(pool)

        @block.vector
        def _(dve):
            link = chained(dve, s["step_v"])
            dve.wait_ge(core.loaded[key], 16)
            if key == "L1_ffn":
                n = sum(wide for _, wide, _ in sub.at.values())
                dve.tensor_scalar(core.converted[:, 0:n], sub.slot[:, 0:n].bitcast(I32), 1.0 / 127.0, None, ALU.mult)\
                    .then_inc(s["converted"], 1)
            nm.vector(dve, link)
            ex.vector(dve, link)

        @block.scalar
        def _(act):
            act.wait_ge(core.loaded[key], 16)
            nm.scalar(act)
            ex.scalar(act)

        @block.tensor
        def _(pe):
            pe.wait_ge(core.loaded[key], 16)
            if whole:
                pe.wait_ge(core.loaded["L3_ffn_gate_up"], 16)
            nm.tensor(pe)
            if key == "L1_ffn":
                pe.wait_ge(s["converted"], 1)
            ex.tensor(pe)


def fourier_sublayer(core, load_next, clear, key, number):
    sub = Sublayer(core, key, number)
    s, w = sub.s, sub.w
    nm = Norm(sub)
    at_real, at_imag, mat = core.tmp[:, 0, 0:128], core.tmp[:, 0, 128:256], core.tmp[:, 0, 256:384]

    with core.nc.Block() as block:

        @block.sync
        def _(sp):
            load_next(sp)

        @block.gpsimd
        def _(pool):
            clear(pool)

        @block.vector
        def _(dve):
            link = chained(dve, s["step_v"])
            nm.vector(dve, link)
            dve.wait_ge(s["up"], 1)
            dve.tensor_copy(core.tmp[:, 0, 0:256], core.ps[:, 0, 0:256]).then_inc(s["hidden"], 1)
            dve.wait_ge(s["up"], 2)
            dve.tensor_scalar(mat, core.ps[:, 1, 0:128], 1.0 / 128, None, ALU.mult).then_inc(s["hidden"], 1)
            dve.wait_ge(s["out"], 1)
            flat = core.x[:, :, :].rearrange("p i d -> p (i d)")
            link(dve.tensor_tensor(flat, flat, core.ps[:, OUT_BANK, :], ALU.add))

        @block.scalar
        def _(act):
            nm.scalar(act)

        @block.tensor
        def _(pe):
            pe.wait_ge(core.loaded[key], 16)
            group = dict(skip_group_check=True)
            pe.matmul(core.ps[:, 0, 0:128], w("real"), core.c("dft_cos"), start=True, stop=False, **group)
            pe.matmul(core.ps[:, 0, 0:128], w("imag"), core.c("dft_sin"), start=False, stop=True, **group)
            pe.matmul(core.ps[:, 0, 128:256], w("imag"), core.c("dft_cos"), start=True, stop=False, **group)
            pe.matmul(core.ps[:, 0, 128:256], w("real"), core.c("dft_minus_sin"), start=False, stop=True,
                      **group).then_inc(s["up"], 1)
            nm.tensor(pe)
            pe.wait_ge(s["hidden"], 1)
            pe.matmul(core.ps[:, 1, 0:128], at_real, core.c("dft_cos"), start=True, stop=False, **group)
            pe.matmul(core.ps[:, 1, 0:128], at_imag, core.c("dft_minus_sin"), start=False, stop=True, **group)\
                .then_inc(s["up"], 1)
            pe.wait_ge(s["hidden"], 2)
            pe.wait_ge(s["features"], 1)
            for i in range(NT):
                out = core.ps[:, OUT_BANK, i * 128:i * 128 + 128]
                pe.matmul(out, core.xt[:, i * 128:i * 128 + 128], mat, start=True, stop=False, **group)
                last = pe.matmul(out, core.c("ones")[:, 0:128], w("bo"), start=False, stop=True, **group)
            last.then_inc(s["out"], 1)



SUBLAYERS = [
    ("L0_attn", 0, dict(wide=False, pattern="causal", scale=8 ** -0.5, alibi=True, norm={})),
    ("L0_xattn", 1, dict(wide=False, own=False, ctx=True, scale=8 ** -0.5, relu=True, norm={})),
    ("L0_ffn", 2, None),
    ("L1_attn", 3, dict(wide=False, alpha=True, value_scale=True, norm={})),
    ("L1_xattn", 4, dict(wide=True, ctx=True, scale=1 / 8, norm=dict(again=LN_EPS))),
    ("L1_ffn", 5, None),
    ("L2_attn_g", 6, dict(wide=False, pattern="causal", scale=8 ** -0.5, grouped=True, rope=True, latent=True,
                          norm=dict(again=RMS_EPS), keep_h=True)),
    ("L2_attn_l", 6, dict(wide=False, pattern="local", scale=8 ** -0.5, grouped=True, rope=True,
                          norm=dict(kind="rms"), add_h=True)),
    ("L2_xattn", 7, dict(wide=True, heads=8, ctx=True, scale=1 / 8, ctx_rope=True, norm=dict(again=LN_EPS))),
    ("L2_ffn", 8, None),
    ("L3_attn", 9, dict(wide=True, pattern="causal", scale=1 / 8, norm=dict(again=LN_EPS))),
    ("L3_xattn", 10, dict(wide=False, own=False, ctx=True, scale=8 ** -0.5, ctx_mask=True, norm={})),
    ("L3_ffn", 11, None),
]


def build(nc, dram, layouts, out, scratch):
    with ExitStack() as ctx:
        core = Core(nc, ctx, dram, layouts)
        core.scratch = scratch
        todo = [x for x in SUBLAYERS if STAGES[0] <= x[1] <= STAGES[1]]

        with nc.Block() as block:

            @block.sync
            def _(sp):
                sp.dma_start(core.consts[:, :], dram["consts"]).then_inc(core.consts_loaded, 16)
                sp.dma_start(core.o[:, 0:masks().width], dram["masks"]).then_inc(core.consts_loaded, 16)

            @block.gpsimd
            def _(pool):
                pool.memset(core.guard_thin[:, :, :, :], 0.0)
                pool.memset(core.guard_wide[:, :, :, :], 0.0)
                for context in (core.ctx_raw_t, core.ctx_t, core.ctx_rotated):
                    pool.memset(context[:, 64:128], 0.0)
                pool.memset(core.mask_vec[:, 64:128], 0.0)

            @block.vector
            def _(dve):
                dve.wait_ge(core.consts_loaded, 32)
                dve.tensor_copy(core.identity_b[:, :], core.c("identity"))
                for name, mask in core.masks_b.items():
                    at, wide, _ = core.mask_at[name]
                    dve.tensor_copy(mask[:, :], core.o[:, at:at + wide])

        def loader(n):
            def load(sp):
                if n >= len(todo):
                    return
                key = todo[n][0]
                wide = sum(cols for _, cols, _ in layouts[key].values())
                slot = core.slot[(n + 1) % 2][:, 0:wide]
                sp.dma_start(slot.bitcast(I32) if key == "L1_ffn" else slot, dram[key])\
                    .then_inc(core.loaded[key], 16)
                if key == "L3_ffn":
                    sp.dma_start(core.gate_up[:, :], dram["L3_ffn_gate_up"])\
                        .then_inc(core.loaded["L3_ffn_gate_up"], 16)
            return load

        def clearer(number):
            def clear(pool):
                nums = [x.num for x in core.sets[(number + 1) % 2].values()]
                assert nums == list(range(nums[0], nums[-1] + 1))
                pool.sem_clear(range(nums[0], nums[-1] + 1))
            return clear

        with nc.Fori(0, BATCHES) as b:
            context_stage(core, loader(0), 0, dram["x"], dram["ctx"], dram["mask"], dram["mask_vec"], b)
            room = ExitStack()
            for n, (key, _, kinds) in enumerate(todo):
                number = n + 1
                args = (core, loader(n + 1), clearer(number), key, number)
                if n == 0 or key != "L3_ffn":
                    room.close()
                    use = "thin" if key == "L3_ffn" else "plain" if not kinds else "wide" if kinds["wide"] else "thin"
                    room.enter_context(core.operands(use, number))
                if kinds is not None:
                    attention_sublayer(*args, **kinds)
                elif key == "L2_ffn":
                    fourier_sublayer(*args)
                else:
                    experts_sublayer(*args)
            room.close()
            with nc.Block() as block:

                @block.sync
                def _(sp):
                    sp.dma_start(out[bass.ds(b, 1)].rearrange("o p c -> (o p) c"),
                                 core.x[:, :, :].rearrange("p i d -> p (i d)")).then_inc(core.x_loaded, 16)
                    sp.wait_ge(core.x_loaded, 80)
            nums = sorted(x.num for x in core.loop_sems)
            assert nums == list(range(nums[0], nums[-1] + 1))
            nc.gpsimd.sem_clear(range(nums[0], nums[-1] + 1))
            nc.all_engine_barrier()


def kernel(**inputs):
    import concourse.bacc as _bacc
    from concourse.bass_utils import run_bass_kernel_spmd as _run

    nc = _bacc.Bacc("TRN2", target_bir_lowering=False, num_devices=1)
    tiles = lambda a: np.ascontiguousarray(a.reshape(B, NT, 128, -1).transpose(0, 2, 1, 3).reshape(B, 128, -1))
    x = np.asarray(inputs["x"] if X_OVERRIDE is None else X_OVERRIDE)
    arrays = {
        "x": tiles(x),
        "ctx": np.ascontiguousarray(inputs["ctx_1024"]),
        "mask": tiles(np.asarray(inputs["mask_BxSxS2_bk1"]).view(np.uint8)).view(np.int32),
        "mask_vec": np.ascontiguousarray(np.asarray(inputs["mask_Bx1x1xS2_fk0"]).reshape(B, 1, NC)),
        "consts": constants().array(),
        "masks": masks().array(),
    }
    layouts = {}
    for key, pack in packs(inputs).items():
        arrays[key] = pack.array()
        layouts[key] = pack.at
    dram = {k: nc.dram_tensor(f"in_{k}", a.shape, mybir.dt.from_np(a.dtype), kind="ExternalInput").ap()
            for k, a in arrays.items()}
    out = nc.dram_tensor("out_x", (B, 128, NT * D), F32, kind="ExternalOutput").ap()
    scratch = nc.dram_tensor("scratch", (16, 8), F32, kind="Internal").ap()
    build(nc, dram, layouts, out, scratch)
    r = _run(nc, [{f"in_{k}": a for k, a in arrays.items()}], core_ids=[0])
    y = np.asarray(r.results[0]["out_x"])
    return np.ascontiguousarray(y.reshape(B, 128, NT, D).transpose(0, 2, 1, 3).reshape(B, N, D))
```

```python
from contextlib import ExitStack, contextmanager

import numpy as np

import concourse.bass as bass
from concourse import mybir

F32 = mybir.dt.float32
F32R = mybir.dt.float32r
BF16 = mybir.dt.bfloat16
I32 = mybir.dt.int32
U8 = mybir.dt.uint8
ALU = mybir.AluOpType
ACT = mybir.ActivationFunctionType
AX = mybir.AxisListType

B, N, D = 4, 512, 128
NC = 77
NT = N // 128
HEADS = 16
STRIP = 32
BANK = 512
COPIES = 3
MAX_ROW, BY_KEY, BY_QUERY, MASKED = 24, 25, 27, 29
NEG = -1e30
LN_EPS = 1e-5
RMS_EPS = 1e-6


PLAIN = [4 * c + s for c in range(4) for s in range(4)]
GROUPED = [4 * s + c for c in range(4) for s in range(4)]


class Pack:

    def __init__(self):
        self.at, self.width, self.parts = {}, 0, []

    def add(self, name, a):
        a = np.asarray(a)
        a = a.reshape(a.shape[0], -1)
        self.at[name] = (self.width, a.shape[1], a.shape[0])
        self.width += a.shape[1]
        self.parts.append(a)

    def array(self):
        out = np.zeros((128, self.width), self.parts[0].dtype)
        for (col, wide, rows), a in zip(self.at.values(), self.parts):
            out[:rows, col:col + wide] = a
        return out


def strips(w, order, extra=None):
    rows = w.shape[0]
    out = np.zeros((rows, len(order), STRIP), w.dtype)
    for n in range(COPIES):
        out[:, :, 8 * n:8 * n + 8] = w.reshape(rows, -1, 8)[:, order, :]
    for feature, v in (extra or {}).items():
        out[:, :, feature] = v[:, order]
    return out.reshape(rows, -1)


def split_columns():
    a, b, bias = np.zeros((4, STRIP), np.float32), np.ones((4, STRIP), np.float32), np.zeros((4, STRIP), np.float32)
    for f in (slice(8, 16), MASKED + 1):
        a[:, f], b[:, f] = 1, -1
    for f in (MAX_ROW, BY_QUERY, BY_QUERY + 1):
        bias[:, f] = 1
    return [v.reshape(128, 1) for v in (a, b, bias)]


def halves(v):
    v = np.asarray(v, np.float32)
    high = (v.view(np.uint32) & np.uint32(0xFFFFF000)).view(np.float32)
    return high, v - high


def rows_by_chunk(a):
    out = np.zeros((4, 32, a.shape[1] // 4), np.float32)
    out[:, 0:a.shape[0]] = a.reshape(a.shape[0], 4, -1).transpose(1, 0, 2)
    return out.reshape(128, -1)


def spreading():
    p = Pack()
    for name, copies in (("q_high", (0, 8)), ("q_low", (16,)), ("k_high", (0, 16)), ("k_low", (8,))):
        m = np.zeros((4, 4, 8, 4, STRIP), np.float32)
        for s in range(4):
            for d in range(8):
                for at in copies:
                    m[:, s, d, s, at + d] = 1
        p.add("spread_" + name, m.reshape(128, 128))
    high, low = halves(alibi_slopes() * np.float32(np.sqrt(8.0)))
    add = {n: np.zeros((2, HEADS, STRIP), np.float32) for n in ("q_alibi", "k_alibi", "q", "k")}
    add["q_alibi"][0, :, BY_KEY], add["q_alibi"][0, :, BY_KEY + 1] = -high, -low
    add["q_alibi"][1, :, BY_QUERY:BY_QUERY + 2] = 1
    add["k_alibi"][1, :, BY_KEY:BY_KEY + 2] = 1
    add["k_alibi"][0, :, BY_QUERY], add["k_alibi"][0, :, BY_QUERY + 1] = high, low
    add["q"][0, :, MASKED:MASKED + 2] = 1
    add["k"][0, :, BY_QUERY:BY_QUERY + 2] = 1
    for side in ("k_alibi", "k"):
        add[side][0, :, MAX_ROW] = 1
    for name, a in add.items():
        p.add("add_" + name, rows_by_chunk(a.reshape(2, -1)))
    p.add("one_and_position", rows_by_chunk(np.tile(np.stack([np.ones(N), np.arange(N)]).astype(np.float32), 4)))
    return p


def by_head(w, order):
    return w.reshape(w.shape[0], -1, 8)[:, order, :].reshape(w.shape[0], -1)


def swap_pairs(w):
    return w.reshape(w.shape[0], -1, 2)[:, :, ::-1].reshape(w.shape[0], -1)


def chunks_of_rows(w):
    n = w.shape[0] // 128
    return w.reshape(n, 128, -1).transpose(1, 0, 2).reshape(128, -1)


def row(v):
    return np.asarray(v, np.float32).reshape(1, -1)


def col(v):
    return np.asarray(v, np.float32).reshape(-1, 1)


def rope_tables(base):
    inv = (1.0 / np.float32(base) ** (np.arange(0, 8, 2, dtype=np.float32) / np.float32(8))).astype(np.float32)
    f = np.arange(N, dtype=np.float32)[:, None] * inv[None, :]
    cos, sin = np.cos(f), np.sin(f)
    c, s = np.zeros((16, 8, N), np.float32), np.zeros((16, 8, N), np.float32)
    for d in range(8):
        c[:, d] = cos[:, d // 2]
        s[:, d] = sin[:, d // 2] * (-1.0 if d % 2 == 0 else 1.0)
    return c.reshape(128, N), s.reshape(128, N)


def context_rope_tables():
    half = 32
    inv = (1.0 / np.float32(10000.0) ** (np.arange(0, 64, 2, dtype=np.float32) / np.float32(64))).astype(np.float32)
    theta = np.arange(NC, dtype=np.float32)[:, None] * inv[None, :]
    c = np.concatenate([np.cos(theta)] * 2, 1).T
    s = np.concatenate([-np.sin(theta), np.sin(theta)], 1).T
    assert c.shape[0] == 2 * half
    return np.concatenate([c, c], 0), np.concatenate([s, s], 0)


def alibi_slopes():
    start = 2 ** (-2 ** (-(np.log2(HEADS) - 3)))
    return np.array([start * start ** i for i in range(HEADS)], np.float32)


def masks():
    p = Pack()
    i = np.arange(128)
    p.add("causal", np.where(i[None, :] <= i[:, None], 0, NEG).astype(np.float32))
    p.add("causal_t", np.where(i[None, :] >= i[:, None], 0, NEG).astype(np.float32))
    wide = np.arange(128 + STRIP)
    gap = i[:, None] + 32 - wide[None, :]
    p.add("local", np.where((gap >= 0) & (gap < 32), 0, NEG).astype(np.float32))
    gap = wide[None, :] - i[:, None]
    p.add("local_t", np.where((gap >= 0) & (gap < 32), 0, NEG).astype(np.float32))
    return p


def constants():
    p = Pack()
    i = np.arange(128)
    p.add("identity", np.eye(128, dtype=np.float32))
    p.add("head_mean", np.where(i[:, None] // 8 == i[None, :] // 8, 1 / 8, 0).astype(np.float32))
    p.add("rms_eps", np.full((128, 1), RMS_EPS, np.float32))
    p.add("ones", np.ones((1, N), np.float32))
    for part, v in zip(("a", "b", "bias"), split_columns()):
        p.add("k_" + part, v)
    m = np.zeros((1, 4, STRIP), np.float32)
    m[:, :, MASKED:MASKED + 2] = -1e9 * np.sqrt(8.0)
    p.add("mask_row", m.reshape(1, -1))
    a = 2 * np.pi * ((i[:, None] * i[None, :]) % 128) / 128
    p.add("dft_cos", np.cos(a).astype(np.float32))
    p.add("dft_sin", np.sin(a).astype(np.float32))
    p.add("dft_minus_sin", -np.sin(a).astype(np.float32))
    return p


def packs(w):
    f = {k: np.asarray(v) for k, v in w.items()}
    out = {}

    p = out["L0_attn"] = Pack()
    p.add("wq", f["L0_attn_Wq"])
    p.add("wk", f["L0_attn_Wk"])
    p.add("wv", f["L0_attn_Wv"])
    p.add("wo", f["L0_attn_Wo"])
    p.add("bq", col(f["L0_attn_bq"]))
    p.add("bk", col(f["L0_attn_bk"]))
    p.add("bv", row(f["L0_attn_bv"]))
    p.add("bo", row(f["L0_attn_bo"]))

    p = out["L0_xattn"] = Pack()
    p.add("wq", f["L0_xattn_Wq"].T)
    p.add("wk", strips(f["L0_xattn_Wk"].T, PLAIN))
    p.add("wv", f["L0_xattn_Wv"].T)
    p.add("wo", f["L0_xattn_Wo"].T)
    p.add("sn_bias", np.broadcast_to(f["L0_xattn_sn_bias"].reshape(1, 1), (128, 1)))

    p = out["L0_ffn"] = Pack()
    p.add("w1", np.concatenate([f["L0_ffn_eW1"], f["L0_ffn_sW1"][None]]).transpose(1, 0, 2))
    p.add("w2", np.concatenate([f["L0_ffn_eW2"], f["L0_ffn_sW2"][None]]).transpose(1, 0, 2))
    p.add("b1", np.concatenate([f["L0_ffn_eb1"], f["L0_ffn_sb1"][None]]).T)
    p.add("b2", np.concatenate([f["L0_ffn_eb2"], f["L0_ffn_sb2"][None]]))
    p.add("router", f["L0_ffn_router_W"])
    p.add("router_b", row(f["L0_ffn_router_b"]))

    p = out["L1_attn"] = Pack()
    wqkv = f["L1_attn_Wqkv"]
    p.add("wq", wqkv[:, 0:128])
    p.add("wk", wqkv[:, 128:256])
    p.add("wv", wqkv[:, 256:384])
    p.add("wo", f["L1_attn_Wproj"])
    p.add("bo", row(f["L1_attn_bproj"]))
    p.add("alpha", col(np.repeat(f["L1_attn_alpha"], 8)))
    nothing, beta = np.zeros((1, 128), np.float32), row(f["L1_attn_beta"])
    p.add("beta_high", rows_by_chunk(strips(nothing, PLAIN, {BY_QUERY: beta})))
    p.add("beta_low", rows_by_chunk(strips(nothing, PLAIN, {BY_QUERY + 1: beta})))
    p.add("wqk_mean", wqkv[:, 0:256].reshape(128, 2, 16, 8).transpose(0, 2, 1, 3))
    p.add("ka_a", f["L1_attn_A"].transpose(1, 0, 2))
    p.add("ka_phi1", f["L1_attn_Wphi1"].transpose(1, 0, 2))
    p.add("ka_bphi1", f["L1_attn_bphi1"].T)
    p.add("ka_phi2", f["L1_attn_Wphi2"].transpose(1, 0, 2))
    p.add("ka_psi1", f["L1_attn_Wpsi1"].transpose(1, 0, 2))
    p.add("ka_psi2", f["L1_attn_Wpsi2"].transpose(1, 0, 2))
    over_heads = lambda a: np.broadcast_to(np.asarray(a).reshape(1, -1), (16, np.asarray(a).size))
    p.add("ka_bpsi1", over_heads(f["L1_attn_bpsi1"]))
    p.add("ka_g", over_heads(f["L1_attn_ln_g"]))
    p.add("ka_b", over_heads(f["L1_attn_ln_b"]))
    p.add("ka_bphi2", over_heads(f["L1_attn_bphi2"]))
    p.add("ka_bpsi2", over_heads(f["L1_attn_bpsi2"]))
    p.add("ka_mix", over_heads(np.repeat(f["L1_attn_mixing"], 2)))
    p.add("ka_temp", over_heads(f["L1_attn_temp_scale"]))
    p.add("gamma", f["L1_attn_gamma"].reshape(16, 1))

    p = out["L1_xattn"] = Pack()
    p.add("wq", f["L1_xattn_Wq"])
    p.add("wk", f["L1_xattn_Wkv"][:, 0:1024])
    p.add("wv", f["L1_xattn_Wkv"][:, 1024:2048])
    p.add("wo", chunks_of_rows(f["L1_xattn_Wo"]))
    p.add("g_ctx", col(f["L1_xattn_ln1_g"]))
    p.add("b_ctx", col(f["L1_xattn_ln1_b"]))
    p.add("g", col(f["L1_xattn_ln2_g"]))
    p.add("b", col(f["L1_xattn_ln2_b"]))

    p = out["L1_ffn"] = Pack()
    p.add("gate", f["L1_ffn_w_gate"].T)
    p.add("up", f["L1_ffn_w_up"].T)
    p.add("down", chunks_of_rows(f["L1_ffn_w_down"].T))

    for kind, base, key in (("g", 1e6, "L2_attn_g"), ("l", 1e4, "L2_attn_l")):
        p = out[key] = Pack()
        wq = f[f"L2_attn_{kind}_wq"]
        p.add("wq", by_head(wq, GROUPED))
        p.add("wq_swapped", by_head(swap_pairs(wq), GROUPED))
        if kind == "g":
            p.add("down", f["L2_attn_g_kv_down"])
            wk, wv = f["L2_attn_g_k_up"], f["L2_attn_g_v_up"]
        else:
            wk, wv = f["L2_attn_l_wk"], f["L2_attn_l_wv"]
        p.add("wk", wk)
        p.add("wk_swapped", swap_pairs(wk))
        p.add("wv", by_head(wv, [h // 4 for h in GROUPED]))
        p.add("wo", f[f"L2_attn_{kind}_wo"].reshape(16, 8, 128)[GROUPED].reshape(128, 128))
        p.add("g", col(f["L2_attn_norm1_w" if kind == "g" else "L2_attn_norm2_w"]))
        c, s = rope_tables(base)
        p.add("cos", c)
        p.add("sin", s)

    p = out["L2_xattn"] = Pack()
    wk = f["L2_xattn_Wkv"][:, 0:512]
    p.add("wq", f["L2_xattn_Wq"])
    p.add("wk", wk)
    p.add("wk_swapped", wk.reshape(128, 8, 2, 32)[:, :, ::-1, :].reshape(128, 512))
    p.add("wv", f["L2_xattn_Wkv"][:, 512:1024])
    p.add("wo", chunks_of_rows(f["L2_xattn_Wo"]))
    p.add("g_ctx", col(f["L2_xattn_gamma_x"]))
    p.add("b_ctx", col(f["L2_xattn_beta_x"]))
    p.add("g", col(f["L2_xattn_gamma_l"]))
    p.add("b", col(f["L2_xattn_beta_l"]))
    c, s = context_rope_tables()
    p.add("cos", c)
    p.add("sin", s)

    p = out["L2_ffn"] = Pack()
    p.add("real", f["L2_ffn_w_freq_real"])
    p.add("imag", f["L2_ffn_w_freq_imag"])
    p.add("bo", row(f["L2_ffn_bias"]))

    p = out["L3_attn"] = Pack()
    w3 = f["L3_attn_w_qkv"].T
    p.add("wq", w3[:, 0:1024])
    p.add("wk", w3[:, 1024:2048])
    p.add("wv", w3[:, 2048:3072])
    p.add("wo", chunks_of_rows(f["L3_attn_w_out"].T))
    p.add("bo", row(f["L3_attn_b_out"]))
    p.add("g", col(f["L3_attn_ln_gamma"]))
    p.add("b", col(f["L3_attn_ln_beta"]))

    p = out["L3_xattn"] = Pack()
    p.add("wq", f["L3_xattn_Wq"])
    p.add("wk", strips(f["L3_xattn_Wk"], PLAIN))
    p.add("wv", f["L3_xattn_Wv"])
    p.add("wo", f["L3_xattn_Wo"])
    p.add("bq", col(f["L3_xattn_bq"]))
    p.add("k_add", strips(row(f["L3_xattn_bk"]), PLAIN))
    p.add("bv", row(f["L3_xattn_bv"]))
    p.add("bo", row(f["L3_xattn_bo"]))

    p = out["L3_ffn"] = Pack()
    down = np.zeros((8, 384, 128), np.float32)
    down[:, 0:352] = f["L3_ffn_down_w"].transpose(0, 2, 1)
    p.add("down", down.reshape(8, 3, 128, 128).transpose(2, 0, 1, 3))
    p.add("router", f["L3_ffn_router_w"].T)

    p = out["L3_ffn_gate_up"] = Pack()
    p.add("gate", f["L3_ffn_gate_w"].transpose(2, 0, 1))
    p.add("up", f["L3_ffn_up_w"].transpose(2, 0, 1))
    return out



BIG_V, BIG_O = 5 * 16 * 128 + 128, 8 * N
ONES_STEPS = 8
LOCAL = 128 + STRIP
RING, KEYS = 6, N + 128
SLOT = 4288

VALUE_LAG, FINISH_LAG = 2, 0

SCORE_BANK, EXPO_BANK, VALUE_BANK, TURN_BANK, OUT_BANK = 0, 2, 4, 6, 7
OUT_BANKS = (OUT_BANK, TURN_BANK, SCORE_BANK, SCORE_BANK + 1)

SIGNALS = [
    "step_v", "alpha_ready", "beta_split", "rope_in", "variance", "deviation", "normed", "turned", "features", "ctx_ready", "filled", "ones_filled",
    "pair_projected", "ctx_rotated", "high", "low", "copied", "projected", "taken_v", "taken_s", "latent", "latent_kept", "rotated", "squared", "mean_square", "root",
    "divided", "rounded", "operand_ready", "score", "maximum", "guard_ready", "guard_turned", "guarded", "expo", "relu",
    "probs", "valued", "lifted", "finished", "out", "added", "keep_loaded", "keep_turned", "keep_ready",
    "logits", "shifted", "exps", "gates", "gates_turned", "gates_kept", "up", "hidden", "down", "summed",
    "converted", "ka_tensor", "ka_vector", "ka_scalar", "ka_moved",
]


class Core:

    def __init__(self, nc, ctx, dram, layouts):
        self.nc, self.dram, self.layouts = nc, dram, layouts
        self.const_at = constants().at

        def sb(name, shape, dt=F32):
            return ctx.enter_context(nc.sbuf_tensor(name, shape, dt))

        self.consts = sb("consts", [128, constants().width])
        self.x = sb("x", [128, NT, D])
        self.h = sb("h", [128, NT, D])
        self.xn = sb("xn", [128, NT, D])
        self.xt = sb("xt", [128, N])
        self.ctx_rows, self.ctx_n = self.xn[:, 0, :], self.xn[:, 1, :]
        self.ctx_raw_t = sb("ctx_raw_t", [128, 128])
        self.ctx_norm_t = sb("ctx_norm_t", [128, 80])
        self.ctx_t = sb("ctx_t", [128, 128])
        self.mask_rows = sb("mask_rows", [128, NT * NC], U8)
        self.mask_vec = sb("mask_vec", [1, 128])
        self.v = sb("v", [128, BIG_V])
        self.o = sb("o", [128, BIG_O])
        self.slot = [sb("weights_even", [128, SLOT]), sb("weights_odd", [128, SLOT])]
        self.guard_thin = sb("guard_thin", [128, 2, NT, 128])
        self.guard_wide = sb("guard_wide", [128, 2, NT, 65])
        self.ctx_rotated = sb("ctx_rotated", [128, 128])
        self.max_ctx = sb("max_ctx", [128, 2, NT])
        self.p = sb("p", [128, 4, N])
        self.sums = sb("sums", [128, 2, N])
        self.tmp = sb("tmp", [128, 2, N])
        self.keep_rows = self.tmp[:, 0, 0:NT * NC]
        self.stats = sb("stats", [128, NT, 6])
        self.mv = sb("mv", [128, NT, 2])
        self.small = sb("small", [128, 16, NT])
        self.ka = sb("ka", [128, 512])
        self.table_cells = sb("table_cells", [1, 32])
        self.scale_o = sb("scale_o", [128, 2])
        self.identity_b = sb("identity_b", [128, 128], BF16)
        self.spread_at = spreading().at
        self.spreading = sb("spreading", [128, spreading().width], F32R)
        self.mask_at = masks().at
        self.masks_b = {n: sb(n + "_b", [128, wide], BF16) for n, (_, wide, _) in self.mask_at.items()}
        self.ps = ctx.enter_context(nc.psum_tensor("ps", [128, 8, BANK], F32))

        self.sets = [{s: ctx.enter_context(nc.semaphore(f"{s}_{half}")) for s in SIGNALS}
                     for half in ("even", "odd")]
        self.loaded = {k: ctx.enter_context(nc.semaphore(f"loaded_{k}")) for k in layouts}
        self.x_loaded = ctx.enter_context(nc.semaphore("x_loaded"))
        self.consts_loaded = ctx.enter_context(nc.semaphore("consts_loaded"))
        self.consts_made = ctx.enter_context(nc.semaphore("consts_made"))
        self.loop_sems = ([s for half in self.sets for s in half.values()]
                          + list(self.loaded.values()) + [self.x_loaded])

    @contextmanager
    def operands(self, use, number):
        with ExitStack() as ctx:
            def sb(name, wide, dt=F32):
                return ctx.enter_context(self.nc.sbuf_tensor(f"{name}_{number}", [128, wide], dt))

            if use == "thin":
                self.q_parts = sb("q_parts", 4 * N, F32R)
                self.k_parts = sb("k_parts", 4 * N, F32R)
                self.q_guarded = sb("q_guarded", 2 * N, F32R)
                self.parts = {side: (sb(side + "_high", N, F32R), sb(side + "_low", N, F32R)) for side in "qk"}
                self.beta_parts = sb("beta_parts", 2 * 128, F32R)
                self.spare = sb("spare", 3 * N)
                self.gate_up = sb("gate_up", 16 * 352)
            elif use == "wide":
                self.q_high = sb("q_high", RING * N, F32R)
                self.q_low = sb("q_low", RING * N, F32R)
                self.k_both = sb("k_both", RING * KEYS, F32R)
                self.k_high = sb("k_high", RING * KEYS, F32R)
            else:
                self.converted = sb("converted", SLOT)
            yield

    def load_table(self, e, function, cell):
        e.activation(self.table_cells[:, cell:cell + 1], self.c("ones")[:, 0:1], function)

    def spread(self, name):
        at, wide, r = self.spread_at[name]
        return self.spreading[0:r, at:at + wide]

    def c(self, name, rows=None):
        at, wide, r = self.const_at[name]
        return self.consts[0:rows or r, at:at + wide]


class Sublayer:

    def __init__(self, core, key, number):
        self.core, self.key, self.number = core, key, number
        self.s = core.sets[number % 2]
        self.slot = core.slot[number % 2]
        self.at = core.layouts[key]

    def w(self, name):
        at, wide, rows = self.at[name]
        return self.slot[0:rows, at:at + wide]


def chained(eng, sem):
    done = [0]

    def link(ins):
        ins.then_inc(sem, 1)
        done[0] += 1
        eng.wait_ge(sem, done[0])
    return link



class Norm:

    def __init__(self, sub, kind="ln", source=None, again=None, gain=None, offset=None, keep=None,
                 next_table=ACT.Exp):
        self.next_table = next_table
        self.sub, self.kind, self.again, self.keep = sub, kind, again, keep
        self.source = source if source is not None else sub.core.x
        self.gain, self.offset = gain, offset
        self.roots = 2 if again is not None else 1

    def vector(self, e, link):
        co, s, src = self.sub.core, self.sub.s, self.source
        mean, var = co.mv[:, :, 0], co.mv[:, :, 1]
        sm = co.small
        for i in range(NT):
            last = e.bn_stats(co.stats[:, i, :], src[:, i, :])
        link(last)
        for i in range(NT):
            last = e.bn_aggr(co.mv[:, i, :], co.stats[:, i, :])
        link(last)
        if self.kind == "rms":
            link(e.tensor_tensor(sm[:, 4, :], mean, mean, ALU.mult))
            link(e.tensor_tensor(sm[:, 5, :], sm[:, 4, :], var, ALU.add))
            e.tensor_scalar(sm[:, 0, :], sm[:, 5, :], RMS_EPS, None, ALU.add).then_inc(s["variance"], 1)
        else:
            e.tensor_scalar(sm[:, 0, :], var, LN_EPS, None, ALU.add).then_inc(s["variance"], 1)
        e.wait_ge(s["deviation"], 1)
        link(e.reciprocal(sm[:, 2, :], sm[:, 1, :]))
        scale = sm[:, 2, :]
        if self.again is not None:
            link(e.tensor_tensor(sm[:, 3, :], var, scale, ALU.mult))
            link(e.tensor_tensor(sm[:, 4, :], sm[:, 3, :], scale, ALU.mult))
            e.tensor_scalar(sm[:, 0, :], sm[:, 4, :], self.again, None, ALU.add).then_inc(s["variance"], 1)
            e.wait_ge(s["deviation"], 2)
            link(e.reciprocal(sm[:, 5, :], sm[:, 1, :]))
            link(e.tensor_tensor(sm[:, 6, :], sm[:, 5, :], scale, ALU.mult))
            if self.keep is not None:
                for i in range(NT):
                    e.tensor_scalar(self.keep[:, i, :], src[:, i, :], mean[:, i:i + 1], scale[:, i:i + 1],
                                    ALU.subtract, ALU.mult)
            scale = sm[:, 6, :]
        for i in range(NT):
            if self.kind == "rms":
                ins = e.tensor_scalar(co.xn[:, i, :], src[:, i, :], scale[:, i:i + 1], None, ALU.mult)
            else:
                ins = e.tensor_scalar(co.xn[:, i, :], src[:, i, :], mean[:, i:i + 1], scale[:, i:i + 1],
                                      ALU.subtract, ALU.mult)
            ins.then_inc(s["normed"], 1)

    def scalar(self, e):
        co, s, sm = self.sub.core, self.sub.s, self.sub.core.small
        for n in range(self.roots):
            e.wait_ge(s["variance"], n + 1)
            e.activation(sm[:, 1, :], sm[:, 0, :], ACT.Sqrt).then_inc(s["deviation"], 1)
        if self.next_table is not None:
            self.sub.core.load_table(e, self.next_table, 2 * self.sub.number)
        e.wait_ge(s["turned"], 1)
        wide = co.ps[:, TURN_BANK, :]
        if self.gain is None:
            ins = e.activation(co.xt[:, :], wide, ACT.Copy)
        else:
            ins = e.activation(co.xt[:, :], wide, ACT.Identity, scale=self.gain,
                               bias=self.offset if self.offset is not None else 0.0)
        ins.then_inc(s["features"], 1)

    def tensor(self, e):
        co, s = self.sub.core, self.sub.s
        for i in range(NT):
            e.wait_ge(s["normed"], i + 1)
            last = e.transpose(co.ps[:, TURN_BANK, i * 128:i * 128 + 128], co.xn[:, i, :], co.c("identity"))
        last.then_inc(s["turned"], 1)



class Attention:
    def __init__(self, sub, wide, heads=HEADS, own=True, ctx=False, pattern="full", scale=1.0, grouped=False,
                 relu=False, alibi=False, ctx_mask=False, rope=False, latent=False, ctx_rope=False, alpha=False,
                 value_scale=False, scores_by=None):
        self.sub, self.wide, self.heads, self.own, self.ctx, self.pattern = sub, wide, heads, own, ctx, pattern
        self.scale, self.grouped, self.relu, self.alibi, self.ctx_mask = scale, grouped, relu, alibi, ctx_mask
        self.rope, self.latent, self.ctx_rope, self.alpha = rope, latent, ctx_rope, alpha
        self.value_scale = value_scale
        self.scores_by = scores_by or (0.75 if wide else 0.85 if own else 0.6)
        self.ctx_rows = NC if wide else 128
        self.kw = KEYS if wide else (N if own else 0) + (128 if ctx else 0)
        self.units = heads if wide else heads // 4
        self.per_unit = 1 if wide else 4
        self.per_group = 1 if wide else 8
        self.vw = heads * 128
        self.key_tiles = (list(range(NT)) if own else []) + (["ctx"] if ctx else [])
        self.step_tiles = [(t, t + 1) for t in range(0, NT, 2)] if pattern == "local" else \
            [(t,) for t in self.key_tiles]
        self.jobs = self.projections()
        self.plan()

    def rows(self, pos):
        return slice(STRIP * (pos % 4), STRIP * (pos % 4) + STRIP)

    def q_col(self, pos):
        return (pos % RING if self.wide else pos // 4) * N

    def k_col(self, pos, tile):
        chunk = pos % RING if self.wide else 0 if self.grouped else pos // 4
        at = (N if self.own else 0) if tile == "ctx" else tile * 128
        return chunk * self.kw + at

    def v_cols(self, pos, tile):
        at = (len(self.key_tiles) - 1 if tile == "ctx" else tile) * self.vw + pos * 128
        return slice(at, at + 128)

    def projections(self):
        jobs = []
        for t in self.key_tiles:
            jobs += [("v", t, half) for half in range(self.heads // 8 if self.wide else 1)]
        if self.wide:
            self.pair_kinds = ["q"] + (["k"] if self.own else []) + (["kc"] if self.ctx else [])
            for i, kind in enumerate(self.pair_kinds):
                jobs.insert(3 * i, ("pair", kind, 0, i))
            return jobs
        sides = ["q"] + (["k"] if self.own else [])
        first = [("parts", side) for side in sides if not self.rope]
        if self.ctx:
            first += [("kc", c) for c in range(4)]
        if self.grouped:
            spread = [("spread", "q", c) for c in range(4)] + [("spread", "k", 0)]
        else:
            spread = [("spread", side, c) for c in range(4) for side in sides]
        return first + jobs + spread

    def ring(self, job):
        return sum(x[0] != "pair" for x in self.jobs[:self.jobs.index(job)])

    def takers(self, job):
        if job[0] in ("parts", "kc"):
            return "sv"
        return "vs"[self.ring(job) % 2]

    def taken(self, count, who):
        return sum(who in self.takers(x) for x in [x for x in self.jobs if x[0] != "pair"][:count])

    def plan(self):
        ev = []

        def score_tiles(u):
            if self.relu or u >= self.units:
                return []
            heads = range(u * self.per_unit, (u + 1) * self.per_unit)
            return [(p, t) for p in heads for t in self.step_tiles]

        def expo_tiles(u):
            heads = range(u * self.per_unit, (u + 1) * self.per_unit)
            return [(p, t) for p in heads for t in self.step_tiles]

        def value(pt):
            ev.append(("value",) + pt)
            if pt[1] == self.step_tiles[-1] and pt[0] % self.per_group == self.per_group - 1:
                ending.append([FINISH_LAG, pt[0] // self.per_group])

        for st in score_tiles(0):
            ev.append(("score",) + st)
        if not self.relu:
            ev.append(("guard", 0))
        waiting, ending = [], []
        for u in range(self.units):
            tiles, ahead = expo_tiles(u), score_tiles(u + 1)
            done, guarded = 0, not ahead
            for i, t in enumerate(tiles):
                ev.append(("expo",) + t)
                pair = 1 if u == 0 else (u + 3) // 2 if u % 2 else self.units
                if self.wide and 2 * pair < self.units and i < len(self.pair_kinds):
                    ev.append(("pair", self.pair_kinds[i], pair, len(self.pair_kinds) * pair + i))
                if not guarded and (i == len(tiles) - 1 or done == len(ahead)):
                    while done < len(ahead):
                        ev.append(("score",) + ahead[done])
                        done += 1
                    ev.append(("guard", u + 1))
                    guarded = True
                want = int(np.ceil((i + 1) * len(ahead) / (self.scores_by * len(tiles))))
                while done < min(want, len(ahead)):
                    ev.append(("score",) + ahead[done])
                    done += 1
                waiting.append(t)
                if len(waiting) > VALUE_LAG:
                    value(waiting.pop(0))
                for x in list(ending):
                    x[0] -= 1
                    if x[0] == -1:
                        ev.append(("lift", x[1]))
                        if x[1] % 2 == 0:
                            ending.remove(x)
                    if x[0] < -1:
                        ev.append(("divide", x[1] // 2, -2 - x[0]))
                        if x[0] == -1 - NT:
                            ending.remove(x)
        for t in waiting:
            value(t)
        for left, g in ending:
            if left >= 0:
                ev.append(("lift", g))
            if g % 2:
                ev += [("divide", g // 2, i) for i in range(max(0, -1 - left), NT)]
        count, self.steps = {}, []
        self.upto = {}
        for e in ev:
            k = e[0]
            if k in ("pair", "lift", "divide"):
                self.steps.append(e)
                continue
            self.steps.append(e + (count.get(k, 0),))
            count[k] = count.get(k, 0) + 1
            if k in ("score", "expo"):
                self.upto[(k, e[1] // self.per_unit)] = count[k]
            if k == "value":
                self.upto[(k, e[1] // self.per_group)] = count[k]

    def score_keys(self, qt):
        if self.pattern == "causal":
            return 0, 128 * (qt + 1), 128 * qt, self.sub.core.masks_b["causal"][:, :]
        if self.pattern == "local":
            first = max(0, 128 * qt - STRIP)
            n = 128 * (qt + 1) - first
            return first, n, 0, self.sub.core.masks_b["local"][:, 160 - n:160]
        return 0, N, None, None

    def expo_queries(self, kt):
        if kt == "ctx" or self.pattern == "full":
            return 0, N, None
        if self.pattern == "causal":
            return 128 * kt, N - 128 * kt, self.sub.core.masks_b["causal_t"][:, :]
        n = min(160, N - 128 * kt)
        return 128 * kt, n, self.sub.core.masks_b["local_t"][:, 0:n]


    def fill(self, e):
        co, s = self.sub.core, self.sub.s
        tiles = len(self.key_tiles)
        if self.wide:
            v = co.v[:, 0:tiles * self.vw].rearrange("p (h two c) -> p h two c", two=2, c=128)
            e.memset(v[:, :, 0, 64:128], 1.0).then_inc(s["filled"], 1)
            e.wait_ge(s["filled"], 1)
            e.memset(v[:, :, 1, 0:64], 1.0).then_inc(s["filled"], 1)
            return
        if self.relu:
            e.memset(co.spare[:, 0:N], 0.0)
        e.memset(co.v[:, 0:tiles * self.vw + 128], 0.0).then_inc(s["filled"], 1)
        e.wait_ge(s["filled"], 1)
        for t in range(tiles):
            for g in range(2):
                at = t * self.vw + g * 1024
                ones = co.v[:, at:at + 8 * 136].rearrange("p (h r) -> p h r", r=136)
                ones = ones[:, :, 64:72] if g == 0 else ones[:, :, 0:8]
                last = e.memset(ones, 1.0)
        last.then_inc(s["filled"], 1)

    def project_tensor(self, e):
        co, s, w = self.sub.core, self.sub.s, self.sub.w
        e.wait_ge(s["features"], 1)
        ctx_t = self.ctx_source()
        if self.ctx and ctx_t is co.ctx_t:
            e.wait_ge(s["ctx_ready"], 1)
        ksrc = co.xt[:, :]
        if self.latent:
            e.matmul(co.ps[0:32, OUT_BANK, :], w("down"), co.xt[:, :], start=True, stop=True)\
                .then_inc(s["latent"], 1)
            e.wait_ge(s["latent_kept"], 1)
            ksrc = co.sums[0:32, 0, :]
        if self.rope:
            self.rope_tensor(e, ksrc)
            self.rope_means(e)
        for job in self.jobs:
            if job[0] == "pair":
                self.pair_tensor(e, job)
                continue
            j = self.ring(job)
            if j >= 6:
                e.wait_ge(s["taken_v"], self.taken(j - 5, "v"))
                if self.taken(j - 5, "s"):
                    e.wait_ge(s["taken_s"], self.taken(j - 5, "s"))
            elif j == 0 and self.rope:
                e.wait_ge(s["rotated"], 2)
            bank = co.ps[:, j % 6, :]
            kind = job[0]
            if kind == "parts":
                last = e.matmul(bank, w("w" + job[1]), co.xt[:, :], start=True, stop=True)
            elif kind == "spread":
                _, side, c = job
                if self.rope:
                    e.wait_ge(s["operand_ready"], 1 if side == "q" else 2)
                else:
                    e.wait_ge(s["taken_v"], self.taken(self.ring(("parts", side)) + 1, "v"))
                high, low = co.parts[side]
                r = slice(32 * c, 32 * c + 32)
                e.matmul(bank, co.spread(f"spread_{side}_high")[r, :], high[r, :], start=True, stop=False)
                e.matmul(bank, co.spread(f"spread_{side}_low")[r, :], low[r, :], start=False, stop=False)
                if self.alpha and side == "q":
                    e.wait_ge(s["beta_split"], 2)
                    one = co.spread("one_and_position")[32 * c:32 * c + 1, :]
                    for part in range(2):
                        e.matmul(bank, co.beta_parts[32 * c:32 * c + 1, part * 128:part * 128 + 128], one,
                                 start=False, stop=False)
                r = slice(32 * c, 32 * c + 2)
                last = e.matmul(bank, co.spread("add_" + side + ("_alibi" if self.alibi else ""))[r, :],
                                co.spread("one_and_position")[r, :], start=False, stop=True)
            elif kind == "kc":
                c = job[1]
                n = 128
                last = e.matmul(bank[:, 0:n], w("wk")[:, c * 128:c * 128 + 128], ctx_t[:, 0:n], start=True,
                                stop=not self.ctx_mask)
                if self.ctx_mask:
                    e.matmul(bank[:, 0:n], w("k_add")[:, c * 128:c * 128 + 128], co.c("ones")[:, 0:n],
                             start=False, stop=False)
                    last = e.matmul(bank[:, 0:n], co.c("mask_row"), co.mask_vec[:, 0:n], start=False, stop=True)
            else:
                _, t, half = job
                m = NC if t == "ctx" else 128
                lhs = ctx_t[:, 0:NC] if t == "ctx" else ksrc[:, t * 128:t * 128 + 128]
                n = 512 if self.wide else 128
                biased = "bv" in self.sub.at
                last = e.matmul(bank[0:m, 0:n], lhs, w("wv")[:, half * n:half * n + n], start=True,
                                stop=not biased)
                if biased:
                    last = e.matmul(bank[0:m, 0:n], co.c("ones")[:, 0:m], w("bv"), start=False, stop=True)
            last.then_inc(s["projected"], 1)
        e.wait_ge(s["taken_v"], self.taken(99, "v"))
        e.wait_ge(s["taken_s"], self.taken(99, "s"))
        e.wait_ge(s["filled"], 2)

    def ctx_source(self):
        co = self.sub.core
        return co.ctx_t if "g_ctx" in self.sub.at else co.ctx_raw_t

    def take(self, e, job, part, copy):
        co, w = self.sub.core, self.sub.w
        bank = co.ps[:, self.ring(job) % 6, :]
        kind = job[0]
        if kind == "parts":
            side = job[1]
            high, low = co.parts[side]
            alpha = co.ka[:, 480:481] if self.alpha and side == "q" else None
            bias = w("b" + side) if "b" + side in self.sub.at else None
            if part == "round":
                return e.activation(high[:, :], bank, ACT.Identity, scale=1.0 if alpha is None else alpha,
                                    bias=0.0 if bias is None else bias)
            if alpha is None and bias is None:
                return e.tensor_tensor(low[:, :], bank, high[:, :].bitcast(F32), ALU.subtract)
            return e.scalar_tensor_tensor(out=low[:, :], in0=bank, scalar=bias if alpha is None else alpha,
                                          in1=high[:, :].bitcast(F32), op0=ALU.add if alpha is None else ALU.mult,
                                          op1=ALU.subtract)
        if kind == "spread":
            _, side, c = job
            return copy((co.q_parts if side == "q" else co.k_parts)[:, c * N:c * N + N], bank)
        if kind == "kc":
            c = job[1]
            rounded = co.tmp[:, self.ring(job) % 2, 0:128]
            if part == "round":
                return e.activation(rounded.bitcast(F32R), bank[:, 0:128], ACT.Identity, scale=co.c("k_b"),
                                    bias=co.c("k_bias"))
            at = self.k_col(4 * c, "ctx")
            return e.scalar_tensor_tensor(out=co.k_parts[:, at:at + 128], in0=bank[:, 0:128], scalar=co.c("k_a"),
                                          in1=rounded, op0=ALU.mult, op1=ALU.add)
        _, t, half = job
        m = NC if t == "ctx" else 128
        if self.wide:
            at = self.v_cols(half * 8, t).start
            dst = co.v[0:m, at:at + 8 * 128].rearrange("p (h two c) -> p h two c", two=4, c=64)[:, :, 0:4:3, :]
            return copy(dst, bank[0:m, 0:512].rearrange("p (h two c) -> p h two c", two=2, c=64))
        at = self.v_cols(0, t).start
        for g in range(2):
            dst = co.v[0:m, at + g * 1024:at + g * 1024 + 8 * 136].rearrange("p (h r) -> p h r", r=136)
            last = copy(dst[:, :, 64 * g:64 * g + 8], bank[0:m, g * 64:g * 64 + 64].rearrange("p (h c) -> p h c", c=8))
        return last

    def project_vector(self, e, link):
        co, s, w = self.sub.core, self.sub.s, self.sub.w
        if self.alpha:
            e.tensor_scalar(co.ka[:, 480:481], w("alpha"), float(8 ** -0.5 / 0.72), None, ALU.mult)\
                .then_inc(s["alpha_ready"], 1)
            e.tensor_copy(co.tmp[:, 0, 0:128].bitcast(F32R), w("beta_low")).then_inc(s["beta_split"], 1)
            e.tensor_copy(co.beta_parts[:, 0:128], w("beta_high"))
            e.wait_ge(s["beta_split"], 1)
            e.tensor_tensor(co.beta_parts[:, 128:256], w("beta_low"), co.tmp[:, 0, 0:128], ALU.subtract)\
                .then_inc(s["beta_split"], 1)
        if self.rope:
            self.rope_vector(e, link)

        for job in self.jobs:
            if job[0] == "pair":
                self.pair_vector(e, link, job)
                continue
            j = self.ring(job)
            if self.takers(job) == "sv":
                e.wait_ge(s["taken_s"], self.taken(j + 1, "s"))
                self.take(e, job, "add", None).then_inc(s["taken_v"], 1)
            elif self.takers(job) == "v":
                e.wait_ge(s["projected"], j + 1)
                if job[0] == "v":
                    e.wait_ge(s["filled"], 2)
                self.take(e, job, None, e.tensor_copy).then_inc(s["taken_v"], 1)

    def project_scalar(self, e):
        co, s, w = self.sub.core, self.sub.s, self.sub.w
        if self.latent:
            e.wait_ge(s["latent"], 1)
            e.activation(co.sums[0:32, 0, :], co.ps[0:32, OUT_BANK, :], ACT.Copy).then_inc(s["latent_kept"], 1)
        if self.rope:
            self.rope_scalar(e)
        if self.alpha:
            e.wait_ge(s["alpha_ready"], 1)

        for job in self.jobs:
            if job[0] == "pair":
                self.pair_scalar(e, job)
                continue
            j = self.ring(job)
            if "s" not in self.takers(job):
                continue
            e.wait_ge(s["projected"], j + 1)
            if self.takers(job) == "sv":
                if job[0] == "kc" and j >= 2:
                    e.wait_ge(s["taken_v"], self.taken(j - 1, "v"))
                self.take(e, job, "round", None).then_inc(s["taken_s"], 1)
            else:
                if job[0] == "v":
                    e.wait_ge(s["filled"], 2)
                self.take(e, job, None, lambda out, in_: e.activation(out, in_, ACT.Copy))\
                    .then_inc(s["taken_s"], 1)


    def pair_at(self, kind, part):
        return slice(64 * part, 64 * part + 64), slice(64 - 64 * part, 128 - 64 * part), \
            N if kind != "kc" else 128

    def pair_cols(self, kind, pair, part):
        pos = 2 * pair + part
        if kind == "q":
            return slice(self.q_col(pos), self.q_col(pos) + N)
        at = self.k_col(pos, "ctx" if kind == "kc" else 0)
        return slice(at, at + (128 if kind == "kc" else N))

    def pair_tensor(self, e, job):
        co, s, w = self.sub.core, self.sub.s, self.sub.w
        _, kind, pair, j = job
        if j >= 1:
            e.wait_ge(s["low"], 2 * j)
        bank = co.ps[:, OUT_BANK, :]
        at = slice(pair * 128, pair * 128 + 128)
        src = co.xt[:, :] if kind != "kc" else self.ctx_source()[:, :]
        last = e.matmul(bank[:, 0:src.shape[1]], w("wq" if kind == "q" else "wk")[:, at], src, start=True,
                        stop=True, skip_group_check=True)
        if kind == "kc" and self.ctx_rope:
            last = e.matmul(bank[:, 128:256], w("wk_swapped")[:, at], src, start=True, stop=True,
                            skip_group_check=True)
        last.then_inc(s["pair_projected"], 1)

    def pair_source(self, kind):
        co = self.sub.core
        return co.ctx_rotated[:, :] if kind == "kc" and self.ctx_rope else co.ps[:, OUT_BANK, :]

    def pair_room(self, e, pair):
        s = self.sub.s
        before = 2 * pair + 1 - RING
        if before >= 0:
            e.wait_ge(s["expo"], self.upto[("expo", before)])
            e.wait_ge(s["score"], self.upto[("score", before)])

    def pair_scalar(self, e, job):
        co, s = self.sub.core, self.sub.s
        _, kind, pair, j = job
        self.pair_room(e, pair)
        if kind == "kc" and self.ctx_rope:
            e.wait_ge(s["ctx_rotated"], pair + 1)
        else:
            e.wait_ge(s["pair_projected"], j + 1)
        for part in range(2):
            rows, _, n = self.pair_at(kind, part)
            dst = co.q_high if kind == "q" else co.k_both
            e.activation(dst[rows, self.pair_cols(kind, pair, part)], self.pair_source(kind)[rows, 0:n], ACT.Copy)\
                .then_inc(s["high"], 1)

    def pair_vector(self, e, link, job):
        co, s, w = self.sub.core, self.sub.s, self.sub.w
        _, kind, pair, j = job
        if kind == "kc" and self.ctx_rope:
            bank, turned = co.ps[:, OUT_BANK, :], co.tmp
            e.wait_ge(s["pair_projected"], j + 1)
            if pair:
                e.wait_ge(s["low"], 2 * (j - len(self.pair_kinds)) + 2)
            link(e.tensor_tensor(turned[:, 0, 0:NC], bank[:, 0:NC], w("cos"), ALU.mult))
            link(e.tensor_tensor(turned[:, 1, 0:NC], bank[:, 128:128 + NC], w("sin"), ALU.mult))
            e.tensor_tensor(co.ctx_rotated[:, 0:NC], turned[:, 0, 0:NC], turned[:, 1, 0:NC], ALU.add)\
                .then_inc(s["ctx_rotated"], 1)
        self.pair_room(e, pair)
        for part in range(2):
            rows, other, n = self.pair_at(kind, part)
            cols = self.pair_cols(kind, pair, part)
            e.wait_ge(s["high"], 2 * j + part + 1)
            high = (co.q_high if kind == "q" else co.k_both)[rows, cols].bitcast(F32)
            low = co.q_low[0:64, cols] if kind == "q" else co.k_both[other, cols]
            e.tensor_tensor(low, self.pair_source(kind)[rows, 0:n], high, ALU.subtract).then_inc(s["low"], 1)

    def pair_pool(self, e, job):
        co, s = self.sub.core, self.sub.s
        _, kind, pair, j = job
        self.pair_room(e, pair)
        for part in range(2):
            rows, other, _ = self.pair_at(kind, part)
            cols = self.pair_cols(kind, pair, part)
            e.wait_ge(s["high"], 2 * j + part + 1)
            if j or part:
                e.wait_ge(s["copied"], 2 * j + part)
            else:
                e.wait_ge(s["filled"], 2)
            if kind == "q":
                ins = e.tensor_copy(co.q_high[other, cols], co.q_high[rows, cols])
            else:
                ins = e.tensor_copy(co.k_high[0:64, cols], co.k_both[rows, cols])
            ins.then_inc(s["copied"], 1)

    def fill_ones(self, e):
        co, s = self.sub.core, self.sub.s
        wide = RING * KEYS // ONES_STEPS
        for i in range(ONES_STEPS):
            last = e.activation(co.k_high[64:65, i * wide:i * wide + wide], co.c("ones")[:, 0:wide], ACT.Copy)
        last.then_inc(s["ones_filled"], 1)

    def attend_pool(self, e):
        for step in self.jobs + self.steps:
            if step[0] == "pair":
                self.pair_pool(e, step)


    def rope_rows(self, j):
        return slice(0, 128 if j == 0 else 32)

    def rope_product(self, j):
        return self.sub.core.spare[self.rope_rows(j), j * N:(j + 1) * N]

    def rope_tensor(self, e, ksrc):
        co, s, w = self.sub.core, self.sub.s, self.sub.w
        for j, (side, src) in enumerate((("q", co.xt[:, :]), ("k", ksrc))):
            for half, name in ((0, ""), (1, "_swapped")):
                last = e.matmul(co.ps[self.rope_rows(j), 2 * j + half, :], w("w" + side + name), src, start=True,
                                stop=True)
            last.then_inc(s["rope_in"], 1)

    def rope_means(self, e):
        co, s = self.sub.core, self.sub.s
        for j in range(2):
            r = self.rope_rows(j)
            e.wait_ge(s["squared"], j + 1)
            e.matmul(co.ps[r, (TURN_BANK, OUT_BANK)[j], :], co.c("head_mean")[r, r], co.o[r, j * N:j * N + N],
                     start=True, stop=True).then_inc(s["mean_square"], 1)

    def rope_vector(self, e, link):
        co, s, w = self.sub.core, self.sub.s, self.sub.w
        for j in range(2):
            r = self.rope_rows(j)
            e.wait_ge(s["rope_in"], j + 1)
            turned = [co.o[r, (2 + 2 * j + i) * N:(3 + 2 * j + i) * N] for i in range(2)]
            link(e.tensor_tensor(turned[0], co.ps[r, 2 * j, :], w("cos")[r, :], ALU.mult))
            link(e.tensor_tensor(turned[1], co.ps[r, 2 * j + 1, :], w("sin")[r, :], ALU.mult))
            e.tensor_tensor(self.rope_product(j), turned[0], turned[1], ALU.add).then_inc(s["rotated"], 1)
        def split(j):
            high, low = co.parts["qk"[j]]
            e.wait_ge(s["rounded"], j + 1)
            e.tensor_tensor(low[self.rope_rows(j), :], self.rope_product(j),
                            high[self.rope_rows(j), :].bitcast(F32), ALU.subtract).then_inc(s["operand_ready"], 1)

        for j in range(2):
            r = self.rope_rows(j)
            e.wait_ge(s["root"], j + 1)
            root = co.o[r, (6 + j) * N:(7 + j) * N]
            for half in range(2):
                cols = slice(half * N // 2, (half + 1) * N // 2)
                link(e.reciprocal(root[:, cols], root[:, cols]))
                if j == 1 and half == 0:
                    split(0)
            e.tensor_tensor(self.rope_product(j), self.rope_product(j), root, ALU.mult)\
                .then_inc(s["divided"], 1)
        split(1)

    def rope_scalar(self, e):
        co, s = self.sub.core, self.sub.s
        for j in range(2):
            e.wait_ge(s["rotated"], j + 1)
            e.activation(co.o[self.rope_rows(j), j * N:j * N + N], self.rope_product(j), ACT.Square)\
                .then_inc(s["squared"], 1)
        for j in range(2):
            r = self.rope_rows(j)
            e.wait_ge(s["mean_square"], j + 1)
            e.activation(co.o[r, (6 + j) * N:(7 + j) * N], co.ps[r, (TURN_BANK, OUT_BANK)[j], :], ACT.Sqrt,
                         bias=co.c("rms_eps")[r, :]).then_inc(s["root"], 1)
        co.load_table(e, ACT.Exp, 2 * self.sub.number)
        for j, side in enumerate("qk"):
            e.wait_ge(s["divided"], j + 1)
            e.activation(co.parts[side][0][self.rope_rows(j), :], self.rope_product(j), ACT.Copy)\
                .then_inc(s["rounded"], 1)


    def guard(self):
        return self.sub.core.guard_wide if self.wide else self.sub.core.guard_thin

    def guard_col(self, pos):
        return 64 if self.wide else STRIP * (pos % 4) + MAX_ROW

    def attend_tensor(self, e):
        co, s = self.sub.core, self.sub.s
        ps = co.ps
        for step in self.steps:
            kind, n = step[0], step[-1]
            if kind == "pair":
                self.pair_tensor(e, step)
            elif kind == "score":
                _, pos, t, _ = step
                if self.wide:
                    r, q, k = slice(0, 128), co.q_high, co.k_both
                    if pos % 2 == 0:
                        e.wait_ge(s["low"], 2 * len(self.pair_kinds) * (pos // 2 + 1))
                        e.wait_ge(s["copied"], 2 * len(self.pair_kinds) * (pos // 2 + 1))
                else:
                    r, q, k = self.rows(pos), co.q_parts, co.k_parts
                qc = self.q_col(pos)
                bank = ps[:, SCORE_BANK + n % 2, :]
                if n >= 2:
                    e.wait_ge(s["maximum"], n - 1)
                if t == ("ctx",):
                    kc = self.k_col(pos, "ctx")
                    for i in range(NT):
                        last = e.matmul(bank[:, i * 80:i * 80 + 80], q[r, qc + i * 128:qc + i * 128 + 128],
                                        k[r, kc:kc + 80], start=True, stop=True, skip_group_check=True)
                for i, qt in enumerate(t if t != ("ctx",) else ()):
                    first, m, mc, mask = self.score_keys(qt)
                    kc, at = self.k_col(pos, 0) + first, i * LOCAL
                    last = e.matmul(bank[:, at:at + m], q[r, qc + qt * 128:qc + qt * 128 + 128], k[r, kc:kc + m],
                                    start=True, stop=mask is None, skip_group_check=True)
                    if mask is not None:
                        last = e.matmul(bank[:, at + mc:at + mc + mask.shape[1]], co.identity_b[:, :], mask,
                                        start=False, stop=True, skip_group_check=True)
                last.then_inc(s["score"], 1)
            elif kind == "guard":
                u = step[1]
                e.wait_ge(s["maximum"], self.upto[("score", u)])
                if self.own and self.ctx:
                    e.wait_ge(s["guard_ready"], (u + 1) * self.per_unit)
                if n >= 1:
                    e.wait_ge(s["guarded"], n)
                g = self.guard()
                m = g.shape[3]
                for i in range(NT):
                    last = e.transpose(ps[0:m, TURN_BANK, i * 128:i * 128 + 128], g[:, u % 2, i, :],
                                       co.c("identity"))
                last.then_inc(s["guard_turned"], 1)
            elif kind == "expo":
                _, pos, tiles, _ = step
                u = pos // self.per_unit
                if n >= 2:
                    e.wait_ge(s["relu" if self.relu else "probs"], n - 1)
                if not self.relu:
                    e.wait_ge(s["guarded"], u + 1)
                if self.wide and n == 0:
                    e.wait_ge(s["ones_filled"], 1)
                for i, t in enumerate(tiles):
                    first, m, mask = self.expo_queries(t)
                    bank = ps[:, EXPO_BANK + n % 2, i * LOCAL:i * LOCAL + m]
                    kc, qc = self.k_col(pos, t), self.q_col(pos) + first
                    if self.wide:
                        e.matmul(bank, co.k_both[:, kc:kc + 128], co.q_high[:, qc:qc + m], start=True, stop=False,
                                 skip_group_check=True)
                        last = e.matmul(bank, co.k_high[0:65, kc:kc + 128], co.q_low[0:65, qc:qc + m], start=False,
                                        stop=mask is None, skip_group_check=True)
                    else:
                        r = self.rows(pos)
                        if self.relu:
                            moving = co.q_parts[r, qc:qc + m]
                        else:
                            moving = co.q_guarded[r, u % 2 * N + first:u % 2 * N + first + m]
                        last = e.matmul(bank, co.k_parts[r, kc:kc + 128], moving, start=True, stop=mask is None,
                                        skip_group_check=True)
                    if mask is not None:
                        last = e.matmul(bank[:, 0:mask.shape[1]], co.identity_b[:, :], mask, start=False,
                                        stop=True, skip_group_check=True)
                last.then_inc(s["expo"], 1)
            elif kind == "value":
                _, pos, tiles, _ = step
                g = pos // self.per_group
                e.wait_ge(s["probs"], n + 1)
                opens = tiles == self.step_tiles[0] and pos % self.per_group == 0
                closes = tiles == self.step_tiles[-1] and pos % self.per_group == self.per_group - 1
                if opens and g >= 2:
                    e.wait_ge(s["lifted"], 2 * g - 2)
                for i, t in enumerate(tiles):
                    first, m, _ = self.expo_queries(t)
                    keys = self.ctx_rows if t == "ctx" else 128
                    last = e.matmul(ps[:, VALUE_BANK + g % 2, first:first + m], co.v[0:keys, self.v_cols(pos, t)],
                                    co.p[0:keys, n % 4, i * LOCAL:i * LOCAL + m], start=opens and i == 0,
                                    stop=closes and t == tiles[-1], skip_group_check=True)
                last.then_inc(s["valued"], 1)

    def attend_vector(self, e, link):
        co, s = self.sub.core, self.sub.s
        ps = co.ps
        if self.relu:
            e.wait_ge(s["keep_ready"], 1)
        for step in self.steps:
            kind, n = step[0], step[-1]
            if kind == "pair":
                self.pair_vector(e, link, step)
            elif kind == "score":
                _, pos, t, _ = step
                u = pos // self.per_unit
                e.wait_ge(s["score"], n + 1)
                bank = ps[:, SCORE_BANK + n % 2, :]
                g = self.guard()[:, u % 2, :, self.guard_col(pos)]
                if t == ("ctx",):
                    out = co.max_ctx[:, n % 2, :] if self.own else g
                    ins = e.tensor_reduce(out, bank[:, 0:NT * 80].rearrange("p (i k) -> p i k", k=80)[:, :, 0:NC], AX.X,
                                          ALU.max, negate=True)
                    ins.then_inc(s["maximum"], 1)
                    if self.own:
                        e.wait_ge(s["maximum"], n + 1)
                        e.tensor_tensor(g, g, out, ALU.min).then_inc(s["guard_ready"], 1)
                else:
                    for i, qt in enumerate(t):
                        _, m, _, _ = self.score_keys(qt)
                        last = e.tensor_reduce(g[:, qt:qt + 1], bank[:, i * LOCAL:i * LOCAL + m], AX.X, ALU.max,
                                               negate=True)
                    last.then_inc(s["maximum"], 1)
            elif kind == "guard":
                u = step[1]
                e.wait_ge(s["guard_turned"], u + 1)
                if self.wide:
                    qc = self.q_col(u)
                    e.tensor_copy(co.q_low[64:65, qc:qc + N], ps[64:65, TURN_BANK, :]).then_inc(s["guarded"], 1)
                else:
                    if u >= 2:
                        e.wait_ge(s["expo"], self.upto[("expo", u - 2)])
                    e.tensor_tensor(co.q_guarded[:, u % 2 * N:u % 2 * N + N],
                                    co.q_parts[:, u * N:u * N + N].bitcast(F32),
                                    ps[:, TURN_BANK, :], ALU.add).then_inc(s["guarded"], 1)
            elif kind == "expo" and self.relu:
                e.wait_ge(s["relu"], n + 1)
                r = co.tmp[:, n % 2, :]
                masked = co.spare[:, (1 + n % 2) * N:(2 + n % 2) * N]
                link(e.tensor_tensor(masked, r, co.spare[:, 0:N], ALU.mult))
                if n >= 4:
                    e.wait_ge(s["valued"], n - 3)
                e.tensor_tensor(co.p[:, n % 4, :], masked, r, ALU.mult).then_inc(s["probs"], 1)
            elif kind == "divide":
                _, pair, i = step
                e.wait_ge(s["lifted"], 4 * pair + 3)
                sums = co.sums[:, pair % 2, i * 128:i * 128 + 128]
                out = co.o[:, pair * N + i * 128:pair * N + i * 128 + 128]
                if self.relu:
                    link(e.tensor_scalar(sums, sums, 1e-32, None, ALU.add))
                link(e.reciprocal(sums, sums))
                e.wait_ge(s["lifted"], 4 * pair + 4)
                if self.value_scale:
                    e.wait_ge(s["ka_moved"], 32)
                    ins = e.scalar_tensor_tensor(out=out, in0=out, scalar=co.scale_o[:, 0:1], in1=sums,
                                                 op0=ALU.mult, op1=ALU.mult)
                else:
                    ins = e.tensor_tensor(out, out, sums, ALU.mult)
                ins.then_inc(s["finished"], 1)

    def attend_scalar(self, e):
        co, s, w = self.sub.core, self.sub.s, self.sub.w
        for step in self.steps:
            if step[0] == "pair":
                self.pair_scalar(e, step)
            elif step[0] == "lift":
                g = step[1]
                e.wait_ge(s["valued"], self.upto[("value", g)])
                if g >= 4:
                    e.wait_ge(s["finished"], NT * (g // 2 - 1))
                rows, other, _ = self.pair_at(None, g % 2)
                bank = co.ps[:, VALUE_BANK + g % 2, :]
                e.activation(co.sums[rows, g // 2 % 2, :], bank[other, :], ACT.Copy).then_inc(s["lifted"], 1)
                e.activation(co.o[rows, g // 2 * N:g // 2 * N + N], bank[rows, :], ACT.Copy)\
                    .then_inc(s["lifted"], 1)
            if step[0] != "expo":
                continue
            _, pos, tiles, n = step
            m = (len(tiles) - 1) * LOCAL + self.expo_queries(tiles[-1])[1]
            keys = self.ctx_rows if tiles == ("ctx",) else 128
            e.wait_ge(s["expo"], n + 1)
            bank = co.ps[0:keys, EXPO_BANK + n % 2, 0:m]
            if self.relu:
                if n >= 2:
                    e.wait_ge(s["probs"], n - 1)
                e.activation(co.tmp[0:keys, n % 2, :], bank, ACT.Relu, scale=self.scale,
                             bias=w("sn_bias")[0:keys, 0:1]).then_inc(s["relu"], 1)
            else:
                if n >= 4:
                    e.wait_ge(s["valued"], n - 3)
                e.activation(co.p[0:keys, n % 4, 0:m], bank, ACT.Exp, scale=self.scale).then_inc(s["probs"], 1)


    def output_tensor(self, e):
        co, s, w = self.sub.core, self.sub.s, self.sub.w
        pairs = self.heads // self.per_group // 2
        biased = "bo" in self.sub.at
        for i in range(NT):
            e.wait_ge(s["finished"], NT * (pairs - 1) + i + 1)
            out = co.ps[:, OUT_BANKS[i], 0:128]
            for c in range(pairs):
                last = e.matmul(out, co.o[:, c * N + i * 128:c * N + i * 128 + 128],
                                w("wo")[:, c * 128:c * 128 + 128], start=c == 0,
                                stop=c == pairs - 1 and not biased, skip_group_check=True)
            if biased:
                last = e.matmul(out, co.c("ones")[:, 0:128], w("bo"), start=False, stop=True,
                                skip_group_check=True)
            last.then_inc(s["out"], 1)

    def output_vector(self, e, link, into):
        co, s = self.sub.core, self.sub.s
        for i in range(NT):
            e.wait_ge(s["out"], i + 1)
            link(e.tensor_tensor(into[:, i, :], into[:, i, :], co.ps[:, OUT_BANKS[i], 0:128], ALU.add))


def attention_sublayer(core, load_next, clear, key, number, norm, keep_h=False, add_h=False, **kinds):
    sub = Sublayer(core, key, number)
    s, w = sub.s, sub.w
    at = Attention(sub, **kinds)
    table = None if at.relu or at.rope or at.value_scale else ACT.Exp
    nm = Norm(sub, next_table=table, gain=w("g") if "g" in sub.at else None, offset=w("b") if "b" in sub.at else None,
              keep=core.h if keep_h else None, source=core.h if add_h else None, **norm)
    into = core.h if keep_h or add_h else core.x
    own_ctx = kinds.get("ctx") and "g_ctx" in sub.at

    with core.nc.Block() as block:

        @block.sync
        def _(sp):
            load_next(sp)
            if at.value_scale:
                ka_sync(sub, sp)

        @block.gpsimd
        def _(pool):
            clear(pool)
            at.fill(pool)
            at.attend_pool(pool)

        @block.vector
        def _(dve):
            link = chained(dve, s["step_v"])
            dve.wait_ge(core.loaded[key], 16)
            nm.vector(dve, link)
            if own_ctx:
                dve.tensor_scalar(core.ctx_t[:, 0:NC], core.ctx_norm_t[:, 0:NC], w("g_ctx"), w("b_ctx"),
                                  ALU.mult, ALU.add).then_inc(s["ctx_ready"], 1)
            if at.relu:
                keep_vector(sub, dve)
            if at.value_scale:
                ka_vector(sub, dve, link)
            at.project_vector(dve, link)
            at.attend_vector(dve, link)
            at.output_vector(dve, link, into)
            if add_h:
                flat = lambda a: a[:, :, :].rearrange("p i d -> p (i d)")
                dve.tensor_tensor(flat(core.x), flat(core.x), flat(core.h), ALU.add).then_inc(s["added"], 1)

        @block.scalar
        def _(act):
            if at.wide:
                at.fill_ones(act)
            act.wait_ge(core.loaded[key], 16)
            nm.scalar(act)
            if at.relu:
                keep_scalar(sub, act)
            if at.value_scale:
                ka_scalar(sub, act)
                core.load_table(act, ACT.Exp, 2 * number)
            at.project_scalar(act)
            at.attend_scalar(act)
            core.load_table(act, ACT.Sqrt, 2 * number + 1)

        @block.tensor
        def _(pe):
            pe.wait_ge(core.loaded[key], 16)
            nm.tensor(pe)
            if at.relu:
                keep_tensor(sub, pe)
            if at.value_scale:
                ka_tensor(sub, pe)
            at.project_tensor(pe)
            at.attend_tensor(pe)
            at.output_tensor(pe)



def keep_vector(sub, e):
    co, s = sub.core, sub.s
    e.wait_ge(co.x_loaded, 64)
    e.tensor_scalar(co.keep_rows[:, :], co.mask_rows[:, :], -1.0, 1.0, ALU.mult, ALU.add)\
        .then_inc(s["keep_loaded"], 1)


def keep_tensor(sub, e):
    co, s = sub.core, sub.s
    e.wait_ge(s["keep_loaded"], 1)
    for i in range(NT):
        last = e.transpose(co.ps[0:NC, OUT_BANK, i * 128:i * 128 + 128], co.keep_rows[:, i * NC:i * NC + NC],
                           co.c("identity"))
    last.then_inc(s["keep_turned"], 1)


def keep_scalar(sub, e):
    co, s = sub.core, sub.s
    e.wait_ge(s["keep_turned"], 1)
    e.wait_ge(s["filled"], 1)
    e.activation(co.spare[0:NC, 0:N], co.ps[0:NC, OUT_BANK, :], ACT.Copy).then_inc(s["keep_ready"], 1)



KA_QK, KA_AX, KA_PHI, KA_PSI, KA_TURNED, KA_PHI2, KA_PSI2, KA_OUT = 16, 32, 96, 160, 240, 304, 320, 336
KA_STATS, KA_VAR = 400, 440


def ka_tensor(sub, e):
    co, s, w = sub.core, sub.s, sub.w
    ps, ka = co.ps[:, OUT_BANK, :], co.ka
    e.wait_ge(s["ka_vector"], 1)
    for h in range(HEADS):
        last = e.matmul(ps[0:16, h:h + 1], w("wqk_mean")[:, 16 * h:16 * h + 16], ka[:, 1:2], start=True,
                        stop=True, skip_group_check=True)
    last.then_inc(s["ka_tensor"], 1)
    e.wait_ge(s["ka_scalar"], 1)
    for t in range(4):
        e.matmul(ps[0:16, KA_AX + 16 * t:KA_AX + 16 * t + 16], w("ka_a")[:, 16 * t:16 * t + 16],
                 ka[0:16, KA_QK:KA_QK + 16], start=True, stop=True, skip_group_check=True)
        last = e.matmul(ps[0:8, KA_PHI + 16 * t:KA_PHI + 16 * t + 16], w("ka_phi1")[:, 8 * t:8 * t + 8],
                        ka[0:16, KA_QK:KA_QK + 16], start=True, stop=True, skip_group_check=True)
    last.then_inc(s["ka_tensor"], 1)
    e.wait_ge(s["ka_vector"], 2)
    e.wait_ge(s["ka_scalar"], 2)
    for t in range(4):
        e.matmul(ps[0:16, KA_PSI + 16 * t:KA_PSI + 16 * t + 16], ka[0:16, KA_AX + 16 * t:KA_AX + 16 * t + 16],
                 w("ka_psi1")[:, 16 * t:16 * t + 16], start=True, stop=True, skip_group_check=True)
        last = e.matmul(ps[0:16, KA_PHI2 + 2 * t:KA_PHI2 + 2 * t + 2], ka[0:8, KA_PHI + 16 * t:KA_PHI + 16 * t + 16],
                        w("ka_phi2")[:, 2 * t:2 * t + 2], start=True, stop=True, skip_group_check=True)
    last.then_inc(s["ka_tensor"], 1)
    e.wait_ge(s["ka_scalar"], 4)
    for t in range(4):
        last = e.transpose(ps[0:16, KA_TURNED + 16 * t:KA_TURNED + 16 * t + 16],
                           ka[0:16, KA_PSI + 16 * t:KA_PSI + 16 * t + 16], co.c("identity")[0:16, 0:16])
    last.then_inc(s["ka_tensor"], 1)
    e.wait_ge(s["ka_vector"], 5)
    for t in range(4):
        last = e.matmul(ps[0:16, KA_PSI2 + 2 * t:KA_PSI2 + 2 * t + 2],
                        ka[0:16, KA_TURNED + 16 * t:KA_TURNED + 16 * t + 16], w("ka_psi2")[:, 2 * t:2 * t + 2],
                        start=True, stop=True, skip_group_check=True)
    last.then_inc(s["ka_tensor"], 1)


def ka_vector(sub, e, link):
    co, s, w = sub.core, sub.s, sub.w
    ps, ka = co.ps[:, OUT_BANK, :], co.ka
    e.wait_ge(s["features"], 1)
    link(e.tensor_reduce(ka[:, 0:1], co.xt[:, :], AX.X, ALU.add))
    e.tensor_scalar(ka[:, 1:2], ka[:, 0:1], 1.0 / N, None, ALU.mult).then_inc(s["ka_vector"], 1)
    e.wait_ge(s["ka_tensor"], 2)
    e.tensor_copy(ka[0:16, KA_AX:KA_AX + 64], ps[0:16, KA_AX:KA_AX + 64]).then_inc(s["ka_vector"], 1)
    e.wait_ge(s["ka_tensor"], 3)
    psi = ka[0:16, KA_PSI:KA_PSI + 64]
    link(e.tensor_tensor(psi, ps[0:16, KA_PSI:KA_PSI + 64], w("ka_bpsi1"), ALU.add))
    link(e.tensor_tensor(ka[0:16, KA_PHI2:KA_PHI2 + 8], ps[0:16, KA_PHI2:KA_PHI2 + 8], w("ka_bphi2"), ALU.add))
    stats, mv = ka[0:16, KA_STATS:KA_STATS + 24], ka[0:16, KA_STATS + 24:KA_STATS + 32]
    for t in range(4):
        last = e.bn_stats(stats[:, 6 * t:6 * t + 6], psi[:, 16 * t:16 * t + 16])
    link(last)
    for t in range(4):
        last = e.bn_aggr(mv[:, 2 * t:2 * t + 2], stats[:, 6 * t:6 * t + 6])
    link(last)
    var, root = ka[0:16, KA_VAR:KA_VAR + 4], ka[0:16, KA_VAR + 4:KA_VAR + 8]
    e.tensor_scalar(var, mv[:, 1:8:2], LN_EPS, None, ALU.add).then_inc(s["ka_vector"], 1)
    e.wait_ge(s["ka_scalar"], 3)
    link(e.reciprocal(root, root))
    for t in range(4):
        last = e.tensor_scalar(psi[:, 16 * t:16 * t + 16], psi[:, 16 * t:16 * t + 16], mv[:, 2 * t:2 * t + 1],
                               root[:, t:t + 1], ALU.subtract, ALU.mult)
    link(last)
    link(e.tensor_tensor(psi, psi, w("ka_g"), ALU.mult))
    e.tensor_tensor(psi, psi, w("ka_b"), ALU.add).then_inc(s["ka_vector"], 1)
    e.wait_ge(s["ka_tensor"], 4)
    e.tensor_copy(ka[0:16, KA_TURNED:KA_TURNED + 64], ps[0:16, KA_TURNED:KA_TURNED + 64])\
        .then_inc(s["ka_vector"], 1)
    e.wait_ge(s["ka_tensor"], 5)
    psi2, out = ka[0:16, KA_PSI2:KA_PSI2 + 8], ka[0:16, KA_OUT:KA_OUT + 8]
    link(e.tensor_tensor(psi2, ps[0:16, KA_PSI2:KA_PSI2 + 8], w("ka_bpsi2"), ALU.add))
    link(e.tensor_tensor(out, ka[0:16, KA_PHI2:KA_PHI2 + 8], psi2, ALU.mult))
    link(e.tensor_scalar(out, out, w("ka_temp"), None, ALU.mult))
    link(e.tensor_tensor(out, out, w("ka_mix"), ALU.mult))
    e.tensor_scalar(out, out, 1.0, w("gamma"), ALU.add, ALU.mult).then_inc(s["ka_vector"], 1)


def ka_scalar(sub, e):
    co, s, w = sub.core, sub.s, sub.w
    ps, ka = co.ps[:, OUT_BANK, :], co.ka
    e.wait_ge(s["ka_tensor"], 1)
    e.activation(ka[0:16, KA_QK:KA_QK + 16], ps[0:16, 0:16], ACT.Copy).then_inc(s["ka_scalar"], 1)
    e.wait_ge(s["ka_vector"], 2)
    for t in range(4):
        last = e.activation(ka[0:8, KA_PHI + 16 * t:KA_PHI + 16 * t + 16],
                            ps[0:8, KA_PHI + 16 * t:KA_PHI + 16 * t + 16], ACT.Silu,
                            bias=w("ka_bphi1")[:, t:t + 1], scale=1.0)
    last.then_inc(s["ka_scalar"], 1)
    e.wait_ge(s["ka_vector"], 3)
    e.activation(ka[0:16, KA_VAR + 4:KA_VAR + 8], ka[0:16, KA_VAR:KA_VAR + 4], ACT.Sqrt)\
        .then_inc(s["ka_scalar"], 1)
    e.wait_ge(s["ka_vector"], 4)
    e.activation(ka[0:16, KA_PSI:KA_PSI + 64], ka[0:16, KA_PSI:KA_PSI + 64], ACT.Gelu)\
        .then_inc(s["ka_scalar"], 1)


def ka_sync(sub, e):
    co, s = sub.core, sub.s
    e.wait_ge(s["ka_vector"], 6)
    e.dma_start(co.scratch, co.ka[0:16, KA_OUT:KA_OUT + 8]).then_inc(s["ka_moved"], 16)
    e.wait_ge(s["ka_moved"], 16)
    with co.nc.allow_non_contiguous_dma("128 words"):
        e.dma_start(co.scale_o[:, 0:1], co.scratch.rearrange("h (d one) -> (h d) one", one=1)).then_inc(s["ka_moved"], 16)
    e.wait_ge(s["ka_moved"], 32)



def context_stage(core, load_next, number, x_in, ctx_in, mask_in, vec_in, b):
    s = core.sets[number % 2]
    sm = core.small

    with core.nc.Block() as block:

        @block.sync
        def _(sp):
            one = lambda a: a[bass.ds(b, 1)].rearrange("o p c -> (o p) c")
            sp.dma_start(core.ctx_rows[0:NC, :], one(ctx_in)).then_inc(core.x_loaded, 16)
            sp.dma_start(core.x[:, :, :].rearrange("p i d -> p (i d)"), one(x_in)).then_inc(core.x_loaded, 16)
            sp.dma_start(core.mask_rows[:, :].bitcast(I32), one(mask_in)).then_inc(core.x_loaded, 16)
            sp.dma_start(core.mask_vec[:, 0:NC], one(vec_in)).then_inc(core.x_loaded, 16)
            load_next(sp)

        @block.vector
        def _(dve):
            link = chained(dve, s["step_v"])
            dve.wait_ge(core.x_loaded, 64)
            rows, stats, mv = core.ctx_rows[0:NC, :], core.stats[0:NC, 0, :], core.mv[0:NC, 0, :]
            link(dve.bn_stats(stats, rows))
            link(dve.bn_aggr(mv, stats))
            dve.tensor_scalar(sm[0:NC, 0, 0:1], mv[:, 1:2], LN_EPS, None, ALU.add).then_inc(s["variance"], 1)
            dve.wait_ge(s["deviation"], 1)
            link(dve.reciprocal(sm[0:NC, 2, 0:1], sm[0:NC, 1, 0:1]))
            dve.tensor_scalar(core.ctx_n[0:NC, :], rows, mv[:, 0:1], sm[0:NC, 2, 0:1], ALU.subtract, ALU.mult)\
                .then_inc(s["normed"], 1)

        @block.scalar
        def _(act):
            act.wait_ge(s["variance"], 1)
            act.activation(sm[0:NC, 1, 0:1], sm[0:NC, 0, 0:1], ACT.Sqrt).then_inc(s["deviation"], 1)
            act.wait_ge(s["turned"], 1)
            act.activation(core.ctx_raw_t[:, 0:NC], core.ps[:, TURN_BANK, 0:NC], ACT.Copy)
            act.activation(core.ctx_norm_t[:, 0:NC], core.ps[:, TURN_BANK, 128:128 + NC], ACT.Copy)

        @block.tensor
        def _(pe):
            pe.wait_ge(core.x_loaded, 64)
            pe.wait_ge(s["normed"], 1)
            eye = core.c("identity")[0:NC, 0:NC]
            pe.transpose(core.ps[:, TURN_BANK, 0:NC], core.ctx_rows[0:NC, :], eye)
            pe.transpose(core.ps[:, TURN_BANK, 128:128 + NC], core.ctx_n[0:NC, :], eye).then_inc(s["turned"], 1)


class Experts:

    def __init__(self, sub, kind, experts, hidden, up, gate, down, b1=None, b2=None, routed=0, top=None):
        self.sub, self.kind, self.experts, self.up, self.gate, self.down = sub, kind, experts, up, gate, down
        self.chunks = [min(128, hidden - at) for at in range(0, hidden, 128)]
        self.hidden, self.b1, self.b2, self.routed, self.top = hidden, b1, b2, routed, top
        co = sub.core
        self.row = 24
        area = co.ka[:, 0:NT * 24 * 4].rearrange("p (a i c) -> p a i c", a=4, i=NT)
        self.exps, self.replaced, self.gates, self.misc = area[:, 0], area[:, 1], area[:, 2], area[:, 3]

    def route_tensor(self, e):
        co, s, w = self.sub.core, self.sub.s, self.sub.w
        for i in range(NT):
            out = co.ps[:, OUT_BANK, 32 * i:32 * i + self.routed]
            biased = "router_b" in self.sub.at
            last = e.matmul(out, co.xt[:, i * 128:i * 128 + 128], w("router"), start=True, stop=not biased,
                            skip_group_check=True)
            if biased:
                last = e.matmul(out, co.c("ones")[:, 0:128], w("router_b"), start=False, stop=True,
                                skip_group_check=True)
        last.then_inc(s["logits"], 1)

    def turn_gates_tensor(self, e):
        co, s = self.sub.core, self.sub.s
        e.wait_ge(s["gates"], 1)
        for i in range(NT):
            last = e.transpose(co.ps[0:self.experts, TURN_BANK, i * 128:i * 128 + 128],
                               self.gates[:, i, 0:self.experts], co.c("identity"))
        last.then_inc(s["gates_turned"], 1)

    def route_vector(self, e, link):
        co, s = self.sub.core, self.sub.s
        r, k = self.routed, self.top
        low, total, tops = self.misc[:, :, 0:1], self.misc[:, :, 1:2], self.misc[:, :, 8:16]
        e.memset(self.exps[:, :, r:self.row], -1.0)
        link(e.memset(self.misc[:, :, 0:self.row], -1.0))
        e.wait_ge(s["logits"], 1)
        logits = co.ps[:, OUT_BANK, 0:NT * 32].rearrange("p (i c) -> p i c", i=NT)[:, :, 0:r]
        e.tensor_reduce(low[:, :, 0], logits, AX.X, ALU.max, negate=True).then_inc(s["shifted"], 1)
        e.wait_ge(s["exps"], 1)
        for i in range(NT):
            last = e.max(tops[:, i, :], self.exps[:, i, 0:r])
        link(last)
        link(e.memset(tops[:, :, k:8], -1.0))
        link(e.reciprocal(total[:, :, 0], total[:, :, 0]))
        for i in range(NT):
            last = e.match_replace(self.replaced[:, i, 0:r + 8 - k], tops[:, i, :],
                                   self.exps[:, i, 0:r + 8 - k], -2.0)
        link(last)
        for i in range(NT):
            last = e.scalar_tensor_tensor(out=self.gates[:, i, 0:r], in0=self.replaced[:, i, 0:r], scalar=-1.5,
                                          in1=self.exps[:, i, 0:r], op0=ALU.is_lt, op1=ALU.mult)
        link(last)
        if self.experts > r:
            e.memset(self.gates[:, :, r:self.experts], 1.0)
        for i in range(NT):
            last = e.tensor_scalar(self.gates[:, i, 0:r], self.gates[:, i, 0:r], total[:, i, :], None, ALU.mult)
        last.then_inc(s["gates"], 1)

    def route_scalar(self, e):
        co, s = self.sub.core, self.sub.s
        e.wait_ge(s["shifted"], 1)
        for i in range(NT):
            last = e.activation(self.exps[:, i, 0:self.routed], co.ps[:, OUT_BANK, 32 * i:32 * i + self.routed],
                                ACT.Exp, bias=self.misc[:, i, 0:1], scale=1.0, accum_out=self.misc[:, i, 1:2])
        last.then_inc(s["exps"], 1)

    def pairs(self):
        return [(x, c) for x in range(self.experts) for c in range(len(self.chunks))]

    def hidden_tile(self, x, c):
        at = ((x % 2) * len(self.chunks) + c) * N
        return self.sub.core.o[0:self.chunks[c], at:at + N]

    def tensor(self, e):
        co, s, w = self.sub.core, self.sub.s, self.sub.w
        n = len(self.chunks)
        e.wait_ge(s["features"], 1)
        if self.top is not None:
            self.route_tensor(e)

        def up(x):
            for c, m in enumerate(self.chunks):
                job = x * n + c
                if job >= 2:
                    e.wait_ge(s["hidden"], job - 1)
                cols = slice(x * self.hidden + 128 * c, x * self.hidden + 128 * c + m)
                for b, weights in enumerate((self.up, self.gate) if self.gate is not None else (self.up,)):
                    last = e.matmul(co.ps[0:m, 2 * (job % 2) + b, :], weights[:, cols], co.xt[:, :],
                                    start=True, stop=True)
                last.then_inc(s["up"], 1)

        up(0)
        if self.b2 is not None:
            self.turn_gates_tensor(e)
            e.wait_ge(s["gates_kept"], 1)
            for i in range(NT):
                last = e.matmul(co.ps[:, OUT_BANK, i * 128:i * 128 + 128],
                                co.tmp[0:self.experts, 0, i * 128:i * 128 + 128], self.b2, start=True,
                                stop=True, skip_group_check=True)
            last.then_inc(s["out"], 1)
        for x in range(self.experts):
            if x + 1 < self.experts:
                up(x + 1)
            e.wait_ge(s["hidden"], (x + 1) * n)
            if x >= 2:
                e.wait_ge(s["summed"], (x - 1) * NT)
            for i in range(NT):
                for c in range(n):
                    last = e.matmul(co.ps[:, 4 + x % 2, i * 128:i * 128 + 128],
                                    self.hidden_tile(x, c)[:, i * 128:i * 128 + 128],
                                    self.down[0:self.chunks[c], (x * n + c) * 128:(x * n + c) * 128 + 128],
                                    start=c == 0, stop=c == n - 1, skip_group_check=True)
            last.then_inc(s["down"], 1)

    def scalar(self, e):
        co, s = self.sub.core, self.sub.s
        if self.top is not None:
            self.route_scalar(e)
        for job, (x, c) in enumerate(self.pairs()):
            m = self.chunks[c]
            e.wait_ge(s["up"], job + 1)
            if self.kind == "relu":
                if x >= 2:
                    e.wait_ge(s["down"], x - 1)
                e.activation(self.hidden_tile(x, c), co.ps[0:m, 2 * (job % 2), :], ACT.Relu,
                             bias=self.b1[:, x:x + 1], scale=1.0).then_inc(s["hidden"], 1)
                if x == 0 and self.b2 is not None:
                    e.wait_ge(s["gates_turned"], 1)
                    e.activation(co.tmp[0:self.experts, 0, :], co.ps[0:self.experts, TURN_BANK, :], ACT.Copy)\
                        .then_inc(s["gates_kept"], 1)
            else:
                if job >= 2:
                    e.wait_ge(s["hidden"], job - 1)
                e.activation(co.tmp[0:m, job % 2, :], co.ps[0:m, 2 * (job % 2) + 1, :], ACT.Silu)\
                    .then_inc(s["relu"], 1)

    def vector(self, e, link):
        co, s = self.sub.core, self.sub.s
        if self.top is not None:
            self.route_vector(e, link)
        if self.b2 is not None:
            e.wait_ge(s["out"], 1)
            flat = co.x[:, :, :].rearrange("p i d -> p (i d)")
            link(e.tensor_tensor(flat, flat, co.ps[:, OUT_BANK, :], ALU.add))
        n = len(self.chunks)

        def hidden(x):
            for c, m in enumerate(self.chunks):
                job = x * n + c
                e.wait_ge(s["relu"], job + 1)
                if x >= 2:
                    e.wait_ge(s["down"], x - 1)
                e.tensor_tensor(self.hidden_tile(x, c), co.tmp[0:m, job % 2, :],
                                co.ps[0:m, 2 * (job % 2), :], ALU.mult).then_inc(s["hidden"], 1)

        if self.kind == "silu":
            hidden(0)
        for x in range(self.experts):
            if self.kind == "silu" and x + 1 < self.experts:
                hidden(x + 1)
            e.wait_ge(s["down"], x + 1)
            if x >= 1:
                e.wait_ge(s["summed"], x * NT)
            for i in range(NT):
                out = co.ps[:, 4 + x % 2, i * 128:i * 128 + 128]
                if self.top is None:
                    ins = e.tensor_tensor(co.x[:, i, :], co.x[:, i, :], out, ALU.add)
                else:
                    ins = e.scalar_tensor_tensor(out=co.x[:, i, :], in0=out, scalar=self.gates[:, i, x:x + 1],
                                                 in1=co.x[:, i, :], op0=ALU.mult, op1=ALU.add)
                ins.then_inc(s["summed"], 1)
        e.wait_ge(s["summed"], self.experts * NT)


def experts_sublayer(core, load_next, clear, key, number):
    sub = Sublayer(core, key, number)
    s, w = sub.s, sub.w
    nm = Norm(sub, next_table=ACT.Silu if key == "L1_ffn" else ACT.Exp)
    if key == "L0_ffn":
        ex = Experts(sub, "relu", 16, 128, w("w1"), None, w("w2"), b1=w("b1"), b2=w("b2"), routed=15, top=3)
    elif key == "L3_ffn":
        gate = core.gate_up[:, 0:8 * 352]
        up = core.gate_up[:, 8 * 352:16 * 352]
        ex = Experts(sub, "silu", 8, 352, up, gate, w("down"), routed=8, top=2)
    else:
        at = sub.at
        real = lambda n: core.converted[:, at[n][0]:at[n][0] + at[n][1]]
        ex = Experts(sub, "silu", 1, 384, real("up"), real("gate"), real("down"))
    whole = key == "L3_ffn"

    with core.nc.Block() as block:

        @block.sync
        def _(sp):
            load_next(sp)

        @block.gpsimd
        def _(pool):
            clear(pool)

        @block.vector
        def _(dve):
            link = chained(dve, s["step_v"])
            dve.wait_ge(core.loaded[key], 16)
            if key == "L1_ffn":
                n = sum(wide for _, wide, _ in sub.at.values())
                dve.tensor_scalar(core.converted[:, 0:n], sub.slot[:, 0:n].bitcast(I32), 1.0 / 127.0, None, ALU.mult)\
                    .then_inc(s["converted"], 1)
            nm.vector(dve, link)
            ex.vector(dve, link)

        @block.scalar
        def _(act):
            act.wait_ge(core.loaded[key], 16)
            nm.scalar(act)
            ex.scalar(act)
            core.load_table(act, ACT.Sqrt, 2 * number + 1)

        @block.tensor
        def _(pe):
            pe.wait_ge(core.loaded[key], 16)
            if whole:
                pe.wait_ge(core.loaded["L3_ffn_gate_up"], 16)
            nm.tensor(pe)
            if key == "L1_ffn":
                pe.wait_ge(s["converted"], 1)
            ex.tensor(pe)


def fourier_sublayer(core, load_next, clear, key, number):
    sub = Sublayer(core, key, number)
    s, w = sub.s, sub.w
    nm = Norm(sub, next_table=None)
    at_real, at_imag, mat = core.tmp[:, 0, 0:128], core.tmp[:, 0, 128:256], core.tmp[:, 0, 256:384]

    with core.nc.Block() as block:

        @block.sync
        def _(sp):
            load_next(sp)

        @block.gpsimd
        def _(pool):
            clear(pool)

        @block.vector
        def _(dve):
            link = chained(dve, s["step_v"])
            nm.vector(dve, link)
            dve.wait_ge(s["up"], 1)
            dve.tensor_copy(core.tmp[:, 0, 0:256], core.ps[:, 0, 0:256]).then_inc(s["hidden"], 1)
            dve.wait_ge(s["up"], 2)
            dve.tensor_scalar(mat, core.ps[:, 1, 0:128], 1.0 / 128, None, ALU.mult).then_inc(s["hidden"], 1)
            dve.wait_ge(s["out"], 1)
            flat = core.x[:, :, :].rearrange("p i d -> p (i d)")
            link(dve.tensor_tensor(flat, flat, core.ps[:, OUT_BANK, :], ALU.add))

        @block.scalar
        def _(act):
            nm.scalar(act)

        @block.tensor
        def _(pe):
            pe.wait_ge(core.loaded[key], 16)
            group = dict(skip_group_check=True)
            pe.matmul(core.ps[:, 0, 0:128], w("real"), core.c("dft_cos"), start=True, stop=False, **group)
            pe.matmul(core.ps[:, 0, 0:128], w("imag"), core.c("dft_sin"), start=False, stop=True, **group)
            pe.matmul(core.ps[:, 0, 128:256], w("imag"), core.c("dft_cos"), start=True, stop=False, **group)
            pe.matmul(core.ps[:, 0, 128:256], w("real"), core.c("dft_minus_sin"), start=False, stop=True,
                      **group).then_inc(s["up"], 1)
            nm.tensor(pe)
            pe.wait_ge(s["hidden"], 1)
            pe.matmul(core.ps[:, 1, 0:128], at_real, core.c("dft_cos"), start=True, stop=False, **group)
            pe.matmul(core.ps[:, 1, 0:128], at_imag, core.c("dft_minus_sin"), start=False, stop=True, **group)\
                .then_inc(s["up"], 1)
            pe.wait_ge(s["hidden"], 2)
            pe.wait_ge(s["features"], 1)
            for i in range(NT):
                out = core.ps[:, OUT_BANK, i * 128:i * 128 + 128]
                pe.matmul(out, core.xt[:, i * 128:i * 128 + 128], mat, start=True, stop=False, **group)
                last = pe.matmul(out, core.c("ones")[:, 0:128], w("bo"), start=False, stop=True, **group)
            last.then_inc(s["out"], 1)



SUBLAYERS = [
    ("L0_attn", 0, dict(wide=False, pattern="causal", scale=8 ** -0.5, alibi=True, norm={})),
    ("L0_xattn", 1, dict(wide=False, own=False, ctx=True, scale=8 ** -0.5, relu=True, norm={})),
    ("L0_ffn", 2, None),
    ("L1_attn", 3, dict(wide=False, alpha=True, value_scale=True, norm={})),
    ("L1_xattn", 4, dict(wide=True, ctx=True, scale=1 / 8, scores_by=0.6, norm=dict(again=LN_EPS))),
    ("L1_ffn", 5, None),
    ("L2_attn_g", 6, dict(wide=False, pattern="causal", scale=8 ** -0.5, grouped=True, rope=True, latent=True, scores_by=0.75,
                          norm=dict(again=RMS_EPS), keep_h=True)),
    ("L2_attn_l", 6, dict(wide=False, pattern="local", scale=8 ** -0.5, grouped=True, rope=True,
                          norm=dict(kind="rms"), add_h=True)),
    ("L2_xattn", 7, dict(wide=True, heads=8, ctx=True, scale=1 / 8, ctx_rope=True, norm=dict(again=LN_EPS))),
    ("L2_ffn", 8, None),
    ("L3_attn", 9, dict(wide=True, pattern="causal", scale=1 / 8, norm=dict(again=LN_EPS))),
    ("L3_xattn", 10, dict(wide=False, own=False, ctx=True, scale=8 ** -0.5, ctx_mask=True, norm={})),
    ("L3_ffn", 11, None),
]


def build(nc, dram, layouts, out, scratch):
    with ExitStack() as ctx:
        core = Core(nc, ctx, dram, layouts)
        core.scratch = scratch
        todo = SUBLAYERS

        with nc.Block() as block:

            @block.sync
            def _(sp):
                sp.dma_start(core.consts[:, :], dram["consts"]).then_inc(core.consts_loaded, 16)
                sp.dma_start(core.o[:, 0:masks().width], dram["masks"]).then_inc(core.consts_loaded, 16)
                at = masks().width
                sp.dma_start(core.o[:, at:at + spreading().width], dram["spreading"])\
                    .then_inc(core.consts_loaded, 16)

            @block.gpsimd
            def _(pool):
                pool.memset(core.guard_thin[:, :, :, :], 0.0)
                pool.memset(core.guard_wide[:, :, :, :], 0.0)
                for context in (core.ctx_raw_t, core.ctx_t, core.ctx_rotated):
                    pool.memset(context[:, 64:128], 0.0)
                pool.memset(core.mask_vec[:, 64:128], 2.0)

            @block.vector
            def _(dve):
                dve.wait_ge(core.consts_loaded, 48)
                at = masks().width
                dve.tensor_copy(core.spreading[:, :], core.o[:, at:at + spreading().width])
                dve.tensor_copy(core.identity_b[:, :], core.c("identity"))
                for name, mask in core.masks_b.items():
                    at, wide, _ = core.mask_at[name]
                    dve.tensor_copy(mask[:, :], core.o[:, at:at + wide])

        def loader(n):
            def load(sp):
                if n >= len(todo):
                    return
                key = todo[n][0]
                wide = sum(cols for _, cols, _ in layouts[key].values())
                slot = core.slot[(n + 1) % 2][:, 0:wide]
                sp.dma_start(slot.bitcast(I32) if key == "L1_ffn" else slot, dram[key])\
                    .then_inc(core.loaded[key], 16)
                if key == "L3_ffn":
                    sp.dma_start(core.gate_up[:, :], dram["L3_ffn_gate_up"])\
                        .then_inc(core.loaded["L3_ffn_gate_up"], 16)
            return load

        def clearer(number):
            def clear(pool):
                nums = [x.num for x in core.sets[(number + 1) % 2].values()]
                assert nums == list(range(nums[0], nums[-1] + 1))
                pool.sem_clear(range(nums[0], nums[-1] + 1))
            return clear

        with nc.Fori(0, B) as b:
            context_stage(core, loader(0), 0, dram["x"], dram["ctx"], dram["mask"], dram["mask_vec"], b)
            room = ExitStack()
            for n, (key, _, kinds) in enumerate(todo):
                number = n + 1
                args = (core, loader(n + 1), clearer(number), key, number)
                if key != "L3_ffn":
                    room.close()
                    use = "plain" if not kinds else "wide" if kinds["wide"] else "thin"
                    room.enter_context(core.operands(use, number))
                if kinds is not None:
                    attention_sublayer(*args, **kinds)
                elif key == "L2_ffn":
                    fourier_sublayer(*args)
                else:
                    experts_sublayer(*args)
            room.close()
            with nc.Block() as block:

                @block.sync
                def _(sp):
                    sp.dma_start(out[bass.ds(b, 1)].rearrange("o p c -> (o p) c"),
                                 core.x[:, :, :].rearrange("p i d -> p (i d)")).then_inc(core.x_loaded, 16)
                    sp.wait_ge(core.x_loaded, 80)
            nums = sorted(x.num for x in core.loop_sems)
            assert nums == list(range(nums[0], nums[-1] + 1))
            nc.gpsimd.sem_clear(range(nums[0], nums[-1] + 1))
            nc.all_engine_barrier()


def kernel(**inputs):
    import concourse.bacc as _bacc
    from concourse.bass_utils import run_bass_kernel_spmd as _run

    nc = _bacc.Bacc("TRN2", target_bir_lowering=False, num_devices=1)
    tiles = lambda a: np.ascontiguousarray(a.reshape(B, NT, 128, -1).transpose(0, 2, 1, 3).reshape(B, 128, -1))
    arrays = {
        "x": tiles(np.asarray(inputs["x"])),
        "ctx": np.ascontiguousarray(inputs["ctx_1024"]),
        "mask": tiles(np.asarray(inputs["mask_BxSxS2_bk1"]).view(np.uint8)).view(np.int32),
        "mask_vec": np.ascontiguousarray(np.asarray(inputs["mask_Bx1x1xS2_fk0"]).reshape(B, 1, NC)),
        "consts": constants().array(),
        "masks": masks().array(),
        "spreading": spreading().array(),
    }
    layouts = {}
    for key, pack in packs(inputs).items():
        arrays[key] = pack.array()
        layouts[key] = pack.at
    dram = {k: nc.dram_tensor(f"in_{k}", a.shape, mybir.dt.from_np(a.dtype), kind="ExternalInput").ap()
            for k, a in arrays.items()}
    out = nc.dram_tensor("out_x", (B, 128, NT * D), F32, kind="ExternalOutput").ap()
    scratch = nc.dram_tensor("scratch", (16, 8), F32, kind="Internal").ap()
    build(nc, dram, layouts, out, scratch)
    r = _run(nc, [{f"in_{k}": a for k, a in arrays.items()}], core_ids=[0])
    y = np.asarray(r.results[0]["out_x"])
    return np.ascontiguousarray(y.reshape(B, 128, NT, D).transpose(0, 2, 1, 3).reshape(B, N, D))
```
